# Optimizing a Trainium2 kernel written in Bass

```python
import numpy as np
import jax
import jax.numpy as jnp

def _softmax(x, axis=-1):
    return jax.nn.softmax(x, axis=axis)

def _gelu(x):
    return jax.nn.gelu(x, approximate=True)

def _silu(x):
    return jax.nn.silu(x)

def _sigmoid(x):
    return jax.nn.sigmoid(x)

def _layernorm(x, axis=-1, eps=1e-05):
    m = jnp.mean(x, axis=axis, keepdims=True)
    v = jnp.var(x, axis=axis, keepdims=True)
    return (x - m) / jnp.sqrt(v + eps)

def _scatter_add(tgt, idx, src, axis=0):
    return tgt.at[idx].add(src)

def _segment_sum(src, seg, n):
    return jax.ops.segment_sum(src, seg, n)
kernel_name = 'mk_gnn_preln_d4_gnn_r32_7f5fc2'

def setup_inputs(seed: int=0):
    np.random.seed(seed)
    _w = jnp.asarray

    def _rec_inputs():
        import jax
        import jax.numpy as jnp
        _gk = jax.random.key(seed)
        x = -0.0003713 + 1 * jax.random.normal(jax.random.fold_in(_gk, 1), (50000, 128), jnp.float32)
        src = jax.random.randint(jax.random.fold_in(_gk, 2), (50000,), 0, 50000, jnp.int32)
        dst = jax.random.randint(jax.random.fold_in(_gk, 3), (50000,), 0, 50000, jnp.int32)
        _o = jnp.argsort(dst, stable=True)
        src = src[_o]
        dst = dst[_o]
        edge_type_32 = jax.random.randint(jax.random.fold_in(_gk, 13), (50000,), 0, 32, jnp.int32)
        edge_weight = jax.random.uniform(jax.random.fold_in(_gk, 14), (50000,), jnp.float32, 0.0, 1)
        return (x, src, dst, edge_type_32, edge_weight)
    x, src, dst, edge_type_32, edge_weight = _rec_inputs()

    def _L0_gnn_setup():
        import jax, jax.numpy as jnp
        import numpy as np
        N = 3125
        E = 50000
        D_IN = 128
        D_OUT = 128
        HEADS = 4
        C = D_OUT // HEADS
        NEG_SLOPE = 0.2
        EPS_SOFTMAX = 1e-16
        EPS_LN = 1e-05

        def _gat_edge_conv(x, src, dst, W, att_src, att_dst, gat_bias, skip_W, skip_b, ln_g, ln_b):
            n = x.shape[0]
            h = (x @ W).reshape(n, HEADS, C)
            a_s = jnp.einsum('nhc,hc->nh', h, att_src)
            a_d = jnp.einsum('nhc,hc->nh', h, att_dst)
            e = jax.nn.leaky_relu(a_s[src] + a_d[dst], NEG_SLOPE)
            m = jax.ops.segment_max(e, dst, num_segments=n)
            p = jnp.exp(e - m[dst])
            z = jax.ops.segment_sum(p, dst, num_segments=n)
            alpha = p / (z[dst] + EPS_SOFTMAX)
            msg = h[src] * alpha[:, :, None]
            out = jax.ops.segment_sum(msg, dst, num_segments=n)
            out = out.reshape(n, HEADS * C) + gat_bias
            out = out + x @ skip_W + skip_b
            mu = out.mean(-1, keepdims=True)
            var = ((out - mu) ** 2).mean(-1, keepdims=True)
            return (out - mu) * jax.lax.rsqrt(var + EPS_LN) * ln_g + ln_b
        key = jax.random.key(seed)
        ks = jax.random.split(key, 10)
        x = jax.random.normal(ks[0], (N, D_IN), dtype=jnp.float32)
        edge_index = jax.random.randint(ks[1], (2, E), 0, N, dtype=jnp.int64)
        s = 1.0 / np.sqrt(D_IN)
        W = jax.random.normal(ks[2], (D_IN, HEADS * C), dtype=jnp.float32) * s
        att_src = jax.random.normal(ks[3], (HEADS, C), dtype=jnp.float32) * (1.0 / np.sqrt(C))
        att_dst = jax.random.normal(ks[4], (HEADS, C), dtype=jnp.float32) * (1.0 / np.sqrt(C))
        gat_bias = jax.random.normal(ks[5], (D_OUT,), dtype=jnp.float32) * 0.02
        skip_W = jax.random.normal(ks[6], (D_IN, D_OUT), dtype=jnp.float32) * s
        skip_b = jax.random.normal(ks[7], (D_OUT,), dtype=jnp.float32) * 0.02
        ln_g = jnp.ones((D_OUT,), dtype=jnp.float32)
        ln_b = jnp.zeros((D_OUT,), dtype=jnp.float32)
        return {'x': x, 'edge_index': edge_index, 'W': W, 'att_src': att_src, 'att_dst': att_dst, 'gat_bias': gat_bias, 'skip_W': skip_W, 'skip_b': skip_b, 'ln_g': ln_g, 'ln_b': ln_b}
    _L0_gnn_all = _L0_gnn_setup()
    _L0_gnn_in = {k: v for k, v in _L0_gnn_all.items() if k in ('W', 'att_src', 'att_dst', 'gat_bias', 'skip_W', 'skip_b', 'ln_g', 'ln_b')}
    del _L0_gnn_all

    def _L1_gnn_setup():
        import jax, jax.numpy as jnp
        import numpy as np
        N_NODES = 50000
        N_EDGES = 25000
        D_IN = 128
        D_OUT = 128
        key = jax.random.key(seed)
        ks = jax.random.split(key, 6)
        x = jax.random.normal(ks[0], (N_NODES, D_IN), dtype=jnp.float32)
        edge_index = jax.random.randint(ks[1], (2, N_EDGES), 0, N_NODES, dtype=jnp.int32)
        s1 = 1.0 / np.sqrt(2 * D_IN)
        s2 = 1.0 / np.sqrt(D_IN)
        W1 = jax.random.normal(ks[2], (2 * D_IN, D_IN), dtype=jnp.float32) * s1
        b1 = jnp.zeros((D_IN,), dtype=jnp.float32)
        W2 = jax.random.normal(ks[3], (D_IN, 1), dtype=jnp.float32) * s2
        b2 = jnp.zeros((1,), dtype=jnp.float32)
        Wl = jax.random.normal(ks[4], (D_IN, D_OUT), dtype=jnp.float32) * s2
        bl = jnp.zeros((D_OUT,), dtype=jnp.float32)
        return {'x': x, 'edge_index': edge_index, 'W1': W1, 'b1': b1, 'W2': W2, 'b2': b2, 'Wl': Wl, 'bl': bl}
    _L1_gnn_all = _L1_gnn_setup()
    _L1_gnn_in = {k: v for k, v in _L1_gnn_all.items() if k in ('W1', 'b1', 'W2', 'b2', 'Wl', 'bl')}
    del _L1_gnn_all

    def _L2_gnn_setup():
        import jax, jax.numpy as jnp
        import numpy as np
        N = 50000
        E = 50000
        R = 32
        B = 8
        DIN = 128
        DOUT = 128
        key = jax.random.key(seed)
        ks = jax.random.split(key, 7)
        x = jax.random.normal(ks[0], (N, DIN), dtype=jnp.float32)
        src = jax.random.randint(ks[1], (E,), 0, N, dtype=jnp.int32)
        dst = jax.random.randint(ks[2], (E,), 0, N, dtype=jnp.int32)
        etypes = jax.random.randint(ks[3], (E,), 0, R, dtype=jnp.int32)
        weight = jax.random.normal(ks[4], (B, DIN, DOUT), dtype=jnp.float32) * 0.05
        w_comp = jax.random.normal(ks[5], (R, B), dtype=jnp.float32) * 0.3
        h_bias = jnp.zeros((DOUT,), dtype=jnp.float32)
        loop_weight = jax.random.normal(ks[6], (DIN, DOUT), dtype=jnp.float32) * 0.05
        return {'x': x, 'src': src, 'dst': dst, 'etypes': etypes, 'weight': weight, 'w_comp': w_comp, 'h_bias': h_bias, 'loop_weight': loop_weight}
    _L2_gnn_all = _L2_gnn_setup()
    _L2_gnn_in = {k: v for k, v in _L2_gnn_all.items() if k in ('weight', 'w_comp', 'h_bias', 'loop_weight')}
    del _L2_gnn_all

    def _L3_gnn_setup():
        import jax, jax.numpy as jnp
        import numpy as np
        N = 50000
        F = 128
        D = 128
        K = 4
        E = 25000
        EPS = 1e-12
        key = jax.random.key(seed)
        k1, k2, k3, k4, k5 = jax.random.split(key, 5)
        x = jax.random.normal(k1, (N, F), dtype=jnp.float32)
        edge_vals = jax.random.uniform(k2, (E,), dtype=jnp.float32)
        weights = jax.random.normal(k3, (K, F, D), dtype=jnp.float32) * 0.05
        edge_row = jax.random.randint(k4, (E,), 0, N, dtype=jnp.int32)
        edge_col = jax.random.randint(k5, (E,), 0, N, dtype=jnp.int32)
        return {'x': x, 'edge_vals': edge_vals, 'weights': weights, 'edge_row': edge_row, 'edge_col': edge_col}
    _L3_gnn_all = _L3_gnn_setup()
    _L3_gnn_in = {k: v for k, v in _L3_gnn_all.items() if k in ('weights',)}
    del _L3_gnn_all
    return {'x': x, 'src': src, 'dst': dst, 'edge_type_32': edge_type_32, 'edge_weight': edge_weight, 'L0_gnn_W': _L0_gnn_in['W'], 'L0_gnn_att_src': _L0_gnn_in['att_src'], 'L0_gnn_att_dst': _L0_gnn_in['att_dst'], 'L0_gnn_gat_bias': _L0_gnn_in['gat_bias'], 'L0_gnn_skip_W': _L0_gnn_in['skip_W'], 'L0_gnn_skip_b': _L0_gnn_in['skip_b'], 'L0_gnn_ln_g': _L0_gnn_in['ln_g'], 'L0_gnn_ln_b': _L0_gnn_in['ln_b'], 'L1_gnn_W1': _L1_gnn_in['W1'], 'L1_gnn_b1': _L1_gnn_in['b1'], 'L1_gnn_W2': _L1_gnn_in['W2'], 'L1_gnn_b2': _L1_gnn_in['b2'], 'L1_gnn_Wl': _L1_gnn_in['Wl'], 'L1_gnn_bl': _L1_gnn_in['bl'], 'L2_gnn_weight': _L2_gnn_in['weight'], 'L2_gnn_w_comp': _L2_gnn_in['w_comp'], 'L2_gnn_h_bias': _L2_gnn_in['h_bias'], 'L2_gnn_loop_weight': _L2_gnn_in['loop_weight'], 'L3_gnn_weights': _L3_gnn_in['weights']}

def reference(x, src, dst, edge_type_32, edge_weight, L0_gnn_W, L0_gnn_att_src, L0_gnn_att_dst, L0_gnn_gat_bias, L0_gnn_skip_W, L0_gnn_skip_b, L0_gnn_ln_g, L0_gnn_ln_b, L1_gnn_W1, L1_gnn_b1, L1_gnn_W2, L1_gnn_b2, L1_gnn_Wl, L1_gnn_bl, L2_gnn_weight, L2_gnn_w_comp, L2_gnn_h_bias, L2_gnn_loop_weight, L3_gnn_weights):
    import jax
    import jax.numpy as jnp

    def _L0_gnn_ref(x, edge_index, W, att_src, att_dst, gat_bias, skip_W, skip_b, ln_g, ln_b):
        import jax, jax.numpy as jnp
        import numpy as np
        N = 3125
        E = 50000
        D_IN = 128
        D_OUT = 128
        HEADS = 4
        C = D_OUT // HEADS
        NEG_SLOPE = 0.2
        EPS_SOFTMAX = 1e-16
        EPS_LN = 1e-05

        def _gat_edge_conv(x, src, dst, W, att_src, att_dst, gat_bias, skip_W, skip_b, ln_g, ln_b):
            n = x.shape[0]
            h = (x @ W).reshape(n, HEADS, C)
            a_s = jnp.einsum('nhc,hc->nh', h, att_src)
            a_d = jnp.einsum('nhc,hc->nh', h, att_dst)
            e = jax.nn.leaky_relu(a_s[src] + a_d[dst], NEG_SLOPE)
            m = jax.ops.segment_max(e, dst, num_segments=n)
            p = jnp.exp(e - m[dst])
            z = jax.ops.segment_sum(p, dst, num_segments=n)
            alpha = p / (z[dst] + EPS_SOFTMAX)
            msg = h[src] * alpha[:, :, None]
            out = jax.ops.segment_sum(msg, dst, num_segments=n)
            out = out.reshape(n, HEADS * C) + gat_bias
            out = out + x @ skip_W + skip_b
            mu = out.mean(-1, keepdims=True)
            var = ((out - mu) ** 2).mean(-1, keepdims=True)
            return (out - mu) * jax.lax.rsqrt(var + EPS_LN) * ln_g + ln_b
        n = x.shape[0]
        loops = jnp.arange(n, dtype=edge_index.dtype)
        src = jnp.concatenate([edge_index[0], loops])
        dst = jnp.concatenate([edge_index[1], loops])
        return _gat_edge_conv(x, src, dst, W, att_src, att_dst, gat_bias, skip_W, skip_b, ln_g, ln_b)

    def _L1_gnn_ref(x, edge_index, W1, b1, W2, b2, Wl, bl):
        import jax, jax.numpy as jnp
        import numpy as np
        N_NODES = 50000
        N_EDGES = 25000
        D_IN = 128
        D_OUT = 128
        row, col = (edge_index[0], edge_index[1])
        n, d = x.shape
        xc = x[row]
        xn = x[col]
        h = jax.nn.relu(xc @ W1[:d] + xn @ W1[d:] + b1)
        mask = jax.nn.sigmoid(h @ W2 + b2)[:, 0]
        seg_sum = jax.ops.segment_sum(mask, row, num_segments=n)
        w = mask / (seg_sum[row] + 1e-09)
        agg = jax.ops.segment_sum(w[:, None] * xn, row, num_segments=n)
        deg = jax.ops.segment_sum(jnp.ones_like(mask), row, num_segments=n)
        out_emb = jnp.where((deg > 0)[:, None], 0.5 * x + 0.5 * agg, x)
        return jax.nn.relu(out_emb @ Wl + bl)

    def _L2_gnn_ref(x, src, dst, etypes, weight, w_comp, h_bias, loop_weight):
        import jax, jax.numpy as jnp
        import numpy as np
        N = 50000
        E = 50000
        R = 32
        B = 8
        DIN = 128
        DOUT = 128
        n = x.shape[0]
        r = w_comp.shape[0]
        seg = dst.astype(jnp.int32) * r + etypes.astype(jnp.int32)
        agg = jax.ops.segment_sum(x[src], seg, num_segments=n * r)
        agg = agg.reshape(n, r, -1)
        tmp = jnp.einsum('nri,rb->nbi', agg, w_comp)
        h = jnp.einsum('nbi,bio->no', tmp, weight)
        h = h + h_bias + x @ loop_weight
        return jax.nn.relu(h)

    def _L3_gnn_ref(x, edge_vals, weights, edge_row, edge_col):
        import jax, jax.numpy as jnp
        import numpy as np
        N = 50000
        F = 128
        D = 128
        K = 4
        E = 25000
        EPS = 1e-12
        n = x.shape[0]
        k = weights.shape[0]

        def spmv(v):
            return jax.ops.segment_sum(edge_vals[:, None] * v[edge_col], edge_row, num_segments=n)
        v0 = x * jax.lax.rsqrt(jnp.maximum(jnp.sum(x * x, axis=0, keepdims=True), EPS))

        def step(carry, _):
            v_prev, v_prev2, beta_prev = carry
            w = spmv(v_prev)
            alpha = jnp.sum(w * v_prev, axis=0, keepdims=True)
            new_v = w - alpha * v_prev - beta_prev * v_prev2
            beta = jnp.sqrt(jnp.sum(new_v * new_v, axis=0, keepdims=True))
            v = new_v / beta
            return ((v, v_prev, beta), v)
        init = (v0, jnp.zeros_like(v0), jnp.zeros((1, x.shape[1]), x.dtype))
        _, vs = jax.lax.scan(step, init, None, length=k - 1)
        Vs = jnp.concatenate([v0[None], vs], axis=0)
        out = jnp.einsum('knf,kfd->nd', Vs, weights)
        return jax.nn.relu(out)
    edge_index = jnp.stack([src, dst])
    h = jnp.maximum(_layernorm(x, axis=-1), 0.0)
    x = x + _L0_gnn_ref(h, edge_index, L0_gnn_W, L0_gnn_att_src, L0_gnn_att_dst, L0_gnn_gat_bias, L0_gnn_skip_W, L0_gnn_skip_b, L0_gnn_ln_g, L0_gnn_ln_b)
    h = jnp.maximum(_layernorm(x, axis=-1), 0.0)
    x = x + _L1_gnn_ref(h, edge_index, L1_gnn_W1, L1_gnn_b1, L1_gnn_W2, L1_gnn_b2, L1_gnn_Wl, L1_gnn_bl)
    h = jnp.maximum(_layernorm(x, axis=-1), 0.0)
    x = x + _L2_gnn_ref(h, src, dst, edge_type_32, L2_gnn_weight, L2_gnn_w_comp, L2_gnn_h_bias, L2_gnn_loop_weight)
    h = jnp.maximum(_layernorm(x, axis=-1), 0.0)
    x = x + _L3_gnn_ref(h, edge_weight, L3_gnn_weights, src, dst)
    return x

_drawn_inputs = setup_inputs


def setup_inputs(seed=0):
    import zlib

    import numpy as np

    out = dict(_drawn_inputs(seed))
    spreads = {'L0_gnn_ln_g': (1.0, 0.2),
     'L0_gnn_ln_b': (0.0, 0.1),
     'L1_gnn_b1': (0.0, 2.0),
     'L1_gnn_bl': (0.0, 0.1),
     'L2_gnn_h_bias': (0.0, 0.1)}
    factors = {'edge_weight': 64.0,
     'L0_gnn_att_dst': 3.322,
     'L0_gnn_gat_bias': 3.381,
     'L0_gnn_skip_b': 3.698,
     'L1_gnn_W1': 8.0,
     'L1_gnn_W2': 8.0,
     'L3_gnn_weights': 32.595}
    for name, (base, spread) in spreads.items():
        noise = np.random.default_rng([zlib.crc32(name.encode()), seed]).standard_normal(out[name].shape)
        drawn = base * np.exp(spread * noise) if base else spread * noise
        out[name] = jnp.asarray(drawn.astype(out[name].dtype))
    for name, factor in factors.items():
        out[name] = (out[name] * factor).astype(out[name].dtype)
    return out
```

```python
import concourse.bass as bass
from concourse import mybir
from contextlib import ExitStack

P = 128
D = 128
N = 50000
K = 7
NB = 56
EC = K * NB
NP = P * EC
ZROW = NP
HI, LO = 196, 256
HH = HI // 2
H = 4
C = D // H
R, B = 32, 8
NEG = 1.0e30
assert HI * LO == NP

fp32 = mybir.dt.float32
bf16 = mybir.dt.bfloat16
i32 = mybir.dt.int32
ALU = mybir.AluOpType
ACT = mybir.ActivationFunctionType
AX = mybir.AxisListType


class Counter:

    def __init__(self, nc, ctx, name, credit=0):
        self.sem = ctx.enter_context(nc.semaphore(name))
        self.base = credit
        self.credit = credit

    def at(self, n):
        return n + self.base


def gnn(nc, x, src, dst, etype, ew, W, att_s, att_d, gat_b, skip_W, skip_b, ln_g, ln_b,
        W1, b1, W2, b2, Wl, bl, wbase, wcomp, h_bias, loop_W, lw, out):
    ctx = ExitStack()
    with ctx:
        def sb(name, shape, dt=fp32, c=ctx):
            return c.enter_context(nc.sbuf_tensor(name, shape, dt))

        def ps(name, shape, dt=fp32, c=ctx):
            return c.enter_context(nc.psum_tensor(name, shape, dt))

        def dram(name, shape, dt=fp32):
            return nc.dram_tensor(name, shape, dt, kind="Internal").ap()

        def cnt(name, credit=0):
            return Counter(nc, ctx, name, credit)

        setup = cnt("setup")
        pdma = cnt("pdma")
        step = cnt("step")
        idx_rdy = [cnt(f"idx_rdy{h}") for h in range(2)]
        idy_rdy = [cnt(f"idy_rdy{h}") for h in range(2)]
        row_rdy = [cnt(f"row_rdy{h}") for h in range(2)]
        roy_rdy = [cnt(f"roy_rdy{h}") for h in range(2)]
        nrow_rdy = [cnt(f"nrow_rdy{h}") for h in range(2)]
        in_rdy = [cnt(f"in_rdy{h}") for h in range(2)]
        st_done = [cnt(f"st_done{h}") for h in range(2)]
        dve_done = cnt("dve_done", 2)
        act_done = cnt("act_done", 2)
        d2a = cnt("d2a")
        a2d = cnt("a2d")
        for_pe = cnt("for_pe")
        for_pe2 = cnt("for_pe2")
        tp_rdy = cnt("tp_rdy")
        hT_rdy = cnt("hT_rdy")
        hT2_rdy = cnt("hT2_rdy", 1)
        mm_rdy = cnt("mm_rdy")
        mm_free = cnt("mm_free", 8)
        hist_o = cnt("hist_o")
        hist_f = cnt("hist_f", K)
        hist_r = cnt("hist_r")
        sc_done = [cnt(f"sc_done{u}") for u in range(K)]
        every = [dve_done, act_done, mm_free, hist_f, hT2_rdy]

        G0 = dram("G0", [NP, D + H])
        AD = dram("AD", [NP, H])
        SK = dram("SK", [NP, D])
        T0 = dram("T0", [NP + P, D + 2 * H])
        X1 = dram("X1", [NP, D])
        P1 = dram("P1", [NP, 2 * D])
        U1 = dram("U1", [NP, D])
        T1 = dram("T1", [NP + P, D + 2])
        X2 = dram("X2", [NP, D])
        H2 = dram("H2", [NP, D])
        LW = dram("LW", [NP, D])
        T2 = dram("T2", [NP + P, D])
        X3 = dram("X3", [NP, D])
        Q = [dram(f"Q{k}", [NP, D]) for k in range(4)]
        T3 = [dram(f"T3{k}", [NP + P, D]) for k in range(3)]
        UU = [dram(f"UU{k}", [NP, D]) for k in range(3)]
        last_src = dram("last_src", [NP], i32)
        last_dst = dram("last_dst", [NP], i32)
        srt = [[dram(f"srt{q}_{u}", [NP, 4]) for u in range(K)] for q in range(2)]
        dst_s = dram("dst_s", [NP], i32)
        src_s = dram("src_s", [NP], i32)

        ident = sb("ident", [P, P])
        identb = sb("identb", [P, P], bf16)
        ones = sb("ones", [P, P])
        lower = sb("lower", [P, P])
        zero = sb("zero", [P, 136])
        iob = sb("iob", [P, LO], bf16)
        iof = sb("iof", [P, LO])
        pcol = sb("pcol", [P, 1])
        eps5 = sb("eps5", [P, 1])
        low = sb("low", [P, H])
        zb = sb("zb", [P, LO], bf16)
        cont = {k: sb(f"cont_{k}", [P, EC]) for k in ("src", "dst")}
        carry = {k: sb(f"carry_{k}", [P, P]) for k in ("src", "dst")}
        fix = {k: sb(f"fix_{k}", [P, 1], i32) for k in ("src", "dst")}
        ew_s = sb("ew_s", [P, EC])
        wc_e = sb("wc_e", [P, EC, B])

        def nrows(t):
            return t[0:NP, :].rearrange("(b p g) d -> b p (g d)", p=P, g=K)

        def erows(t):
            return t[0:NP, :].rearrange("(p b g) d -> b p (g d)", p=P, g=K)

        def nparts(t, lo, hi):
            return t[0:NP, lo:hi].rearrange("(b p g) d -> b p g d", p=P, g=K)

        def ncol(t):
            return t.rearrange("(b p g) -> b p g", p=P, g=K)

        def ecol(t):
            return t.rearrange("(p b g) -> b p g", p=P, g=K)

        def pick(v, b):
            if isinstance(b, int):
                return v[b]
            if len(v.shape) == 4:
                return v[bass.ds(b, 1)].rearrange("o p g d -> (o p) g d")
            return v[bass.ds(b, 1)].rearrange("o p f -> (o p) f")

        def blocks(eng, body, lo=0):
            with eng.Fori(lo, NB // 2) as i:
                for h in range(2):
                    body(2 * i + h, h, i)

        def gather(pool, o, table, slot):
            return pool.indirect_dma_start(out=o, out_offset=None, in_=table[:, :],
                                           in_offset=bass.IndirectOffsetOnAxis(ap=slot, axis=0))

        with nc.Block() as block:
            @block.gpsimd
            def _(pool):
                for c in every:
                    if c.credit:
                        pool.sem_inc(c.sem, c.credit)
                nc.gpsimd.memset(ident[:, :], 0.0)
                nc.gpsimd.memset(ones[:, :], 1.0)
                nc.gpsimd.memset(zero[:, :], 0.0)
                nc.gpsimd.memset(eps5[:, :], 1e-5)
                nc.gpsimd.memset(low[:, :], -NEG)
                nc.gpsimd.memset(zb[:, :], 0.0)
                nc.gpsimd.memset(lower[:, :], 1.0)
                nc.gpsimd.iota(iof[:, :], pattern=[[1, LO]], base=0, channel_multiplier=0,
                               allow_small_or_imprecise_dtypes=True)
                nc.gpsimd.iota(pcol[:, :], pattern=[[0, 1]], base=0, channel_multiplier=EC,
                               allow_small_or_imprecise_dtypes=True).then_inc(step.sem, 1)
                pool.wait_ge(step.sem, step.at(1))
                nc.gpsimd.affine_select(out=ident[:, :], in_=ident[:, :], compare_op=ALU.not_equal, fill=1.0,
                                        base=0, pattern=[[-1, P]], channel_multiplier=1)
                nc.gpsimd.affine_select(out=lower[:, :], in_=lower[:, :], compare_op=ALU.is_ge, fill=0.0,
                                        base=-1, pattern=[[1, P]], channel_multiplier=-1).then_inc(step.sem, 1)
                pool.wait_ge(step.sem, step.at(2))
                nc.gpsimd.tensor_copy(identb[:, :], ident[:, :])
                nc.gpsimd.tensor_copy(iob[:, :], iof[:, :])
            @block.sync
            def _(sp):
                sp.wait_ge(step.sem, step.at(2))
                tz = [(T1, D + 2), (T2, D), *((t, D) for t in T3)]
                for n, (t, w) in enumerate(tz):
                    sp.dma_start(t[NP:NP + P, :], zero[:, 0:w]).then_inc(st_done[n % 2].sem, 16)
                sp.dma_start(T0[NP:NP + P, 0:D + H], zero[:, 0:D + H]).then_inc(st_done[1].sem, 16)
                sp.dma_start(T0[NP:NP + P, D + H:D + 2 * H], low[:, :]).then_inc(setup.sem, 16)
                for h in range(2):
                    sp.wait_ge(st_done[h].sem, 48)
                sp.wait_ge(setup.sem, 16)
        step.base += 2
        setup.base += 16
        for h in range(2):
            st_done[h].base += 48

        def histogram(key_dram, last, name):
            with ExitStack() as c:
                ki = sb(f"ki_{name}", [P, EC], i32, c)
                kd = sb(f"kd_{name}", [P, 2, EC], i32, c)
                kf = sb(f"kf_{name}", [P, 2, EC], fp32, c)
                oh = sb(f"oh_{name}", [P, K, LO + HI], bf16, c)
                hs = sb(f"hs_{name}", [HH, 2, LO], fp32, c)
                cu = sb(f"cu_{name}", [HH, 2, LO], fp32, c)
                tot = sb(f"tot_{name}", [HH, 2], fp32, c)
                lp = sb(f"lp_{name}", [HH, 2, LO], fp32, c)
                lpi = sb(f"lpi_{name}", [HH, 2, LO], i32, c)
                acc = [ps(f"acc{m}_{name}", [P, 512], fp32, c) for m in range(2)]
                bs = ps(f"bs_{name}", [P, 512], fp32, c)
                with nc.Block() as block:
                    @block.sync
                    def _(sp):
                        sp.dma_start(ki[:, :], key_dram.rearrange("(p j) -> p j", p=P)).then_inc(setup.sem, 16)
                        sp.wait_ge(step.sem, step.at(1))
                        sp.dma_start(last.rearrange("(m h l) -> h m l", m=2, l=LO), lpi[:, :, :]).then_inc(setup.sem, 16)
                        sp.wait_ge(setup.sem, setup.at(32))

                    @block.vector
                    def _(dve):
                        dve.wait_ge(setup.sem, setup.at(16))
                        nc.vector.tensor_scalar(kd[:, 0, :], ki[:, :], LO - 1, None, ALU.bitwise_and)
                        nc.vector.tensor_scalar(kd[:, 1, :], ki[:, :], 8, None, ALU.logical_shift_right)
                        nc.vector.drain()
                        nc.vector.tensor_copy(kf[:, :, :], kd[:, :, :])
                        nc.vector.drain()
                        with dve.Fori(0, NB) as i:
                            for u in range(K):
                                dve.wait_ge(hist_f.sem, hist_f.at(i * K + (u + 1 - K)))
                                nc.vector.tensor_scalar(oh[:, u, 0:LO], iob[:, :], kf[:, 0, bass.ds(i * K + u, 1)],
                                                        None, ALU.is_equal)
                                nc.vector.tensor_scalar(oh[:, u, LO:LO + HI], iob[:, 0:HI], kf[:, 1, bass.ds(i * K + u, 1)],
                                                        None, ALU.is_equal).then_inc(hist_o.sem, 1)
                        dve.wait_ge(mm_rdy.sem, mm_rdy.at(1))
                        for m in range(2):
                            nc.vector.tensor_copy(hs[:, m, :], acc[m][0:HH, 0:LO])
                        nc.vector.drain()
                        for m in range(2):
                            nc.vector.tensor_tensor_scan(cu[:, m, :], hs[:, m, :], hs[:, m, :], 0.0, ALU.add, ALU.bypass)
                        nc.vector.drain()
                        nc.vector.tensor_copy(tot[:, :], cu[:, :, LO - 1:LO].rearrange("p m o -> p (m o)")).then_inc(hist_r.sem, 1)
                        dve.wait_ge(mm_rdy.sem, mm_rdy.at(2))
                        for m in range(2):
                            nc.vector.tensor_scalar(lp[:, m, :], cu[:, m, :], bs[0:HH, m:m + 1], -1.0 - ZROW, ALU.add, ALU.add)
                            nc.vector.tensor_scalar(hs[:, m, :], hs[:, m, :], 1.0, None, ALU.min)
                        nc.vector.drain()
                        nc.vector.tensor_tensor(lp[:, :, :], lp[:, :, :], hs[:, :, :], ALU.mult)
                        nc.vector.drain()
                        nc.vector.tensor_scalar(lpi[:, :, :], lp[:, :, :], float(ZROW), None, ALU.add).then_inc(step.sem, 1)

                    @block.tensor
                    def _(pe):
                        for m in range(2):
                            nc.tensor.matmul(acc[m][0:HH, 0:LO], zb[:, 0:HH], zb[:, :], start=True, stop=False)
                        with pe.Fori(0, NB) as i:
                            for u in range(K):
                                pe.wait_ge(hist_o.sem, hist_o.at(i * K + u + 1))
                                for m in range(2):
                                    q = nc.tensor.matmul(acc[m][0:HH, 0:LO], oh[:, u, LO + m * HH:LO + (m + 1) * HH],
                                                         oh[:, u, 0:LO], start=False, stop=False)
                                q.then_inc(hist_f.sem, 1)
                        for m in range(2):
                            q = nc.tensor.matmul(acc[m][0:HH, 0:LO], zb[:, 0:HH], zb[:, :], start=False, stop=True)
                        q.then_inc(mm_rdy.sem, 1)
                        pe.wait_ge(hist_r.sem, hist_r.at(1))
                        nc.tensor.matmul(bs[0:HH, 0:1], lower[0:HH, 0:HH], tot[:, 0:1], start=True, stop=True)
                        nc.tensor.matmul(bs[0:HH, 1:2], lower[0:HH, 0:HH], tot[:, 1:2], start=True, stop=False)
                        nc.tensor.matmul(bs[0:HH, 1:2], ones[0:HH, 0:HH], tot[:, 0:1], start=False, stop=True)\
                            .then_inc(mm_rdy.sem, 1)
                setup.base += 32
                step.base += 1
                hist_r.base += 1
                mm_rdy.base += 2
                hist_o.base += EC
                hist_f.base += EC

        histogram(src, last_src, "src")
        histogram(dst, last_dst, "dst")

        def sort_pass(q, pay, key_col, high):
            with ExitStack() as c:
                di = sb(f"di{q}", [P, EC], i32, c)
                dg = sb(f"dg{q}", [P, EC], fp32, c)
                oh = sb(f"so{q}", [P, K, LO], bf16, c)
                R0 = sb(f"R0{q}", [P, LO], fp32, c)
                tt = sb(f"tt{q}", [P, LO], fp32, c)
                junk = sb(f"junk{q}", [P, 2, LO], fp32, c)
                rk = sb(f"rk{q}", [P, 2, K], fp32, c)
                rki = sb(f"rki{q}", [P, 2, K], i32, c)
                pr = sb(f"pr{q}", [P, 2, K, 4], fp32, c)
                zz = sb(f"zz{q}", [P, EC * 4], fp32, c)
                acc = ps(f"sacc{q}", [P, 512], fp32, c)
                RP = ps(f"RP{q}", [P, 512], fp32, c)
                with nc.Block() as block:
                    @block.vector
                    def _(dve):
                        nc.vector.memset(zz[:, :], 0.0).then_inc(step.sem, 1)
                        nc.vector.tensor_copy(di[:, :], pay[:, :, key_col])
                        nc.vector.drain()
                        if high:
                            nc.vector.tensor_scalar(di[:, :], di[:, :], 8, None, ALU.logical_shift_right)
                        else:
                            nc.vector.tensor_scalar(di[:, :], di[:, :], LO - 1, None, ALU.bitwise_and)
                        nc.vector.drain()
                        nc.vector.tensor_copy(dg[:, :], di[:, :])
                        nc.vector.drain()
                        with dve.Fori(0, NB) as i:
                            for u in range(K):
                                dve.wait_ge(hist_f.sem, hist_f.at(i * K + (u + 1 - K)))
                                nc.vector.tensor_scalar(oh[:, u, :], iob[:, :], dg[:, bass.ds(i * K + u, 1)],
                                                        None, ALU.is_equal).then_inc(hist_o.sem, 1)
                        dve.wait_ge(mm_rdy.sem, mm_rdy.at(1))
                        nc.vector.tensor_copy(R0[:, :], acc[:, 0:LO]).then_inc(hist_r.sem, 1)
                        dve.wait_ge(mm_rdy.sem, mm_rdy.at(2))
                        nc.vector.tensor_copy(junk[:, 0, :], acc[:, LO:2 * LO])
                        nc.vector.drain()
                        nc.vector.tensor_tensor_scan(tt[:, :], junk[:, 0, :], junk[:, 0, :], 0.0, ALU.add, ALU.bypass)
                        nc.vector.drain()
                        nc.vector.tensor_tensor(tt[:, :], tt[:, :], junk[:, 0, :], ALU.subtract)
                        nc.vector.drain()
                        nc.vector.tensor_tensor(R0[:, :], tt[:, :], acc[:, 0:LO], ALU.add).then_inc(hist_r.sem, 1)
                        nc.vector.drain()

                        def ranks(b, h, i):
                            dve.wait_ge(act_done.sem, act_done.at(b - 1))
                            nc.vector.tensor_copy(pr[:, h, :, :], pay[:, bass.ds(b * K, K), :])
                            for u in range(K):
                                nc.vector.tensor_scalar(oh[:, u, :], iob[:, :], dg[:, bass.ds(b * K + u, 1)],
                                                        None, ALU.is_equal)
                                nc.vector.drain()
                                dve.wait_ge(mm_rdy.sem, mm_rdy.at(b * K + u + 3))
                                nc.vector.tensor_tensor_reduce(out=junk[:, u % 2, :], in0=oh[:, u, :], in1=RP[:, 0:LO],
                                                               scale=1.0, scalar=0.0, op0=ALU.mult, op1=ALU.add,
                                                               accum_out=rk[:, h, u:u + 1]).then_inc(hist_o.sem, 1)
                            nc.vector.drain()
                            nc.vector.tensor_copy(rki[:, h, :], rk[:, h, :]).then_inc(d2a.sem, 1)
                        blocks(dve, ranks)
                        dve.wait_ge(in_rdy[0].sem, in_rdy[0].at(16))
                        for u in range(1, K):
                            dve.wait_ge(in_rdy[u % 2].sem, in_rdy[u % 2].at(16 * (u // 2 + 1)))
                            nc.vector.tensor_tensor(pay[:, :, :].rearrange("p j c -> p (j c)"),
                                                    pay[:, :, :].rearrange("p j c -> p (j c)"), zz[:, :],
                                                    ALU.add).then_inc(a2d.sem, 1)
                            nc.vector.drain()

                    @block.tensor
                    def _(pe):
                        nc.tensor.matmul(acc[:, 0:LO], identb[:, :], zb[:, :], start=True, stop=False)
                        with pe.Fori(0, NB) as i:
                            for u in range(K):
                                pe.wait_ge(hist_o.sem, hist_o.at(i * K + u + 1))
                                nc.tensor.matmul(acc[:, 0:LO], identb[:, :], oh[:, u, :], start=False, stop=False)\
                                    .then_inc(hist_f.sem, 1)
                        nc.tensor.matmul(acc[:, 0:LO], identb[:, :], zb[:, :], start=False, stop=True).then_inc(mm_rdy.sem, 1)
                        pe.wait_ge(hist_r.sem, hist_r.at(1))
                        nc.tensor.matmul(acc[:, 0:LO], lower[:, :], R0[:, :], start=True, stop=True)
                        nc.tensor.matmul(acc[:, LO:2 * LO], ones[:, :], R0[:, :], start=True, stop=True).then_inc(mm_rdy.sem, 1)
                        pe.wait_ge(hist_r.sem, hist_r.at(2))
                        nc.tensor.matmul(RP[:, 0:LO], ident[:, :], R0[:, :], start=True, stop=True).then_inc(mm_rdy.sem, 1)
                        with pe.Fori(0, NB) as i:
                            for u in range(K):
                                pe.wait_ge(hist_o.sem, hist_o.at(i * K + u + 1 + EC))
                                nc.tensor.matmul(RP[:, 0:LO], identb[:, :], oh[:, u, :], start=False, stop=True,
                                                 skip_group_check=True)\
                                    .then_inc(mm_rdy.sem, 1)

                    @block.gpsimd
                    def _(pool):
                        pool.wait_ge(step.sem, step.at(1))
                        for u in range(K):
                            pool.dma_start(srt[q][u].rearrange("(p j) c -> p (j c)", p=P), zz[:, :])\
                                .then_inc(sc_done[u].sem, 16)

                        def scatter(b, h, i):
                            pool.wait_ge(d2a.sem, d2a.at(b + 1))
                            pool.nop(nofuse=True)
                            for u in range(K):
                                pool.wait_ge(sc_done[u].sem, sc_done[u].at(b * 16 + 16))
                                pool.nop(nofuse=True)
                                pool.indirect_dma_start(
                                    out=srt[q][u][:, :],
                                    out_offset=bass.IndirectOffsetOnAxis(ap=rki[:, h, u:u + 1], axis=0),
                                    in_=pr[:, h, u, :], in_offset=None).then_inc(sc_done[u].sem, 16)
                        blocks(pool, scatter)

                    @block.scalar
                    def _(act):
                        def freed(b, h, i):
                            for u in range(K):
                                act.wait_ge(sc_done[u].sem, sc_done[u].at(b * 16 + 32))
                            act.nop(nofuse=True)
                            act.sem_inc(act_done.sem, 1)
                        blocks(act, freed)
                        pf = pay[:, :, :].rearrange("p j c -> p (j c)")
                        act.dma_start(pf, srt[q][0].rearrange("(p j) c -> p (j c)", p=P)).then_inc(in_rdy[0].sem, 16)
                        for u in range(1, K):
                            if u > 1:
                                act.wait_ge(a2d.sem, a2d.at(u - 1))
                            act.dma_start(zz[:, :], srt[q][u].rearrange("(p j) c -> p (j c)", p=P))\
                                .then_inc(in_rdy[u % 2].sem, 16)
                step.base += 1
                hist_f.base += EC
                hist_o.base += 2 * EC
                hist_r.base += 2
                mm_rdy.base += 3 + EC
                act_done.base += NB
                d2a.base += NB
                a2d.base += K - 1
                in_rdy[0].base += 16 * ((K + 1) // 2)
                in_rdy[1].base += 16 * (K // 2)
                for u in range(K):
                    sc_done[u].base += 16 * (NB + 1)

        def edge_flags(name, kf):
            with ExitStack() as c:
                eq = sb(f"eq_{name}", [P, EC], fp32, c)
                rowk = sb(f"rowk_{name}", [P, P], fp32, c)
                fx = sb(f"fx_{name}", [P, 1], fp32, c)
                kb = ps(f"kb_{name}", [P, 512], fp32, c)
                with nc.Block() as block:
                    @block.vector
                    def _(dve):
                        nc.vector.memset(cont[name][:, 0:1], 0.0)
                        nc.vector.tensor_tensor(cont[name][:, 1:EC], kf[:, 1:EC], kf[:, 0:EC - 1], ALU.is_equal)
                        nc.vector.tensor_scalar(eq[:, :], kf[:, :], kf[:, 0:1], None, ALU.is_equal)
                        nc.vector.tensor_scalar(rowk[:, :], ident[:, :], kf[:, 0:1], None, ALU.mult).then_inc(step.sem, 1)
                        nc.vector.drain()
                        nc.vector.tensor_reduce(fx[:, :], eq[:, :], AX.X, ALU.add)
                        nc.vector.drain()
                        nc.vector.scalar_tensor_tensor(fix[name][:, :], fx[:, :], -1.0, pcol[:, :], ALU.add, ALU.add)
                        dve.wait_ge(mm_rdy.sem, mm_rdy.at(1))
                        nc.vector.scalar_tensor_tensor(carry[name][:, :], kb[:, 0:P], kf[:, EC - 1:EC], lower[:, :],
                                                       ALU.is_equal, ALU.mult)

                    @block.tensor
                    def _(pe):
                        pe.wait_ge(step.sem, step.at(1))
                        nc.tensor.matmul(kb[:, 0:P], ones[:, :], rowk[:, :], start=True, stop=True).then_inc(mm_rdy.sem, 1)
                step.base += 1
                mm_rdy.base += 1

        with ExitStack() as c:
            pay = sb("pay", [P, EC, 4], fp32, c)
            pi = sb("pi", [P, 2, EC], i32, c)
            pf = sb("pf", [P, EC], fp32, c)
            with nc.Block() as block:
                @block.sync
                def _(sp):
                    sp.dma_start(pi[:, 0, :], src.rearrange("(p j) -> p j", p=P)).then_inc(setup.sem, 16)
                    sp.dma_start(pi[:, 1, :], dst.rearrange("(p j) -> p j", p=P)).then_inc(setup.sem, 16)
                    sp.dma_start(pf[:, :], ew.rearrange("(p j) -> p j", p=P)).then_inc(setup.sem, 16)

                @block.vector
                def _(dve):
                    nc.vector.memset(pay[:, :, 3], 0.0)
                    dve.wait_ge(setup.sem, setup.at(48))
                    nc.vector.tensor_copy(pay[:, :, 0:2].rearrange("p j c -> p c j"), pi[:, :, :])
                    nc.vector.tensor_copy(pay[:, :, 2], pf[:, :])
            setup.base += 48
            sort_pass(0, pay, 0, False)
            sort_pass(1, pay, 0, True)
            with nc.Block() as block:
                @block.vector
                def _(dve):
                    nc.vector.tensor_copy(pf[:, :], pay[:, :, 0])
                    nc.vector.tensor_copy(ew_s[:, :], pay[:, :, 2])
                    nc.vector.tensor_copy(pi[:, :, :], pay[:, :, 0:2].rearrange("p j c -> p c j")).then_inc(step.sem, 1)

                @block.sync
                def _(sp):
                    sp.wait_ge(step.sem, step.at(1))
                    sp.dma_start(src_s.rearrange("(p j) -> p j", p=P), pi[:, 0, :]).then_inc(setup.sem, 16)
                    sp.dma_start(dst_s.rearrange("(p j) -> p j", p=P), pi[:, 1, :]).then_inc(setup.sem, 16)
                    sp.wait_ge(setup.sem, setup.at(32))
            step.base += 1
            setup.base += 32
            edge_flags("src", pf)
        with ExitStack() as c:
            di = sb("di", [P, EC], i32, c)
            df = sb("df", [P, EC], fp32, c)
            ti = sb("ti", [P, EC], i32, c)
            tf = sb("tf", [P, EC], fp32, c)
            tm = sb("tm", [P, 2, EC], fp32, c)
            wcb = sb("wcb", [P, R * B], fp32, c)
            with nc.Block() as block:
                @block.sync
                def _(sp):
                    sp.dma_start(di[:, :], dst.rearrange("(p j) -> p j", p=P)).then_inc(setup.sem, 16)
                    sp.dma_start(ti[:, :], etype.rearrange("(p j) -> p j", p=P)).then_inc(setup.sem, 16)
                    sp.dma_start(wcb[:, :], wcomp.rearrange("(o r) b -> o (r b)", o=1).broadcast_to([P, R * B]))\
                        .then_inc(setup.sem, 16)

                @block.vector
                def _(dve):
                    nc.vector.memset(wc_e[:, :, :], 0.0)
                    dve.wait_ge(setup.sem, setup.at(48))
                    nc.vector.tensor_copy(df[:, :], di[:, :])
                    nc.vector.tensor_copy(tf[:, :], ti[:, :])
                    nc.vector.drain()
                    for r in range(R):
                        nc.vector.tensor_scalar(tm[:, r % 2, :], tf[:, :], float(r), None, ALU.is_equal)
                        nc.vector.drain()
                        for b in range(B):
                            nc.vector.scalar_tensor_tensor(wc_e[:, :, b], tm[:, r % 2, :], wcb[:, r * B + b:r * B + b + 1],
                                                           wc_e[:, :, b], ALU.mult, ALU.add)
            setup.base += 48
            edge_flags("dst", df)


        wcat = sb("wcat", [P, 2 * D + 2 * H])
        wuv = sb("wuv", [P, 2 * D])
        wl = sb("wl", [P, D])
        wlp = sb("wlp", [P, D])
        wb = sb("wb", [P, B, D])
        wf = sb("wf", [P, 4, D])
        gb = sb("gb", [P, 2, D])
        w2b = sb("w2b", [P, D])
        b2b = sb("b2b", [P, 1])
        bcat = sb("bcat", [1, 2 * D + 2 * H])
        buv = sb("buv", [1, 2 * D])
        bl_r = sb("bl_r", [1, D])
        hb_r = sb("hb_r", [1, D])
        with ExitStack() as c:
            at = sb("at", [P, 2, D], fp32, c)
            pt = sb("pt", [P, 2, D], fp32, c)
            br = sb("br", [1, 2, D], fp32, c)

            def row(v):
                return v.rearrange("(o d) -> o d", o=1)
            with nc.Block() as block:
                @block.sync
                def _(sp):
                    loads = [(wcat[:, 0:D], W), (wcat[:, D + 2 * H:], skip_W),
                             (wuv[:, 0:D], W1[0:D, :]), (wuv[:, D:2 * D], W1[D:2 * D, :]), (wl[:, :], Wl),
                             (wlp[:, :], loop_W), (wb[:, :, :], wbase.rearrange("b i o -> i b o")),
                             (wf[:, :, :], lw.rearrange("k i o -> i k o")),
                             (gb[:, 0, :], row(ln_g).broadcast_to([P, D])), (gb[:, 1, :], row(ln_b).broadcast_to([P, D])),
                             (w2b[:, :], W2.rearrange("d o -> o d").broadcast_to([P, D])),
                             (b2b[:, :], row(b2).broadcast_to([P, 1])),
                             (at[:, 0, :], att_s.rearrange("(o h) c -> o (h c)", o=1).broadcast_to([P, D])),
                             (at[:, 1, :], att_d.rearrange("(o h) c -> o (h c)", o=1).broadcast_to([P, D])),
                             (br[0:1, 0, :], row(gat_b)), (br[0:1, 1, :], row(skip_b)),
                             (buv[0:1, 0:D], row(b1)), (bl_r[0:1, :], row(bl)), (hb_r[0:1, :], row(h_bias))]
                    for o, i in loads:
                        sp.dma_start(o, i).then_inc(setup.sem, 16)
                    assert len(loads) == 19

                @block.vector
                def _(dve):
                    nc.vector.memset(bcat[:, :], 0.0)
                    nc.vector.memset(buv[0:1, D:2 * D], 0.0)
                    dve.wait_ge(setup.sem, setup.at(16 * 19))
                    for m in range(2):
                        nc.vector.tensor_tensor(pt[:, m, :], wcat[:, 0:D], at[:, m, :], ALU.mult)
                    nc.vector.drain()
                    nc.vector.tensor_reduce(wcat[:, D:D + 2 * H], pt[:, :, :].rearrange("p m (h c) -> p (m h) c", c=C),
                                            AX.X, ALU.add)
                    nc.vector.tensor_tensor(bcat[0:1, D + 2 * H:], br[0:1, 0, :], br[0:1, 1, :], ALU.add)
        setup.base += 16 * 19

        def sp_stream(sp, load, store):
            for h in range(2):
                load(h, h, 0)
            with sp.Fori(1, NB // 2) as i:
                for h in range(2):
                    load(2 * i + h, h, i)
                    store(2 * i + (h - 2), h, i - 1)
            for h in range(2):
                store(NB - 2 + h, h, NB // 2 - 1)

        def stored(eng, n):
            for h in range(2):
                eng.wait_ge(st_done[h].sem, st_done[h].at(16 * n * NB // 2))

        def stats(xt, st, mv):
            for g in range(K):
                nc.vector.bn_stats(st[:, g, :], xt[:, g, :])
            nc.vector.drain()
            for g in range(K):
                q = nc.vector.bn_aggr(mv[:, g, :], st[:, g, :])
            return q

        def scale_shift(mv, sd, rs, nm):
            nc.vector.reciprocal(rs, sd)
            nc.vector.drain()
            return nc.vector.scalar_tensor_tensor(nm, mv, -1.0, rs, ALU.mult, ALU.mult)

        class Product:

            def __init__(self, c, name, width, per):
                self.tp = ps(f"tp_{name}", [P, 2, 512], fp32, c)
                self.mm = ps(f"mm_{name}", [P, 4, 512], fp32, c)
                self.hT = sb(f"hT_{name}", [P, K * D], fp32, c)
                self.per = per

            def pe(self, pe, b, n, rows, w, bias, rdy):
                at = b * self.per + n
                pe.wait_ge(rdy.sem, rdy.at(b + 1))
                for g in range(K):
                    q = nc.tensor.transpose(self.tp[:, g // 4, (g % 4) * D:(g % 4 + 1) * D], rows[:, g, :], ident[:, :])
                    if g == 3 or g == K - 1:
                        q.then_inc(tp_rdy.sem, 1)
                width = w.shape[-1]
                for g in range(K):
                    if g == 0 or g == 4:
                        pe.wait_ge(hT_rdy.sem, hT_rdy.at(at * 2 + (1 if g == 0 else 2)))
                    pe.wait_ge(mm_free.sem, mm_free.at(at * K + (g - 3)))
                    o = self.mm[:, g % 4, 0:width]
                    nc.tensor.matmul(o, ones[0:1, :], bias, start=True, stop=False)
                    nc.tensor.matmul(o, self.hT[:, g * D:(g + 1) * D], w, start=False, stop=True)\
                        .then_inc(mm_rdy.sem, 1)

            def act_copy(self, act, b, n):
                at = b * self.per + n
                act.wait_ge(tp_rdy.sem, tp_rdy.at(at * 2 + 1))
                nc.scalar.activation(self.hT[:, 0:512], self.tp[:, 0, :], ACT.Copy).then_inc(hT_rdy.sem, 1)
                act.wait_ge(tp_rdy.sem, tp_rdy.at(at * 2 + 2))
                nc.scalar.activation(self.hT[:, 512:K * D], self.tp[:, 1, 0:K * D - 512], ACT.Copy).then_inc(hT_rdy.sem, 1)

            def act_take(self, act, b, n, o, func=ACT.Copy):
                at = b * self.per + n
                for g in range(K):
                    act.wait_ge(mm_rdy.sem, mm_rdy.at(at * K + g + 1))
                    nc.scalar.activation(o[:, g, :], self.mm[:, g % 4, 0:o.shape[-1]], func).then_inc(mm_free.sem, 1)

            def end(self):
                n = NB * self.per
                tp_rdy.base += 2 * n
                hT_rdy.base += 2 * n
                mm_rdy.base += K * n
                mm_free.base += K * n

        def stage_base(nd=0, na=0, loads=0, stores=0, gathers=None, idx=0):
            d2a.base += nd * NB
            a2d.base += na * NB
            for h in range(2):
                in_rdy[h].base += 16 * loads * NB // 2
                st_done[h].base += 16 * stores * NB // 2
                idx_rdy[h].base += 16 * idx * NB // 2
                for t in gathers or ():
                    t[h].base += 16 * K * NB // 2

        xn = nrows(x)
        with ExitStack() as c:
            xin = sb("xin", [P, 2, K, D], fp32, c)
            st = sb("st", [P, 2, K, 6], fp32, c)
            mv = sb("mv", [P, 2, K, 2], fp32, c)
            sd = sb("sd", [P, 2, K], fp32, c)
            rs = sb("rs", [P, 2, K], fp32, c)
            nm = sb("nm", [P, 2, K], fp32, c)
            hh = sb("hh", [P, 2, K, D], fp32, c)
            o0 = sb("o0", [P, 2, K, 2 * D + 2 * H], fp32, c)
            pr = Product(c, "n0", 2 * D + 2 * H, 1)
            with nc.Block() as block:
                @block.sync
                def _(sp):
                    def load(b, h, i):
                        sp.wait_ge(dve_done.sem, dve_done.at(b - 1))
                        sp.nop(nofuse=True)
                        sp.wait_ge(act_done.sem, act_done.at(b - 1))
                        sp.nop(nofuse=True)
                        sp.dma_start(xin[:, h, :, :].rearrange("p g d -> p (g d)"), pick(xn, b)).then_inc(in_rdy[h].sem, 16)

                    def store(b, h, i):
                        sp.wait_ge(act_done.sem, act_done.at(b + 1))
                        sp.nop(nofuse=True)
                        sp.dma_start(pick(nparts(G0, 0, D + H), b), o0[:, h, :, 0:D + H]).then_inc(st_done[h].sem, 16)
                        sp.dma_start(pick(nparts(AD, 0, H), b), o0[:, h, :, D + H:D + 2 * H]).then_inc(st_done[h].sem, 16)
                        sp.dma_start(pick(nparts(SK, 0, D), b), o0[:, h, :, D + 2 * H:]).then_inc(st_done[h].sem, 16)
                    sp_stream(sp, load, store)
                    stored(sp, 3)

                @block.vector
                def _(dve):
                    def body(b, h, i):
                        dve.wait_ge(in_rdy[h].sem, in_rdy[h].at(16 * i + 16))
                        stats(xin[:, h], st[:, h], mv[:, h]).then_inc(d2a.sem, 1)
                        dve.wait_ge(a2d.sem, a2d.at(b + 1))
                        scale_shift(mv[:, h, :, 0], sd[:, h, :], rs[:, h, :], nm[:, h, :]).then_inc(dve_done.sem, 1)
                    blocks(dve, body)

                @block.scalar
                def _(act):
                    def body(b, h, i):
                        act.wait_ge(d2a.sem, d2a.at(b + 1))
                        nc.scalar.activation(sd[:, h, :], mv[:, h, :, 1], ACT.Sqrt, bias=eps5[:, :]).then_inc(a2d.sem, 1)
                        act.wait_ge(dve_done.sem, dve_done.at(b + 1))
                        for g in range(K):
                            q = nc.scalar.activation(hh[:, h, g, :], xin[:, h, g, :], ACT.Relu,
                                                     bias=nm[:, h, g:g + 1], scale=rs[:, h, g:g + 1])
                        q.then_inc(for_pe.sem, 1)
                        pr.act_copy(act, b, 0)
                        act.wait_ge(st_done[h].sem, st_done[h].at(48 * i))
                        pr.act_take(act, b, 0, o0[:, h])
                        act.drain()
                        act.sem_inc(act_done.sem, 1)
                    blocks(act, body)

                @block.tensor
                def _(pe):
                    def body(b, h, i):
                        pr.pe(pe, b, 0, hh[:, h], wcat[:, :], bcat[0:1, :], for_pe)
                    blocks(pe, body)
            pr.end()
            for_pe.base += NB
            dve_done.base += NB
            act_done.base += NB
            stage_base(nd=1, na=1, loads=1, stores=3)

        def gather_rows(pool, slot, slot_rdy, table, rows, rdy):
            def body(b, h, i):
                pool.wait_ge(slot_rdy[h].sem, slot_rdy[h].at(16 * i + 16))
                pool.nop(nofuse=True)
                for g in range(K):
                    gather(pool, rows[:, h, g, :], table, slot[:, h, g:g + 1]).then_inc(rdy[h].sem, 16)
            return body

        def add_carry(name, table, tail, width):
            with ExitStack() as c:
                fr = sb(f"fr_{table.name}", [P, table.shape[1]], fp32, c)
                cp = ps(f"cp_{table.name}", [P, 512], fp32, c)
                with nc.Block() as block:
                    @block.gpsimd
                    def _(pool):
                        gather(pool, fr[:, :], table, fix[name][:, :]).then_inc(pdma.sem, 16)
                        pool.wait_ge(step.sem, step.at(1))
                        pool.indirect_dma_start(out=table[:, :], in_=fr[:, :], in_offset=None,
                                                out_offset=bass.IndirectOffsetOnAxis(ap=fix[name][:, :], axis=0))\
                            .then_inc(pdma.sem, 16)
                        pool.wait_ge(pdma.sem, pdma.at(32))

                    @block.tensor
                    def _(pe):
                        nc.tensor.matmul(cp[:, 0:width], carry[name][:, :], tail[:, 0:width], start=True, stop=True)\
                            .then_inc(mm_rdy.sem, 1)

                    @block.vector
                    def _(dve):
                        dve.wait_ge(pdma.sem, pdma.at(16))
                        dve.wait_ge(mm_rdy.sem, mm_rdy.at(1))
                        nc.vector.tensor_tensor(fr[:, 0:width], fr[:, 0:width], cp[:, 0:width], ALU.add)\
                            .then_inc(step.sem, 1)
                pdma.base += 32
                step.base += 1
                mm_rdy.base += 1

        WT = D + 2 * H
        with ExitStack() as c:
            ib = sb("e0_ib", [P, 2, K], i32, c)
            jb = sb("e0_jb", [P, 2, K], i32, c)
            rst = sb("e0_rst", [P, EC], fp32, c)
            xr = sb("e0_xr", [P, 2, K, D + H], fp32, c)
            ar = sb("e0_ar", [P, 2, K, H], fp32, c)
            eb = sb("e0_eb", [P, K, H], fp32, c)
            mb = sb("e0_mb", [P, 2, H, K + 1], fp32, c)
            zr = sb("e0_zr", [P, 2, H, K + 1], fp32, c)
            fg = sb("e0_fg", [P, 2, 2, H, K], fp32, c)
            S = sb("e0_S", [P, 2, K, WT], fp32, c)
            src_e, dst_e, t0e = ecol(src), ecol(dst), erows(T0)
            with nc.Block() as block:
                @block.sync
                def _(sp):
                    def load(b, h, i):
                        sp.wait_ge(dve_done.sem, dve_done.at(b - 1))
                        sp.nop(nofuse=True)
                        sp.dma_start(ib[:, h, :], pick(src_e, b)).then_inc(idx_rdy[h].sem, 16)
                        sp.dma_start(jb[:, h, :], pick(dst_e, b)).then_inc(idy_rdy[h].sem, 16)

                    def store(b, h, i):
                        sp.wait_ge(dve_done.sem, dve_done.at(b + 1))
                        sp.nop(nofuse=True)
                        sp.dma_start(pick(t0e, b), S[:, h, :, :].rearrange("p g d -> p (g d)")).then_inc(st_done[h].sem, 16)
                    sp_stream(sp, load, store)
                    stored(sp, 1)

                @block.gpsimd
                def _(pool):
                    rows = gather_rows(pool, ib, idx_rdy, G0, xr, row_rdy)
                    scores = gather_rows(pool, jb, idy_rdy, AD, ar, roy_rdy)

                    def body(b, h, i):
                        scores(b, h, i)
                        rows(b, h, i)
                    blocks(pool, body)

                @block.vector
                def _(dve):
                    nc.vector.tensor_scalar(rst[:, :], cont["dst"][:, :], -1.0, NEG, ALU.add, ALU.mult)
                    nc.vector.memset(mb[:, :, :, :], -NEG)
                    nc.vector.memset(zr[:, :, :, :], 0.0)
                    nc.vector.memset(S[:, :, :, :], 0.0)
                    nc.vector.drain()

                    def body(b, h, i):
                        dve.wait_ge(row_rdy[h].sem, row_rdy[h].at(16 * K * i + 16 * K))
                        dve.wait_ge(roy_rdy[h].sem, roy_rdy[h].at(16 * K * i + 16 * K))
                        nc.vector.tensor_tensor(eb[:, :, :], xr[:, h, :, D:D + H], ar[:, h, :, :], ALU.add)
                        nc.vector.tensor_copy(mb[:, h, :, 0], mb[:, 1 - h, :, K])
                        nc.vector.tensor_copy(zr[:, h, :, 0], zr[:, 1 - h, :, K])
                        nc.vector.drain()
                        nc.vector.scalar_tensor_tensor(eb[:, :, :], eb[:, :, :], 0.2, eb[:, :, :], ALU.mult, ALU.max)
                        nc.vector.drain()
                        for a in range(H):
                            nc.vector.tensor_tensor_scan(mb[:, h, a, 1:K + 1], rst[:, bass.ds(b * K, K)], eb[:, :, a],
                                                         mb[:, h, a, 0:1], ALU.add, ALU.max)
                        nc.vector.drain()
                        nc.vector.tensor_tensor(fg[:, h, 1], eb[:, :, :].rearrange("p g a -> p a g"),
                                                mb[:, h, :, 1:K + 1], ALU.subtract)
                        nc.vector.tensor_tensor(fg[:, h, 0], mb[:, h, :, 0:K], mb[:, h, :, 1:K + 1], ALU.subtract)
                        nc.vector.drain()
                        nc.vector.tensor_tensor(fg[:, h, 0], fg[:, h, 0],
                                                rst[:, bass.ds(b * K, K)].rearrange("p (o g) -> p o g", o=1)
                                                .broadcast_to([P, H, K]), ALU.add).then_inc(d2a.sem, 1)
                        dve.wait_ge(a2d.sem, a2d.at(b + 1))
                        for a in range(H):
                            nc.vector.tensor_tensor_scan(zr[:, h, a, 1:K + 1], fg[:, h, 0, a, :], fg[:, h, 1, a, :],
                                                         zr[:, h, a, 0:1], ALU.mult, ALU.add)
                        xv = xr[:, h, :, 0:D].rearrange("p g (a c) -> p g a c", a=H)
                        nc.vector.tensor_tensor(xv, xv, fg[:, h, 1].rearrange("p a g -> p g a").unsqueeze(3)
                                                .broadcast_to([P, K, H, C]), ALU.mult)
                        dve.wait_ge(st_done[h].sem, st_done[h].at(16 * i))
                        for g in range(K):
                            pv = S[:, h, g - 1, 0:D] if g else S[:, 1 - h, K - 1, 0:D]
                            nc.vector.tensor_tensor(S[:, h, g, 0:D].rearrange("p (a c) -> p a c", a=H),
                                                    pv.rearrange("p (a c) -> p a c", a=H),
                                                    fg[:, h, 0, :, g].unsqueeze(2).broadcast_to([P, H, C]), ALU.mult)
                            nc.vector.drain()
                            nc.vector.tensor_tensor(S[:, h, g, 0:D], S[:, h, g, 0:D], xr[:, h, g, 0:D], ALU.add)
                            nc.vector.drain()
                        nc.vector.tensor_copy(S[:, h, :, D:D + H], zr[:, h, :, 1:K + 1].rearrange("p a g -> p g a"))
                        nc.vector.tensor_copy(S[:, h, :, D + H:WT], mb[:, h, :, 1:K + 1].rearrange("p a g -> p g a"))\
                            .then_inc(dve_done.sem, 1)
                    blocks(dve, body)

                @block.scalar
                def _(act):
                    def body(b, h, i):
                        act.wait_ge(d2a.sem, d2a.at(b + 1))
                        v = fg[:, h].rearrange("p m a g -> p (m a g)")
                        nc.scalar.activation(v, v, ACT.Exp).then_inc(a2d.sem, 1)
                    blocks(act, body)
            dve_done.base += NB
            stage_base(nd=1, na=1, stores=1, gathers=(row_rdy, roy_rdy), idx=1)
            for h in range(2):
                idy_rdy[h].base += 16 * NB // 2

            tail = S[:, 1, K - 1, :]
            with ExitStack() as c2:
                fr = sb("f0_fr", [P, WT], fp32, c2)
                cT = sb("f0_cT", [P, P], fp32, c2)
                pen = sb("f0_pen", [P, P], fp32, c2)
                dg = sb("f0_dg", [P, H, P], fp32, c2)
                vl = sb("f0_vl", [P, H, P], fp32, c2)
                vT = sb("f0_vT", [P, H, P], fp32, c2)
                top = sb("f0_top", [P, H], fp32, c2)
                ab = sb("f0_ab", [P, 2, H], fp32, c2)
                mx = sb("f0_mx", [P, H], fp32, c2)
                cs = sb("f0_cs", [P, D + H], fp32, c2)
                pc = ps("f0_pc", [P, 512], fp32, c2)
                pm = ps("f0_pm", [P, H * P], fp32, c2)
                pv = ps("f0_pv", [P, H * P], fp32, c2)
                po = ps("f0_po", [P, 512], fp32, c2)
                with nc.Block() as block:
                    @block.gpsimd
                    def _(pool):
                        gather(pool, fr[:, :], T0, fix["dst"][:, :]).then_inc(pdma.sem, 16)
                        pool.wait_ge(step.sem, step.at(3))
                        pool.indirect_dma_start(out=T0[:, :], in_=fr[:, :], in_offset=None,
                                                out_offset=bass.IndirectOffsetOnAxis(ap=fix["dst"][:, :], axis=0))\
                            .then_inc(pdma.sem, 16)
                        pool.wait_ge(pdma.sem, pdma.at(32))

                    @block.tensor
                    def _(pe):
                        nc.tensor.transpose(pc[:, 0:P], carry["dst"][:, :], ident[:, :]).then_inc(mm_rdy.sem, 1)
                        pe.wait_ge(step.sem, step.at(1))
                        nc.tensor.matmul(pm[:, :], ones[:, :], dg[:, :, :].rearrange("p a q -> p (a q)"),
                                         start=True, stop=True).then_inc(mm_rdy.sem, 1)
                        pe.wait_ge(step.sem, step.at(2))
                        for a in range(H):
                            q = nc.tensor.transpose(pv[:, a * P:(a + 1) * P], vl[:, a, :], ident[:, :])
                        q.then_inc(mm_rdy.sem, 1)
                        pe.wait_ge(for_pe.sem, for_pe.at(1))
                        for a in range(H):
                            nc.tensor.matmul(po[:, a * C:(a + 1) * C], vT[:, a, :], tail[:, a * C:(a + 1) * C],
                                             start=True, stop=True)
                            q = nc.tensor.matmul(po[:, D + a:D + a + 1], vT[:, a, :], tail[:, D + a:D + a + 1],
                                                 start=True, stop=True)
                        q.then_inc(mm_rdy.sem, 1)

                    @block.vector
                    def _(dve):
                        for a in range(H):
                            q = nc.vector.tensor_scalar(dg[:, a, :], ident[:, :], tail[:, D + H + a:D + H + a + 1],
                                                        None, ALU.mult)
                        q.then_inc(step.sem, 1)
                        dve.wait_ge(mm_rdy.sem, mm_rdy.at(1))
                        nc.vector.tensor_copy(cT[:, :], pc[:, 0:P])
                        nc.vector.drain()
                        nc.vector.tensor_scalar(pen[:, :], cT[:, :], -1.0, NEG, ALU.add, ALU.mult)
                        nc.vector.drain()
                        dve.wait_ge(mm_rdy.sem, mm_rdy.at(2))
                        for a in range(H):
                            nc.vector.tensor_tensor(vl[:, a, :], pm[:, a * P:(a + 1) * P], pen[:, :], ALU.add)
                        nc.vector.drain()
                        nc.vector.tensor_reduce(top[:, :], vl[:, :, :], AX.X, ALU.max)
                        nc.vector.drain()
                        nc.vector.tensor_tensor(vl[:, :, :], vl[:, :, :], top[:, :].unsqueeze(2).broadcast_to([P, H, P]),
                                                ALU.subtract).then_inc(d2a.sem, 1)
                        dve.wait_ge(a2d.sem, a2d.at(1))
                        for a in range(H):
                            q = nc.vector.tensor_tensor(vl[:, a, :], vl[:, a, :], cT[:, :], ALU.mult)
                        q.then_inc(step.sem, 1)
                        dve.wait_ge(pdma.sem, pdma.at(16))
                        nc.vector.tensor_tensor(mx[:, :], fr[:, D + H:WT], top[:, :], ALU.max)
                        nc.vector.drain()
                        nc.vector.tensor_tensor(ab[:, 0, :], fr[:, D + H:WT], mx[:, :], ALU.subtract)
                        nc.vector.tensor_tensor(ab[:, 1, :], top[:, :], mx[:, :], ALU.subtract).then_inc(d2a.sem, 1)
                        dve.wait_ge(mm_rdy.sem, mm_rdy.at(3))
                        nc.vector.tensor_copy(vT[:, :, :].rearrange("p a q -> p (a q)"), pv[:, :]).then_inc(for_pe.sem, 1)
                        dve.wait_ge(a2d.sem, a2d.at(2))
                        dve.wait_ge(mm_rdy.sem, mm_rdy.at(4))
                        for o, w in ((0, C), (D, 1)):
                            f = fr[:, o:o + H * w].rearrange("p (a c) -> p a c", a=H)
                            nc.vector.tensor_tensor(f, f, ab[:, 0, :].unsqueeze(2).broadcast_to([P, H, w]), ALU.mult)
                            nc.vector.tensor_tensor(cs[:, o:o + H * w].rearrange("p (a c) -> p a c", a=H),
                                                    po[:, o:o + H * w].rearrange("p (a c) -> p a c", a=H),
                                                    ab[:, 1, :].unsqueeze(2).broadcast_to([P, H, w]), ALU.mult)
                        nc.vector.drain()
                        nc.vector.tensor_copy(fr[:, D + H:WT], mx[:, :])
                        nc.vector.tensor_tensor(fr[:, 0:D + H], fr[:, 0:D + H], cs[:, :], ALU.add).then_inc(step.sem, 1)

                    @block.scalar
                    def _(act):
                        act.wait_ge(d2a.sem, d2a.at(1))
                        nc.scalar.activation(vl[:, :, :], vl[:, :, :], ACT.Exp).then_inc(a2d.sem, 1)
                        act.wait_ge(d2a.sem, d2a.at(2))
                        nc.scalar.activation(ab[:, :, :], ab[:, :, :], ACT.Exp).then_inc(a2d.sem, 1)
                pdma.base += 32
                step.base += 3
                mm_rdy.base += 4
                for_pe.base += 1
                d2a.base += 2
                a2d.base += 2

        with ExitStack() as c:
            ib = sb("n1_ib", [P, 2, K], i32, c)
            tr = sb("n1_tr", [P, 2, K, WT], fp32, c)
            g0 = sb("n1_g0", [P, 2, K, D + H], fp32, c)
            ad = sb("n1_ad", [P, 2, K, H], fp32, c)
            sk = sb("n1_sk", [P, 2, K, D], fp32, c)
            xin = sb("n1_xin", [P, 2, K, D], fp32, c)
            eb = sb("n1_eb", [P, K, H], fp32, c)
            mx = sb("n1_mx", [P, K, H], fp32, c)
            fg = sb("n1_fg", [P, 2, K, H], fp32, c)
            st = sb("n1_st", [P, K, 6], fp32, c)
            mv = sb("n1_mv", [P, 2, K, 2], fp32, c)
            sd = sb("n1_sd", [P, 2, K], fp32, c)
            rs = sb("n1_rs", [P, 2, K], fp32, c)
            nm = sb("n1_nm", [P, 2, K], fp32, c)
            x1 = sb("n1_x1", [P, 2, K, D], fp32, c)
            hh = sb("n1_hh", [P, 2, K, D], fp32, c)
            uv = sb("n1_uv", [P, 2, K, 2 * D], fp32, c)
            pr = Product(c, "n1", 2 * D, 1)
            lst, x1n = ncol(last_dst), nrows(X1)
            with nc.Block() as block:
                @block.sync
                def _(sp):
                    def load(b, h, i):
                        sp.wait_ge(dve_done.sem, dve_done.at(b - 1))
                        sp.nop(nofuse=True)
                        sp.dma_start(ib[:, h, :], pick(lst, b)).then_inc(idx_rdy[h].sem, 16)
                        sp.dma_start(g0[:, h, :, :].rearrange("p g d -> p (g d)"), pick(nrows(G0), b)).then_inc(in_rdy[h].sem, 16)
                        sp.dma_start(ad[:, h, :, :].rearrange("p g d -> p (g d)"), pick(nrows(AD), b)).then_inc(in_rdy[h].sem, 16)
                        sp.dma_start(sk[:, h, :, :].rearrange("p g d -> p (g d)"), pick(nrows(SK), b)).then_inc(in_rdy[h].sem, 16)
                        sp.dma_start(xin[:, h, :, :].rearrange("p g d -> p (g d)"), pick(xn, b)).then_inc(in_rdy[h].sem, 16)

                    def store(b, h, i):
                        sp.wait_ge(act_done.sem, act_done.at(b + 1))
                        sp.nop(nofuse=True)
                        sp.dma_start(pick(x1n, b), x1[:, h, :, :].rearrange("p g d -> p (g d)")).then_inc(st_done[h].sem, 16)
                        sp.dma_start(pick(nparts(P1, 0, D), b), hh[:, h]).then_inc(st_done[h].sem, 16)
                        sp.dma_start(pick(nparts(P1, D, 2 * D), b), uv[:, h, :, D:2 * D]).then_inc(st_done[h].sem, 16)
                        sp.dma_start(pick(nparts(U1, 0, D), b), uv[:, h, :, 0:D]).then_inc(st_done[h].sem, 16)
                    sp_stream(sp, load, store)
                    stored(sp, 4)

                @block.gpsimd
                def _(pool):
                    blocks(pool, gather_rows(pool, ib, idx_rdy, T0, tr, nrow_rdy))

                @block.vector
                def _(dve):
                    def body(b, h, i):
                        dve.wait_ge(in_rdy[h].sem, in_rdy[h].at(64 * i + 64))
                        dve.wait_ge(nrow_rdy[h].sem, nrow_rdy[h].at(16 * K * i + 16 * K))
                        T, G = tr[:, h], g0[:, h]
                        nc.vector.tensor_tensor(eb[:, :, :], G[:, :, D:D + H], ad[:, h], ALU.add)
                        nc.vector.drain()
                        nc.vector.scalar_tensor_tensor(eb[:, :, :], eb[:, :, :], 0.2, eb[:, :, :], ALU.mult, ALU.max)
                        nc.vector.drain()
                        nc.vector.tensor_tensor(mx[:, :, :], eb[:, :, :], T[:, :, D + H:WT], ALU.max)
                        nc.vector.drain()
                        nc.vector.tensor_tensor(fg[:, 0], T[:, :, D + H:WT], mx[:, :, :], ALU.subtract)
                        nc.vector.tensor_tensor(fg[:, 1], eb[:, :, :], mx[:, :, :], ALU.subtract).then_inc(d2a.sem, 1)
                        dve.wait_ge(a2d.sem, a2d.at(3 * b + 1))
                        Tv = T[:, :, 0:D].rearrange("p g (a c) -> p g a c", a=H)
                        Gv = G[:, :, 0:D].rearrange("p g (a c) -> p g a c", a=H)
                        nc.vector.tensor_tensor(T[:, :, D:D + H], T[:, :, D:D + H], fg[:, 0], ALU.mult)
                        nc.vector.tensor_tensor(Tv, Tv, fg[:, 0].unsqueeze(3).broadcast_to([P, K, H, C]), ALU.mult)
                        nc.vector.tensor_tensor(Gv, Gv, fg[:, 1].unsqueeze(3).broadcast_to([P, K, H, C]), ALU.mult)
                        nc.vector.drain()
                        nc.vector.scalar_tensor_tensor(fg[:, 1], fg[:, 1], 1e-16, T[:, :, D:D + H], ALU.add, ALU.add)
                        nc.vector.tensor_tensor(T[:, :, 0:D], T[:, :, 0:D], G[:, :, 0:D], ALU.add)
                        nc.vector.drain()
                        nc.vector.reciprocal(fg[:, 1], fg[:, 1])
                        nc.vector.drain()
                        nc.vector.tensor_tensor(Tv, Tv, fg[:, 1].unsqueeze(3).broadcast_to([P, K, H, C]), ALU.mult)
                        nc.vector.drain()
                        nc.vector.tensor_tensor(T[:, :, 0:D], T[:, :, 0:D], sk[:, h], ALU.add)
                        nc.vector.drain()
                        stats(T[:, :, 0:D], st, mv[:, 0]).then_inc(d2a.sem, 1)
                        dve.wait_ge(a2d.sem, a2d.at(3 * b + 2))
                        scale_shift(mv[:, 0, :, 0], sd[:, 0, :], rs[:, 0, :], nm[:, 0, :])
                        nc.vector.drain()
                        for g in range(K):
                            nc.vector.tensor_scalar(T[:, g, 0:D], T[:, g, 0:D], rs[:, 0, g:g + 1], nm[:, 0, g:g + 1],
                                                    ALU.mult, ALU.add)
                        nc.vector.drain()
                        for m, op in ((0, ALU.mult), (1, ALU.add)):
                            nc.vector.tensor_tensor(T[:, :, 0:D], T[:, :, 0:D],
                                                    gb[:, m:m + 1, :].broadcast_to([P, K, D]), op)
                            nc.vector.drain()
                        dve.wait_ge(st_done[h].sem, st_done[h].at(64 * i))
                        nc.vector.tensor_tensor(x1[:, h], T[:, :, 0:D], xin[:, h], ALU.add)
                        nc.vector.drain()
                        stats(x1[:, h], st, mv[:, 1]).then_inc(d2a.sem, 1)
                        dve.wait_ge(a2d.sem, a2d.at(3 * b + 3))
                        scale_shift(mv[:, 1, :, 0], sd[:, 1, :], rs[:, 1, :], nm[:, 1, :]).then_inc(dve_done.sem, 1)
                    blocks(dve, body)

                @block.scalar
                def _(act):
                    def body(b, h, i):
                        act.wait_ge(d2a.sem, d2a.at(3 * b + 1))
                        nc.scalar.activation(fg[:, :, :, :], fg[:, :, :, :], ACT.Exp).then_inc(a2d.sem, 1)
                        for m in range(2):
                            act.wait_ge(d2a.sem, d2a.at(3 * b + 2 + m))
                            nc.scalar.activation(sd[:, m, :], mv[:, m, :, 1], ACT.Sqrt, bias=eps5[:, :]).then_inc(a2d.sem, 1)
                        act.wait_ge(dve_done.sem, dve_done.at(b + 1))
                        act.wait_ge(st_done[h].sem, st_done[h].at(64 * i))
                        for g in range(K):
                            q = nc.scalar.activation(hh[:, h, g, :], x1[:, h, g, :], ACT.Relu,
                                                     bias=nm[:, 1, g:g + 1], scale=rs[:, 1, g:g + 1])
                        q.then_inc(for_pe.sem, 1)
                        pr.act_copy(act, b, 0)
                        pr.act_take(act, b, 0, uv[:, h])
                        act.drain()
                        act.sem_inc(act_done.sem, 1)
                    blocks(act, body)

                @block.tensor
                def _(pe):
                    def body(b, h, i):
                        pr.pe(pe, b, 0, hh[:, h], wuv[:, :], buv[0:1, :], for_pe)
                    blocks(pe, body)
            pr.end()
            for_pe.base += NB
            dve_done.base += NB
            act_done.base += NB
            stage_base(nd=3, na=3, loads=4, stores=4, gathers=(nrow_rdy,), idx=1)

        with ExitStack() as c:
            ib = sb("e1_ib", [P, 2, K], i32, c)
            jb = sb("e1_jb", [P, 2, K], i32, c)
            xr = sb("e1_xr", [P, 2, K, 2 * D], fp32, c)
            ur = sb("e1_ur", [P, 2, K, D], fp32, c)
            lg = sb("e1_lg", [P, 2, K], fp32, c)
            mk = sb("e1_mk", [P, 2, K], fp32, c)
            zr = sb("e1_zr", [P, 2, K], fp32, c)
            S = sb("e1_S", [P, 2, K, D + 2], fp32, c)
            with nc.Block() as block:
                @block.sync
                def _(sp):
                    def load(b, h, i):
                        sp.wait_ge(dve_done.sem, dve_done.at(b - 1))
                        sp.nop(nofuse=True)
                        sp.dma_start(ib[:, h, :], pick(ecol(dst_s), b)).then_inc(idx_rdy[h].sem, 16)
                        sp.dma_start(jb[:, h, :], pick(ecol(src_s), b)).then_inc(idy_rdy[h].sem, 16)

                    def store(b, h, i):
                        sp.wait_ge(dve_done.sem, dve_done.at(b + 1))
                        sp.nop(nofuse=True)
                        sp.dma_start(pick(erows(T1), b), S[:, h, :, :].rearrange("p g d -> p (g d)")).then_inc(st_done[h].sem, 16)
                    sp_stream(sp, load, store)
                    stored(sp, 1)

                @block.gpsimd
                def _(pool):
                    rows = gather_rows(pool, ib, idx_rdy, P1, xr, row_rdy)
                    centres = gather_rows(pool, jb, idy_rdy, U1, ur, roy_rdy)

                    def body(b, h, i):
                        rows(b, h, i)
                        centres(b, h, i)
                    blocks(pool, body)

                @block.vector
                def _(dve):
                    nc.vector.memset(S[:, :, :, :], 0.0)
                    nc.vector.memset(zr[:, :, :], 0.0)
                    nc.vector.drain()
                    nc.vector.memset(S[:, :, :, D + 1:D + 2], 1.0)
                    nc.vector.drain()

                    def body(b, h, i):
                        dve.wait_ge(row_rdy[h].sem, row_rdy[h].at(16 * K * i + 16 * K))
                        dve.wait_ge(roy_rdy[h].sem, roy_rdy[h].at(16 * K * i + 16 * K))
                        u = ur[:, h]
                        nc.vector.tensor_tensor(u, u, xr[:, h, :, D:2 * D], ALU.add)
                        nc.vector.drain()
                        nc.vector.tensor_scalar(u, u, 0.0, None, ALU.max)
                        nc.vector.drain()
                        nc.vector.tensor_tensor(u, u, w2b[:, :].unsqueeze(1).broadcast_to([P, K, D]), ALU.mult)
                        nc.vector.drain()
                        nc.vector.tensor_reduce(lg[:, h, :], u, AX.X, ALU.add).then_inc(d2a.sem, 1)
                        dve.wait_ge(a2d.sem, a2d.at(2 * b + 1))
                        nc.vector.tensor_tensor_scan(zr[:, h, :], cont["src"][:, bass.ds(b * K, K)], mk[:, h, :],
                                                     zr[:, 1 - h, K - 1:K], ALU.mult, ALU.add)
                        nc.vector.drain()
                        dve.wait_ge(st_done[h].sem, st_done[h].at(16 * i))
                        nc.vector.tensor_copy(S[:, h, :, D], zr[:, h, :])
                        dve.wait_ge(a2d.sem, a2d.at(2 * b + 2))
                        for g in range(K):
                            pv = S[:, h, g - 1, 0:D] if g else S[:, 1 - h, K - 1, 0:D]
                            q = nc.vector.scalar_tensor_tensor(S[:, h, g, 0:D], pv, cont["src"][:, bass.ds(b * K + g, 1)],
                                                               xr[:, h, g, 0:D], ALU.mult, ALU.add)
                            if g < K - 1:
                                nc.vector.drain()
                        q.then_inc(dve_done.sem, 1)
                        nc.vector.drain()
                    blocks(dve, body)

                @block.scalar
                def _(act):
                    def body(b, h, i):
                        act.wait_ge(d2a.sem, d2a.at(b + 1))
                        nc.scalar.activation(mk[:, h, :], lg[:, h, :], ACT.Sigmoid, bias=b2b[:, :]).then_inc(a2d.sem, 1)
                        act.drain()
                        for g in range(K):
                            q = nc.scalar.activation(xr[:, h, g, 0:D], xr[:, h, g, 0:D], ACT.Copy, scale=mk[:, h, g:g + 1])
                        q.then_inc(a2d.sem, 1)
                    blocks(act, body)
            dve_done.base += NB
            stage_base(nd=1, na=2, stores=1, gathers=(row_rdy, roy_rdy), idx=1)
            for h in range(2):
                idy_rdy[h].base += 16 * NB // 2
            add_carry("src", T1, S[:, 1, K - 1, :], D + 1)

        with ExitStack() as c:
            ib = sb("n2_ib", [P, 2, K], i32, c)
            tr = sb("n2_tr", [P, 2, K, D + 2], fp32, c)
            h1 = sb("n2_h1", [P, 2, K, D], fp32, c)
            x1 = sb("n2_x1", [P, 2, K, D], fp32, c)
            zi = sb("n2_zi", [P, 2, K], fp32, c)
            em = sb("n2_em", [P, 2, K, D], fp32, c)
            y = sb("n2_y", [P, 2, K, D], fp32, c)
            x2 = sb("n2_x2", [P, 2, K, D], fp32, c)
            st = sb("n2_st", [P, K, 6], fp32, c)
            mv = sb("n2_mv", [P, 2, K, 2], fp32, c)
            sd = sb("n2_sd", [P, 2, K], fp32, c)
            rs = sb("n2_rs", [P, 2, K], fp32, c)
            nm = sb("n2_nm", [P, 2, K], fp32, c)
            h2 = sb("n2_h2", [P, 2, K, D], fp32, c)
            lo = sb("n2_lo", [P, 2, K, D], fp32, c)
            pr = Product(c, "n2", D, 2)
            with nc.Block() as block:
                @block.sync
                def _(sp):
                    def load(b, h, i):
                        sp.wait_ge(dve_done.sem, dve_done.at(b - 1))
                        sp.nop(nofuse=True)
                        sp.dma_start(ib[:, h, :], pick(ncol(last_src), b)).then_inc(idx_rdy[h].sem, 16)
                        sp.dma_start(h1[:, h], pick(nparts(P1, 0, D), b)).then_inc(in_rdy[h].sem, 16)
                        sp.dma_start(x1[:, h, :, :].rearrange("p g d -> p (g d)"), pick(nrows(X1), b)).then_inc(in_rdy[h].sem, 16)

                    def store(b, h, i):
                        sp.wait_ge(act_done.sem, act_done.at(b + 1))
                        sp.nop(nofuse=True)
                        for t, o in ((X2, x2), (H2, h2), (LW, lo)):
                            sp.dma_start(pick(nrows(t), b), o[:, h, :, :].rearrange("p g d -> p (g d)")).then_inc(st_done[h].sem, 16)
                    sp_stream(sp, load, store)
                    stored(sp, 3)

                @block.gpsimd
                def _(pool):
                    blocks(pool, gather_rows(pool, ib, idx_rdy, T1, tr, nrow_rdy))

                @block.vector
                def _(dve):
                    def body(b, h, i):
                        dve.wait_ge(in_rdy[h].sem, in_rdy[h].at(32 * i + 32))
                        dve.wait_ge(nrow_rdy[h].sem, nrow_rdy[h].at(16 * K * i + 16 * K))
                        T = tr[:, h]
                        nc.vector.tensor_scalar(zi[:, 0, :], T[:, :, D], 1e-9, None, ALU.add)
                        nc.vector.tensor_scalar(zi[:, 1, :], T[:, :, D + 1], -0.5, 1.0, ALU.mult, ALU.add)
                        nc.vector.drain()
                        nc.vector.reciprocal(zi[:, 0, :], zi[:, 0, :])
                        nc.vector.drain()
                        nc.vector.tensor_scalar(zi[:, 0, :], zi[:, 0, :], 0.5, None, ALU.mult)
                        nc.vector.tensor_tensor(h1[:, h], h1[:, h], zi[:, 1, :].unsqueeze(2).broadcast_to([P, K, D]), ALU.mult)
                        nc.vector.drain()
                        nc.vector.tensor_tensor(T[:, :, 0:D], T[:, :, 0:D], zi[:, 0, :].unsqueeze(2).broadcast_to([P, K, D]), ALU.mult)
                        nc.vector.drain()
                        nc.vector.tensor_tensor(em[:, h], T[:, :, 0:D], h1[:, h], ALU.add).then_inc(for_pe.sem, 1)
                        dve.wait_ge(a2d.sem, a2d.at(2 * b + 1))
                        dve.wait_ge(st_done[h].sem, st_done[h].at(48 * i))
                        nc.vector.tensor_tensor(x2[:, h], y[:, h], x1[:, h], ALU.add)
                        nc.vector.drain()
                        stats(x2[:, h], st, mv[:, h]).then_inc(d2a.sem, 1)
                        dve.wait_ge(a2d.sem, a2d.at(2 * b + 2))
                        scale_shift(mv[:, h, :, 0], sd[:, h, :], rs[:, h, :], nm[:, h, :]).then_inc(dve_done.sem, 1)
                    blocks(dve, body)

                @block.scalar
                def _(act):
                    def body(b, h, i):
                        pr.act_copy(act, b, 0)
                        pr.act_take(act, b, 0, y[:, h], ACT.Relu)
                        act.drain()
                        act.sem_inc(a2d.sem, 1)
                        act.wait_ge(d2a.sem, d2a.at(b + 1))
                        nc.scalar.activation(sd[:, h, :], mv[:, h, :, 1], ACT.Sqrt, bias=eps5[:, :]).then_inc(a2d.sem, 1)
                        act.wait_ge(dve_done.sem, dve_done.at(b + 1))
                        act.wait_ge(st_done[h].sem, st_done[h].at(48 * i))
                        for g in range(K):
                            q = nc.scalar.activation(h2[:, h, g, :], x2[:, h, g, :], ACT.Relu,
                                                     bias=nm[:, h, g:g + 1], scale=rs[:, h, g:g + 1])
                        q.then_inc(for_pe2.sem, 1)
                        pr.act_copy(act, b, 1)
                        pr.act_take(act, b, 1, lo[:, h])
                        act.drain()
                        act.sem_inc(act_done.sem, 1)
                    blocks(act, body)

                @block.tensor
                def _(pe):
                    def body(b, h, i):
                        pr.pe(pe, b, 0, em[:, h], wl[:, :], bl_r[0:1, :], for_pe)
                        pr.pe(pe, b, 1, h2[:, h], wlp[:, :], hb_r[0:1, :], for_pe2)
                    blocks(pe, body)
            pr.end()
            for_pe.base += NB
            for_pe2.base += NB
            dve_done.base += NB
            act_done.base += NB
            stage_base(nd=1, na=2, loads=2, stores=3, gathers=(nrow_rdy,), idx=1)

        with ExitStack() as c:
            ib = sb("e2_ib", [P, 2, K], i32, c)
            xr = sb("e2_xr", [P, 2, K, D], fp32, c)
            xT = sb("e2_xT", [P, 2, D], fp32, c)
            ms = sb("e2_ms", [P, 2, B, D], fp32, c)
            S = sb("e2_S", [P, 2, K, D], fp32, c)
            tp = ps("e2_tp", [P, 2, 512], fp32, c)
            mm = ps("e2_mm", [P, 2, B * D], fp32, c)
            with nc.Block() as block:
                @block.sync
                def _(sp):
                    def load(b, h, i):
                        sp.wait_ge(dve_done.sem, dve_done.at(b - 1))
                        sp.nop(nofuse=True)
                        sp.dma_start(ib[:, h, :], pick(ecol(src), b)).then_inc(idx_rdy[h].sem, 16)

                    def store(b, h, i):
                        sp.wait_ge(dve_done.sem, dve_done.at(b + 1))
                        sp.nop(nofuse=True)
                        sp.dma_start(pick(erows(T2), b), S[:, h, :, :].rearrange("p g d -> p (g d)")).then_inc(st_done[h].sem, 16)
                    sp_stream(sp, load, store)
                    stored(sp, 1)

                @block.gpsimd
                def _(pool):
                    blocks(pool, gather_rows(pool, ib, idx_rdy, H2, xr, row_rdy))

                @block.tensor
                def _(pe):
                    def body(b, h, i):
                        pe.wait_ge(row_rdy[h].sem, row_rdy[h].at(16 * K * i + 16 * K))
                        for g in range(K):
                            pe.wait_ge(hT_rdy.sem, hT_rdy.at(b * K + (g - 1)))
                            nc.tensor.transpose(tp[:, (h + g) % 2, 0:D], xr[:, h, g, :], ident[:, :]).then_inc(tp_rdy.sem, 1)
                            pe.wait_ge(hT_rdy.sem, hT_rdy.at(b * K + g + 1))
                            pe.wait_ge(mm_free.sem, mm_free.at(b * K + g - 1))
                            for m in range(2):
                                q = nc.tensor.matmul(mm[:, (h + g) % 2, m * 512:(m + 1) * 512], xT[:, (h + g) % 2, :],
                                                     wb[:, 4 * m:4 * m + 4, :].rearrange("i b o -> i (b o)"),
                                                     start=True, stop=True)
                            q.then_inc(mm_rdy.sem, 1)
                    blocks(pe, body)

                @block.scalar
                def _(act):
                    def body(b, h, i):
                        for g in range(K):
                            s = (h + g) % 2
                            act.wait_ge(tp_rdy.sem, tp_rdy.at(b * K + g + 1))
                            act.wait_ge(mm_rdy.sem, mm_rdy.at(b * K + g - 1))
                            nc.scalar.activation(xT[:, s, :], tp[:, s, 0:D], ACT.Copy).then_inc(hT_rdy.sem, 1)
                    blocks(act, body)

                @block.vector
                def _(dve):
                    nc.vector.memset(S[:, :, :, :], 0.0)
                    nc.vector.drain()

                    def body(b, h, i):
                        dve.wait_ge(st_done[h].sem, st_done[h].at(16 * i))
                        for g in range(K):
                            s = (h + g) % 2
                            pv = S[:, h, g - 1, :] if g else S[:, 1 - h, K - 1, :]
                            dve.wait_ge(mm_rdy.sem, mm_rdy.at(b * K + g + 1))
                            nc.vector.tensor_tensor(ms[:, s], mm[:, s, :].rearrange("p (b o) -> p b o", b=B),
                                                    wc_e[:, bass.ds(b * K + g, 1), :].rearrange("p o b -> p (o b)")
                                                    .unsqueeze(2).broadcast_to([P, B, D]), ALU.mult)\
                                .then_inc(mm_free.sem, 1)
                            nc.vector.drain()
                            nc.vector.tensor_tensor(ms[:, s, 0:4], ms[:, s, 0:4], ms[:, s, 4:8], ALU.add)
                            nc.vector.drain()
                            nc.vector.tensor_tensor(ms[:, s, 0:2], ms[:, s, 0:2], ms[:, s, 2:4], ALU.add)
                            nc.vector.drain()
                            nc.vector.tensor_tensor(ms[:, s, 0], ms[:, s, 0], ms[:, s, 1], ALU.add)
                            nc.vector.drain()
                            q = nc.vector.scalar_tensor_tensor(S[:, h, g, :], pv, cont["dst"][:, bass.ds(b * K + g, 1)],
                                                               ms[:, s, 0], ALU.mult, ALU.add)
                            if g == K - 1:
                                q.then_inc(dve_done.sem, 1)
                            nc.vector.drain()
                    blocks(dve, body)
            dve_done.base += NB
            for q in (tp_rdy, hT_rdy, mm_rdy, mm_free):
                q.base += EC
            stage_base(stores=1, gathers=(row_rdy,), idx=1)
            add_carry("dst", T2, S[:, 1, K - 1, :], D)

        own = sb("own", [P, K])
        sumq = sb("sumq", [P, 4, D])
        with ExitStack() as c:
            ib = sb("n3_ib", [P, 2, K], i32, c)
            tr = sb("n3_tr", [P, 2, K, D], fp32, c)
            lo = sb("n3_lo", [P, 2, K, D], fp32, c)
            x2 = sb("n3_x2", [P, 2, K, D], fp32, c)
            x3 = sb("n3_x3", [P, 2, K, D], fp32, c)
            st = sb("n3_st", [P, K, 6], fp32, c)
            mv = sb("n3_mv", [P, 2, K, 2], fp32, c)
            sd = sb("n3_sd", [P, 2, K], fp32, c)
            rs = sb("n3_rs", [P, 2, K], fp32, c)
            nm = sb("n3_nm", [P, 2, K], fp32, c)
            h3 = sb("n3_h3", [P, 2, K, D], fp32, c)
            sq = sb("n3_sq", [P, 2, K, D], fp32, c)
            acc = ps("n3_acc", [P, 512], fp32, c)
            with nc.Block() as block:
                @block.sync
                def _(sp):
                    def load(b, h, i):
                        sp.wait_ge(dve_done.sem, dve_done.at(b - 1))
                        sp.nop(nofuse=True)
                        sp.dma_start(ib[:, h, :], pick(ncol(last_dst), b)).then_inc(idx_rdy[h].sem, 16)
                        for t, o in ((LW, lo), (X2, x2)):
                            sp.dma_start(o[:, h, :, :].rearrange("p g d -> p (g d)"), pick(nrows(t), b)).then_inc(in_rdy[h].sem, 16)

                    def store(b, h, i):
                        sp.wait_ge(act_done.sem, act_done.at(b + 1))
                        sp.nop(nofuse=True)
                        for t, o in ((X3, x3), (Q[0], h3)):
                            sp.dma_start(pick(nrows(t), b), o[:, h, :, :].rearrange("p g d -> p (g d)")).then_inc(st_done[h].sem, 16)
                    sp_stream(sp, load, store)
                    stored(sp, 2)

                @block.gpsimd
                def _(pool):
                    nc.gpsimd.memset(own[:, :], 1.0).then_inc(step.sem, 1)
                    pool.wait_ge(step.sem, step.at(1))
                    nc.gpsimd.affine_select(out=own[:, :], in_=own[:, :], compare_op=ALU.is_ge, fill=0.0,
                                            base=N - 1 - (NB - 1) * K * P, pattern=[[-1, K]], channel_multiplier=-K)\
                        .then_inc(step.sem, 1)
                    blocks(pool, gather_rows(pool, ib, idx_rdy, T2, tr, nrow_rdy))

                @block.vector
                def _(dve):
                    dve.wait_ge(step.sem, step.at(2))

                    def body(b, h, i):
                        dve.wait_ge(in_rdy[h].sem, in_rdy[h].at(32 * i + 32))
                        dve.wait_ge(nrow_rdy[h].sem, nrow_rdy[h].at(16 * K * i + 16 * K))
                        nc.vector.tensor_tensor(lo[:, h], lo[:, h], tr[:, h], ALU.add)
                        nc.vector.drain()
                        dve.wait_ge(st_done[h].sem, st_done[h].at(32 * i))
                        nc.vector.tensor_scalar(lo[:, h], lo[:, h], 0.0, None, ALU.max)
                        nc.vector.drain()
                        nc.vector.tensor_tensor(x3[:, h], lo[:, h], x2[:, h], ALU.add)
                        nc.vector.drain()
                        stats(x3[:, h], st, mv[:, h]).then_inc(d2a.sem, 1)
                        dve.wait_ge(a2d.sem, a2d.at(b + 1))
                        q = scale_shift(mv[:, h, :, 0], sd[:, h, :], rs[:, h, :], nm[:, h, :])
                        if isinstance(b, int) and b == NB - 1:
                            nc.vector.drain()
                            nc.vector.tensor_tensor(rs[:, h, :], rs[:, h, :], own[:, :], ALU.mult)
                            q = nc.vector.tensor_tensor(nm[:, h, :], nm[:, h, :], own[:, :], ALU.mult)
                        q.then_inc(dve_done.sem, 1)
                    with dve.Fori(0, NB // 2 - 1) as i:
                        for h in range(2):
                            body(2 * i + h, h, i)
                    for h in range(2):
                        body(NB - 2 + h, h, NB // 2 - 1)
                    dve.wait_ge(mm_rdy.sem, mm_rdy.at(2))
                    nc.vector.tensor_copy(sumq[:, 0, :], acc[:, 0:D])

                @block.scalar
                def _(act):
                    def body(b, h, i):
                        act.wait_ge(d2a.sem, d2a.at(b + 1))
                        nc.scalar.activation(sd[:, h, :], mv[:, h, :, 1], ACT.Sqrt, bias=eps5[:, :]).then_inc(a2d.sem, 1)
                        act.wait_ge(dve_done.sem, dve_done.at(b + 1))
                        act.wait_ge(st_done[h].sem, st_done[h].at(32 * i))
                        for g in range(K):
                            nc.scalar.activation(h3[:, h, g, :], x3[:, h, g, :], ACT.Relu,
                                                 bias=nm[:, h, g:g + 1], scale=rs[:, h, g:g + 1])
                        act.drain()
                        act.sem_inc(act_done.sem, 1)
                        act.wait_ge(mm_free.sem, mm_free.at(b - 1))
                        nc.scalar.activation(sq[:, h], h3[:, h], ACT.Square).then_inc(for_pe.sem, 1)
                    blocks(act, body)

                @block.tensor
                def _(pe):
                    nc.tensor.matmul(acc[:, 0:D], ones[:, :], zero[:, 0:D], start=True, stop=False).then_inc(mm_rdy.sem, 1)

                    def body(b, h, i):
                        pe.wait_ge(for_pe.sem, for_pe.at(b + 1))
                        for g in range(K):
                            q = nc.tensor.matmul(acc[:, 0:D], ones[:, :], sq[:, h, g, :], start=False, stop=False)
                        q.then_inc(mm_free.sem, 1)
                    blocks(pe, body)
                    nc.tensor.matmul(acc[:, 0:D], ones[:, :], zero[:, 0:D], start=False, stop=True).then_inc(mm_rdy.sem, 1)
            step.base += 2
            mm_rdy.base += 2
            mm_free.base += NB
            for_pe.base += NB
            dve_done.base += NB
            act_done.base += NB
            stage_base(nd=1, na=1, loads=2, stores=2, gathers=(nrow_rdy,), idx=1)

        scale = sb("scale", [P, 4, D])
        beta = sb("beta", [P, 4, D])
        coef = sb("coef", [P, 3, D])

        def scale_of(k):
            with nc.Block() as block:
                @block.vector
                def _(dve):
                    if k == 0:
                        nc.vector.tensor_scalar(sumq[:, 0, :], sumq[:, 0, :], 1e-12, None, ALU.max)
                        nc.vector.drain()
                    nc.vector.memset(mid[:, :], 0.0).then_inc(d2a.sem, 1)
                    dve.wait_ge(a2d.sem, a2d.at(1))
                    nc.vector.reciprocal(scale[:, k, :], beta[:, k, :])

                @block.scalar
                def _(act):
                    act.wait_ge(d2a.sem, d2a.at(1))
                    nc.scalar.activation(beta[:, k, :], sumq[:, k, :], ACT.Sqrt).then_inc(a2d.sem, 1)
            d2a.base += 1
            a2d.base += 1
        mid = sb("mid", [P, D])
        scale_of(0)

        def sum_rows(pe, acc, rows):
            nc.tensor.matmul(acc[:, 0:D], ones[:, :], zero[:, 0:D], start=True, stop=False)

            def body(b, h, i):
                pe.wait_ge(for_pe.sem, for_pe.at(b + 1))
                for g in range(K):
                    q = nc.tensor.matmul(acc[:, 0:D], ones[:, :], rows[:, h, g, :], start=False, stop=False)
                q.then_inc(mm_free.sem, 1)
            blocks(pe, body)
            nc.tensor.matmul(acc[:, 0:D], ones[:, :], zero[:, 0:D], start=False, stop=True).then_inc(mm_rdy.sem, 1)

        def flat(t):
            return t.rearrange("p g d -> p (g d)")

        for k in range(1, 4):
            T = T3[k - 1]
            with ExitStack() as c:
                ib = sb(f"l{k}_ib", [P, 2, K], i32, c)
                xr = sb(f"l{k}_xr", [P, 2, K, D], fp32, c)
                S = sb(f"l{k}_S", [P, 2, K, D], fp32, c)
                with nc.Block() as block:
                    @block.sync
                    def _(sp):
                        def load(b, h, i):
                            sp.wait_ge(dve_done.sem, dve_done.at(b - 1))
                            sp.nop(nofuse=True)
                            sp.dma_start(ib[:, h, :], pick(ecol(dst_s), b)).then_inc(idx_rdy[h].sem, 16)

                        def store(b, h, i):
                            sp.wait_ge(dve_done.sem, dve_done.at(b + 1))
                            sp.nop(nofuse=True)
                            sp.dma_start(pick(erows(T), b), flat(S[:, h])).then_inc(st_done[h].sem, 16)
                        sp_stream(sp, load, store)
                        stored(sp, 1)

                    @block.gpsimd
                    def _(pool):
                        blocks(pool, gather_rows(pool, ib, idx_rdy, Q[k - 1], xr, row_rdy))

                    @block.scalar
                    def _(act):
                        def body(b, h, i):
                            act.wait_ge(row_rdy[h].sem, row_rdy[h].at(16 * K * i + 16 * K))
                            for g in range(K):
                                q = nc.scalar.activation(xr[:, h, g, :], xr[:, h, g, :], ACT.Copy,
                                                         scale=ew_s[:, bass.ds(b * K + g, 1)])
                            q.then_inc(a2d.sem, 1)
                        blocks(act, body)

                    @block.vector
                    def _(dve):
                        nc.vector.memset(S[:, :, :, :], 0.0)
                        nc.vector.drain()

                        def body(b, h, i):
                            dve.wait_ge(st_done[h].sem, st_done[h].at(16 * i))
                            dve.wait_ge(a2d.sem, a2d.at(b + 1))
                            for g in range(K):
                                pv = S[:, h, g - 1, :] if g else S[:, 1 - h, K - 1, :]
                                q = nc.vector.scalar_tensor_tensor(S[:, h, g, :], pv, cont["src"][:, bass.ds(b * K + g, 1)],
                                                                   xr[:, h, g, :], ALU.mult, ALU.add)
                                if g == K - 1:
                                    q.then_inc(dve_done.sem, 1)
                                nc.vector.drain()
                        blocks(dve, body)
                dve_done.base += NB
                stage_base(na=1, stores=1, gathers=(row_rdy,), idx=1)
                add_carry("src", T, S[:, 1, K - 1, :], D)

            with ExitStack() as c:
                ib = sb(f"a{k}_ib", [P, 2, K], i32, c)
                tr = sb(f"a{k}_tr", [P, 2, K, D], fp32, c)
                uo = sb(f"a{k}_uo", [P, 2, K, D], fp32, c)
                q1 = sb(f"a{k}_q1", [P, 2, K, D], fp32, c)
                pq = sb(f"a{k}_pq", [P, 2, K, D], fp32, c)
                acc = ps(f"a{k}_acc", [P, 512], fp32, c)
                with nc.Block() as block:
                    @block.sync
                    def _(sp):
                        def load(b, h, i):
                            sp.wait_ge(dve_done.sem, dve_done.at(b - 1))
                            sp.nop(nofuse=True)
                            sp.wait_ge(act_done.sem, act_done.at(b - 1))
                            sp.nop(nofuse=True)
                            sp.dma_start(ib[:, h, :], pick(ncol(last_src), b)).then_inc(idx_rdy[h].sem, 16)
                            sp.dma_start(flat(q1[:, h]), pick(nrows(Q[k - 1]), b)).then_inc(in_rdy[h].sem, 16)

                        def store(b, h, i):
                            sp.wait_ge(act_done.sem, act_done.at(b + 1))
                            sp.nop(nofuse=True)
                            sp.dma_start(pick(nrows(UU[k - 1]), b), flat(uo[:, h])).then_inc(st_done[h].sem, 16)
                        sp_stream(sp, load, store)
                        stored(sp, 1)

                    @block.gpsimd
                    def _(pool):
                        blocks(pool, gather_rows(pool, ib, idx_rdy, T, tr, nrow_rdy))

                    @block.scalar
                    def _(act):
                        def body(b, h, i):
                            act.wait_ge(nrow_rdy[h].sem, nrow_rdy[h].at(16 * K * i + 16 * K))
                            act.wait_ge(st_done[h].sem, st_done[h].at(16 * i))
                            nc.scalar.activation(flat(uo[:, h]), flat(tr[:, h]), ACT.Copy).then_inc(act_done.sem, 1)
                        blocks(act, body)

                    @block.vector
                    def _(dve):
                        def body(b, h, i):
                            dve.wait_ge(nrow_rdy[h].sem, nrow_rdy[h].at(16 * K * i + 16 * K))
                            dve.wait_ge(in_rdy[h].sem, in_rdy[h].at(16 * i + 16))
                            dve.wait_ge(mm_free.sem, mm_free.at(b - 1))
                            nc.vector.tensor_tensor(pq[:, h], tr[:, h], q1[:, h], ALU.mult).then_inc(for_pe.sem, 1)
                            nc.vector.drain().then_inc(dve_done.sem, 1)
                        blocks(dve, body)
                        dve.wait_ge(mm_rdy.sem, mm_rdy.at(1))
                        nc.vector.tensor_tensor(mid[:, :], acc[:, 0:D], scale[:, k - 1, :], ALU.mult)
                        nc.vector.drain()
                        nc.vector.tensor_tensor(mid[:, :], mid[:, :], scale[:, k - 1, :], ALU.mult)
                        nc.vector.drain()
                        nc.vector.tensor_tensor(coef[:, 1, :], mid[:, :], scale[:, k - 1, :], ALU.mult)
                        nc.vector.tensor_copy(coef[:, 0, :], scale[:, k - 1, :])
                        if k > 1:
                            nc.vector.tensor_tensor(coef[:, 2, :], beta[:, k - 1, :], scale[:, k - 2, :], ALU.mult)

                    @block.tensor
                    def _(pe):
                        sum_rows(pe, acc, pq)
                dve_done.base += NB
                act_done.base += NB
                for_pe.base += NB
                mm_free.base += NB
                mm_rdy.base += 1
                stage_base(loads=1, stores=1, gathers=(nrow_rdy,), idx=1)

            with ExitStack() as c:
                u = sb(f"b{k}_u", [P, 2, K, D], fp32, c)
                q1 = sb(f"b{k}_q1", [P, 2, K, D], fp32, c)
                q2 = sb(f"b{k}_q2", [P, 2, K, D], fp32, c)
                qo = sb(f"b{k}_qo", [P, 2, K, D], fp32, c)
                sq = sb(f"b{k}_sq", [P, 2, K, D], fp32, c)
                acc = ps(f"b{k}_acc", [P, 512], fp32, c)
                ins = [(u, UU[k - 1]), (q1, Q[k - 1])] + ([(q2, Q[k - 2])] if k > 1 else [])
                with nc.Block() as block:
                    @block.sync
                    def _(sp):
                        def load(b, h, i):
                            sp.wait_ge(dve_done.sem, dve_done.at(b - 1))
                            sp.nop(nofuse=True)
                            for o, t in ins:
                                sp.dma_start(flat(o[:, h]), pick(nrows(t), b)).then_inc(in_rdy[h].sem, 16)

                        def store(b, h, i):
                            sp.wait_ge(dve_done.sem, dve_done.at(b + 1))
                            sp.nop(nofuse=True)
                            sp.dma_start(pick(nrows(Q[k]), b), flat(qo[:, h])).then_inc(st_done[h].sem, 16)
                        sp_stream(sp, load, store)
                        stored(sp, 1)

                    @block.vector
                    def _(dve):
                        def body(b, h, i):
                            dve.wait_ge(in_rdy[h].sem, in_rdy[h].at(16 * len(ins) * (i + 1)))
                            for m, (o, _t) in enumerate(ins):
                                nc.vector.tensor_tensor(o[:, h], o[:, h], coef[:, m:m + 1, :].broadcast_to([P, K, D]), ALU.mult)
                            nc.vector.drain()
                            dve.wait_ge(st_done[h].sem, st_done[h].at(16 * i))
                            dve.wait_ge(act_done.sem, act_done.at(b - 1))
                            q = nc.vector.tensor_tensor(qo[:, h], u[:, h], q1[:, h], ALU.subtract)
                            if k > 1:
                                nc.vector.drain()
                                q = nc.vector.tensor_tensor(qo[:, h], qo[:, h], q2[:, h], ALU.subtract)
                            q.then_inc(dve_done.sem, 1)
                        blocks(dve, body)
                        dve.wait_ge(mm_rdy.sem, mm_rdy.at(1))
                        nc.vector.tensor_copy(sumq[:, k, :], acc[:, 0:D])

                    @block.scalar
                    def _(act):
                        def body(b, h, i):
                            act.wait_ge(dve_done.sem, dve_done.at(b + 1))
                            act.wait_ge(mm_free.sem, mm_free.at(b - 1))
                            nc.scalar.activation(flat(sq[:, h]), flat(qo[:, h]), ACT.Square).then_inc(for_pe.sem, 1)
                            act.drain()
                            act.sem_inc(act_done.sem, 1)
                        blocks(act, body)

                    @block.tensor
                    def _(pe):
                        sum_rows(pe, acc, sq)
                dve_done.base += NB
                act_done.base += NB
                for_pe.base += NB
                mm_free.base += NB
                mm_rdy.base += 1
                stage_base(loads=len(ins), stores=1)
            scale_of(k)

        with ExitStack() as c:
            dg = sb("o_dg", [P, 4, D], fp32, c)
            sc = sb("o_sc", [P, 4], fp32, c)
            qi = sb("o_qi", [P, 2, 4, K, D], fp32, c)
            x3 = sb("o_x3", [P, 2, K, D], fp32, c)
            hT = sb("o_hT", [P, 4, K * D], fp32, c)
            y = sb("o_y", [P, 2, K, D], fp32, c)
            tp = ps("o_tp", [P, 2, 2, 512], fp32, c)
            mm = ps("o_mm", [P, 4, 512], fp32, c)
            on = nrows(out)
            with nc.Block() as block:
                @block.sync
                def _(sp):
                    def load(b, h, i):
                        sp.wait_ge(dve_done.sem, dve_done.at(b - 1))
                        sp.nop(nofuse=True)
                        for k in range(4):
                            sp.dma_start(flat(qi[:, h, k]), pick(nrows(Q[k]), b)).then_inc(in_rdy[h].sem, 16)
                        sp.dma_start(flat(x3[:, h]), pick(nrows(X3), b)).then_inc(in_rdy[h].sem, 16)

                    def store(b, h, i):
                        sp.wait_ge(dve_done.sem, dve_done.at(b + 1))
                        sp.nop(nofuse=True)
                        sp.dma_start(pick(on, b), flat(y[:, h])).then_inc(st_done[h].sem, 16)
                    sp_stream(sp, load, store)
                    stored(sp, 1)

                @block.vector
                def _(dve):
                    nc.vector.tensor_tensor(dg[:, :, :], scale[:, :, :], ident[:, :].unsqueeze(1).broadcast_to([P, 4, D]), ALU.mult)
                    nc.vector.drain()
                    nc.vector.tensor_reduce(sc[:, :], dg[:, :, :], AX.X, ALU.add)
                    nc.vector.drain()
                    for k in range(4):
                        q = nc.vector.tensor_scalar(wf[:, k, :], wf[:, k, :], sc[:, k:k + 1], None, ALU.mult)
                    q.then_inc(step.sem, 1)

                    def body(b, h, i):
                        for n, k in enumerate((1, 3)):
                            dve.wait_ge(tp_rdy.sem, tp_rdy.at(4 * b + k + 1))
                            nc.vector.tensor_copy(hT[:, k, 0:512], tp[:, 1, 0, :])
                            nc.vector.tensor_copy(hT[:, k, 512:K * D], tp[:, 1, 1, 0:K * D - 512]).then_inc(hT2_rdy.sem, 1)
                        dve.wait_ge(a2d.sem, a2d.at(b + 1))
                        dve.wait_ge(in_rdy[h].sem, in_rdy[h].at(80 * i + 80))
                        nc.vector.tensor_tensor(y[:, h], y[:, h], x3[:, h], ALU.add).then_inc(dve_done.sem, 1)
                    blocks(dve, body)

                @block.scalar
                def _(act):
                    def body(b, h, i):
                        for n, k in enumerate((0, 2)):
                            act.wait_ge(tp_rdy.sem, tp_rdy.at(4 * b + k + 1))
                            nc.scalar.activation(hT[:, k, 0:512], tp[:, 0, 0, :], ACT.Copy)
                            nc.scalar.activation(hT[:, k, 512:K * D], tp[:, 0, 1, 0:K * D - 512], ACT.Copy).then_inc(hT_rdy.sem, 1)
                        act.wait_ge(st_done[h].sem, st_done[h].at(16 * i))
                        for g in range(K):
                            act.wait_ge(mm_rdy.sem, mm_rdy.at(b * K + g + 1))
                            nc.scalar.activation(y[:, h, g, :], mm[:, g % 4, 0:D], ACT.Relu).then_inc(mm_free.sem, 1)
                        act.drain()
                        act.sem_inc(a2d.sem, 1)
                    blocks(act, body)

                @block.tensor
                def _(pe):
                    pe.wait_ge(step.sem, step.at(1))

                    def body(b, h, i):
                        pe.wait_ge(in_rdy[h].sem, in_rdy[h].at(80 * i + 80))
                        for k in range(4):
                            cr = hT2_rdy if k % 2 else hT_rdy
                            pe.wait_ge(cr.sem, cr.at(2 * b + k // 2))
                            for g in range(K):
                                q = nc.tensor.transpose(tp[:, k % 2, g // 4, (g % 4) * D:(g % 4 + 1) * D], qi[:, h, k, g, :],
                                                        ident[:, :])
                            q.then_inc(tp_rdy.sem, 1)
                        pe.wait_ge(hT_rdy.sem, hT_rdy.at(2 * b + 2))
                        pe.wait_ge(hT2_rdy.sem, hT2_rdy.at(2 * b + 2))
                        for g in range(K):
                            pe.wait_ge(mm_free.sem, mm_free.at(b * K + g - 3))
                            for k in range(4):
                                q = nc.tensor.matmul(mm[:, g % 4, 0:D], hT[:, k, g * D:(g + 1) * D], wf[:, k, :],
                                                     start=(k == 0), stop=(k == 3))
                            q.then_inc(mm_rdy.sem, 1)
                    blocks(pe, body)


_INS = ["x", "src", "dst", "edge_type_32", "edge_weight", "L0_gnn_W", "L0_gnn_att_src", "L0_gnn_att_dst",
        "L0_gnn_gat_bias", "L0_gnn_skip_W", "L0_gnn_skip_b", "L0_gnn_ln_g", "L0_gnn_ln_b", "L1_gnn_W1", "L1_gnn_b1",
        "L1_gnn_W2", "L1_gnn_b2", "L1_gnn_Wl", "L1_gnn_bl", "L2_gnn_weight", "L2_gnn_w_comp", "L2_gnn_h_bias",
        "L2_gnn_loop_weight", "L3_gnn_weights"]
_FILL = {"x": 0, "src": N, "dst": N, "edge_type_32": 0, "edge_weight": 0}


def kernel(**inputs):
    import numpy as _np
    import concourse.bacc as _bacc
    from concourse import mybir as _mybir
    from concourse.bass_utils import run_bass_kernel_spmd as _run

    nc = _bacc.Bacc("TRN2", target_bir_lowering=False, num_devices=1)
    arrays, args = {}, []
    for name in _INS:
        a = _np.ascontiguousarray(inputs[name])
        if name in _FILL:
            a = _np.concatenate([a, _np.full((NP - N,) + a.shape[1:], _FILL[name], a.dtype)])
        arrays[f"in_{name}_dram"] = a
        args.append(nc.dram_tensor(f"in_{name}_dram", a.shape, _mybir.dt.from_np(a.dtype), kind="ExternalInput").ap())
    args.append(nc.dram_tensor("out_0_dram", (NP, D), _mybir.dt.float32, kind="ExternalOutput").ap())
    gnn(nc, *args)
    r = _run(nc, [arrays], core_ids=[0])
    return r.results[0]["out_0_dram"][0:N]
```

```python
import concourse.bass as bass
from concourse import mybir
from contextlib import ExitStack

P = 128
D = 128
N = 50000
K = 7
NB = 56
EC = K * NB
NP = P * EC
ZROW = NP
HI, LO = 196, 256
HH = HI // 2
H = 4
C = D // H
R, B = 32, 8
NEG = 1.0e30
assert HI * LO == NP

fp32 = mybir.dt.float32
bf16 = mybir.dt.bfloat16
i32 = mybir.dt.int32
ALU = mybir.AluOpType
ACT = mybir.ActivationFunctionType
AX = mybir.AxisListType


class Counter:

    def __init__(self, nc, ctx, name, credit=0):
        self.sem = ctx.enter_context(nc.semaphore(name))
        self.base = credit
        self.credit = credit

    def at(self, n):
        return n + self.base


def gnn(nc, x, src, dst, etype, ew, W, att_s, att_d, gat_b, skip_W, skip_b, ln_g, ln_b,
        W1, b1, W2, b2, Wl, bl, wbase, wcomp, h_bias, loop_W, lw, out):
    ctx = ExitStack()
    with ctx:
        def sb(name, shape, dt=fp32, c=ctx):
            return c.enter_context(nc.sbuf_tensor(name, shape, dt))

        def ps(name, shape, dt=fp32, c=ctx):
            return c.enter_context(nc.psum_tensor(name, shape, dt))

        def dram(name, shape, dt=fp32):
            return nc.dram_tensor(name, shape, dt, kind="Internal").ap()

        def cnt(name, credit=0):
            return Counter(nc, ctx, name, credit)

        setup = cnt("setup")
        pdma = cnt("pdma")
        step = cnt("step")
        idx_rdy = [cnt(f"idx_rdy{h}") for h in range(2)]
        idy_rdy = [cnt(f"idy_rdy{h}") for h in range(2)]
        row_rdy = [cnt(f"row_rdy{h}") for h in range(2)]
        roy_rdy = [cnt(f"roy_rdy{h}") for h in range(2)]
        nrow_rdy = [cnt(f"nrow_rdy{h}") for h in range(2)]
        in_rdy = [cnt(f"in_rdy{h}") for h in range(2)]
        in2_rdy = [cnt(f"in2_rdy{h}") for h in range(2)]
        st_done = [cnt(f"st_done{h}") for h in range(2)]
        st2_done = [cnt(f"st2_done{h}") for h in range(2)]
        dve_done = cnt("dve_done", 2)
        act_done = cnt("act_done", 2)
        taken = cnt("taken")
        taken2 = cnt("taken2")
        rows_free = cnt("rows_free", 2)
        d2a = cnt("d2a")
        a2d = cnt("a2d")
        d2v = cnt("d2v")
        v2d = cnt("v2d")
        for_pe = cnt("for_pe")
        for_pe2 = cnt("for_pe2")
        tp_rdy = cnt("tp_rdy")
        hT_rdy = cnt("hT_rdy")
        hT2_rdy = cnt("hT2_rdy", 1)
        mm_rdy = cnt("mm_rdy")
        mm_free = cnt("mm_free", 8)
        dense_c = [[cnt(f"dn{n}_{w}", int(w == "used")) for w in ("there", "copied", "product", "biased", "back", "used")]
                   for n in range(2)]
        hist_o = cnt("hist_o")
        hist_f = cnt("hist_f", K)
        hist_r = cnt("hist_r")
        sc_done = [cnt(f"sc_done{u}") for u in range(K)]
        every = [dense_c[0][5], dense_c[1][5], dve_done, act_done, rows_free, mm_free, hist_f, hT2_rdy]

        G0 = dram("G0", [NP, D + H])
        AD = dram("AD", [NP, H])
        SK = dram("SK", [NP, D])
        T0 = dram("T0", [NP + P, D + 2 * H])
        X1 = dram("X1", [NP, D])
        P1 = dram("P1", [NP, 2 * D])
        U1 = dram("U1", [NP, D])
        T1 = dram("T1", [NP + P, D + 2])
        X2 = dram("X2", [NP, D])
        H2 = dram("H2", [NP, D])
        LW = dram("LW", [NP, D])
        T2 = dram("T2", [NP + P, D])
        X3 = dram("X3", [NP, D])
        Q = [dram(f"Q{k}", [NP, D]) for k in range(4)]
        T3 = [dram(f"T3{k}", [NP + P, D]) for k in range(3)]
        UU = [dram(f"UU{k}", [NP, D]) for k in range(3)]
        last_src = dram("last_src", [NP], i32)
        last_dst = dram("last_dst", [NP], i32)
        srt = [[dram(f"srt{q}_{u}", [NP, 4]) for u in range(K)] for q in range(2)]
        dst_s = dram("dst_s", [NP], i32)
        src_s = dram("src_s", [NP], i32)

        ident = sb("ident", [P, P])
        identb = sb("identb", [P, P], bf16)
        ones = sb("ones", [P, P])
        lower = sb("lower", [P, P])
        zero = sb("zero", [P, 136])
        iob = sb("iob", [P, LO], bf16)
        iof = sb("iof", [P, LO])
        pcol = sb("pcol", [P, 1])
        eps5 = sb("eps5", [P, 1])
        low = sb("low", [P, H])
        half = sb("half", [P, K])
        zb = sb("zb", [P, LO], bf16)
        cont = {k: sb(f"cont_{k}", [P, EC]) for k in ("src", "dst")}
        carry = {k: sb(f"carry_{k}", [P, P]) for k in ("src", "dst")}
        fix = {k: sb(f"fix_{k}", [P, 1], i32) for k in ("src", "dst")}
        ew_s = sb("ew_s", [P, EC])
        wc_e = sb("wc_e", [P, EC, B])

        def nrows(t):
            return t[0:NP, :].rearrange("(b p g) d -> b p (g d)", p=P, g=K)

        def erows(t):
            return t[0:NP, :].rearrange("(p b g) d -> b p (g d)", p=P, g=K)

        def nparts(t, lo, hi):
            return t[0:NP, lo:hi].rearrange("(b p g) d -> b p g d", p=P, g=K)

        def ncol(t):
            return t.rearrange("(b p g) -> b p g", p=P, g=K)

        def ecol(t):
            return t.rearrange("(p b g) -> b p g", p=P, g=K)

        def pick(v, b):
            if isinstance(b, int):
                return v[b]
            if len(v.shape) == 4:
                return v[bass.ds(b, 1)].rearrange("o p g d -> (o p) g d")
            return v[bass.ds(b, 1)].rearrange("o p f -> (o p) f")

        def blocks(eng, body, lo=0, hi=NB // 2):
            with eng.Fori(lo, hi) as i:
                for h in range(2):
                    body(2 * i + h, h, i)

        def gather(pool, o, table, slot):
            return pool.indirect_dma_start(out=o, out_offset=None, in_=table[:, :],
                                           in_offset=bass.IndirectOffsetOnAxis(ap=slot, axis=0))

        with nc.Block() as block:
            @block.gpsimd
            def _(pool):
                for c in every:
                    if c.credit:
                        pool.sem_inc(c.sem, c.credit)
                nc.gpsimd.memset(ident[:, :], 0.0)
                nc.gpsimd.memset(ones[:, :], 1.0)
                nc.gpsimd.memset(zero[:, :], 0.0)
                nc.gpsimd.memset(eps5[:, :], 1e-5)
                nc.gpsimd.memset(low[:, :], -NEG)
                nc.gpsimd.memset(half[:, :], -0.5)
                nc.gpsimd.memset(zb[:, :], 0.0)
                nc.gpsimd.memset(lower[:, :], 1.0)
                nc.gpsimd.iota(iof[:, :], pattern=[[1, LO]], base=0, channel_multiplier=0,
                               allow_small_or_imprecise_dtypes=True)
                nc.gpsimd.iota(pcol[:, :], pattern=[[0, 1]], base=0, channel_multiplier=EC,
                               allow_small_or_imprecise_dtypes=True).then_inc(step.sem, 1)
                pool.wait_ge(step.sem, step.at(1))
                nc.gpsimd.affine_select(out=ident[:, :], in_=ident[:, :], compare_op=ALU.not_equal, fill=1.0,
                                        base=0, pattern=[[-1, P]], channel_multiplier=1)
                nc.gpsimd.affine_select(out=lower[:, :], in_=lower[:, :], compare_op=ALU.is_ge, fill=0.0,
                                        base=-1, pattern=[[1, P]], channel_multiplier=-1).then_inc(step.sem, 1)
                pool.wait_ge(step.sem, step.at(2))
                nc.gpsimd.tensor_copy(identb[:, :], ident[:, :])
                nc.gpsimd.tensor_copy(iob[:, :], iof[:, :])
            @block.sync
            def _(sp):
                sp.wait_ge(step.sem, step.at(2))
                tz = [(T1, D + 2), (T2, D), *((t, D) for t in T3)]
                for n, (t, w) in enumerate(tz):
                    sp.dma_start(t[NP:NP + P, :], zero[:, 0:w]).then_inc(st_done[n % 2].sem, 16)
                sp.dma_start(T0[NP:NP + P, 0:D + H], zero[:, 0:D + H]).then_inc(st_done[1].sem, 16)
                sp.dma_start(T0[NP:NP + P, D + H:D + 2 * H], low[:, :]).then_inc(setup.sem, 16)
                for h in range(2):
                    sp.wait_ge(st_done[h].sem, 48)
                sp.wait_ge(setup.sem, 16)
        step.base += 2
        setup.base += 16
        for h in range(2):
            st_done[h].base += 48

        def histogram(key_dram, last, name):
            with ExitStack() as c:
                ki = sb(f"ki_{name}", [P, EC], i32, c)
                kd = sb(f"kd_{name}", [P, 2, EC], i32, c)
                kf = sb(f"kf_{name}", [P, 2, EC], fp32, c)
                oh = sb(f"oh_{name}", [P, K, LO + HI], bf16, c)
                hs = sb(f"hs_{name}", [HH, 2, LO], fp32, c)
                cu = sb(f"cu_{name}", [HH, 2, LO], fp32, c)
                tot = sb(f"tot_{name}", [HH, 2], fp32, c)
                lp = sb(f"lp_{name}", [HH, 2, LO], fp32, c)
                lpi = sb(f"lpi_{name}", [HH, 2, LO], i32, c)
                acc = [ps(f"acc{m}_{name}", [P, 512], fp32, c) for m in range(2)]
                bs = ps(f"bs_{name}", [P, 512], fp32, c)
                with nc.Block() as block:
                    @block.sync
                    def _(sp):
                        sp.dma_start(ki[:, :], key_dram.rearrange("(p j) -> p j", p=P)).then_inc(setup.sem, 16)
                        sp.wait_ge(step.sem, step.at(1))
                        sp.dma_start(last.rearrange("(m h l) -> h m l", m=2, l=LO), lpi[:, :, :]).then_inc(setup.sem, 16)
                        sp.wait_ge(setup.sem, setup.at(32))

                    @block.vector
                    def _(dve):
                        dve.wait_ge(setup.sem, setup.at(16))
                        nc.vector.tensor_scalar(kd[:, 0, :], ki[:, :], LO - 1, None, ALU.bitwise_and)
                        nc.vector.tensor_scalar(kd[:, 1, :], ki[:, :], 8, None, ALU.logical_shift_right)
                        nc.vector.drain()
                        nc.vector.tensor_copy(kf[:, :, :], kd[:, :, :])
                        nc.vector.drain()
                        with dve.Fori(0, NB) as i:
                            for u in range(K):
                                dve.wait_ge(hist_f.sem, hist_f.at(i * K + (u + 1 - K)))
                                nc.vector.tensor_scalar(oh[:, u, 0:LO], iob[:, :], kf[:, 0, bass.ds(i * K + u, 1)],
                                                        None, ALU.is_equal)
                                nc.vector.tensor_scalar(oh[:, u, LO:LO + HI], iob[:, 0:HI], kf[:, 1, bass.ds(i * K + u, 1)],
                                                        None, ALU.is_equal).then_inc(hist_o.sem, 1)
                        dve.wait_ge(mm_rdy.sem, mm_rdy.at(1))
                        for m in range(2):
                            nc.vector.tensor_copy(hs[:, m, :], acc[m][0:HH, 0:LO])
                        nc.vector.drain()
                        for m in range(2):
                            nc.vector.tensor_tensor_scan(cu[:, m, :], hs[:, m, :], hs[:, m, :], 0.0, ALU.add, ALU.bypass)
                        nc.vector.drain()
                        nc.vector.tensor_copy(tot[:, :], cu[:, :, LO - 1:LO].rearrange("p m o -> p (m o)")).then_inc(hist_r.sem, 1)
                        dve.wait_ge(mm_rdy.sem, mm_rdy.at(2))
                        for m in range(2):
                            nc.vector.tensor_scalar(lp[:, m, :], cu[:, m, :], bs[0:HH, m:m + 1], -1.0 - ZROW, ALU.add, ALU.add)
                            nc.vector.tensor_scalar(hs[:, m, :], hs[:, m, :], 1.0, None, ALU.min)
                        nc.vector.drain()
                        nc.vector.tensor_tensor(lp[:, :, :], lp[:, :, :], hs[:, :, :], ALU.mult)
                        nc.vector.drain()
                        nc.vector.tensor_scalar(lpi[:, :, :], lp[:, :, :], float(ZROW), None, ALU.add).then_inc(step.sem, 1)

                    @block.tensor
                    def _(pe):
                        for m in range(2):
                            nc.tensor.matmul(acc[m][0:HH, 0:LO], zb[:, 0:HH], zb[:, :], start=True, stop=False)
                        with pe.Fori(0, NB) as i:
                            for u in range(K):
                                pe.wait_ge(hist_o.sem, hist_o.at(i * K + u + 1))
                                for m in range(2):
                                    q = nc.tensor.matmul(acc[m][0:HH, 0:LO], oh[:, u, LO + m * HH:LO + (m + 1) * HH],
                                                         oh[:, u, 0:LO], start=False, stop=False)
                                q.then_inc(hist_f.sem, 1)
                        for m in range(2):
                            q = nc.tensor.matmul(acc[m][0:HH, 0:LO], zb[:, 0:HH], zb[:, :], start=False, stop=True)
                        q.then_inc(mm_rdy.sem, 1)
                        pe.wait_ge(hist_r.sem, hist_r.at(1))
                        nc.tensor.matmul(bs[0:HH, 0:1], lower[0:HH, 0:HH], tot[:, 0:1], start=True, stop=True)
                        nc.tensor.matmul(bs[0:HH, 1:2], lower[0:HH, 0:HH], tot[:, 1:2], start=True, stop=False)
                        nc.tensor.matmul(bs[0:HH, 1:2], ones[0:HH, 0:HH], tot[:, 0:1], start=False, stop=True)\
                            .then_inc(mm_rdy.sem, 1)
                setup.base += 32
                step.base += 1
                hist_r.base += 1
                mm_rdy.base += 2
                hist_o.base += EC
                hist_f.base += EC

        histogram(src, last_src, "src")
        histogram(dst, last_dst, "dst")

        def sort_pass(q, pay, key_col, high):
            with ExitStack() as c:
                di = sb(f"di{q}", [P, EC], i32, c)
                dg = sb(f"dg{q}", [P, EC], fp32, c)
                oh = sb(f"so{q}", [P, K, LO], bf16, c)
                R0 = sb(f"R0{q}", [P, LO], fp32, c)
                tt = sb(f"tt{q}", [P, LO], fp32, c)
                junk = sb(f"junk{q}", [P, 2, LO], fp32, c)
                rk = sb(f"rk{q}", [P, 2, K], fp32, c)
                rki = sb(f"rki{q}", [P, 2, K], i32, c)
                pr = sb(f"pr{q}", [P, 2, K, 4], fp32, c)
                zz = sb(f"zz{q}", [P, EC * 4], fp32, c)
                acc = ps(f"sacc{q}", [P, 512], fp32, c)
                RP = ps(f"RP{q}", [P, 512], fp32, c)
                with nc.Block() as block:
                    @block.vector
                    def _(dve):
                        nc.vector.memset(zz[:, :], 0.0).then_inc(step.sem, 1)
                        nc.vector.tensor_copy(di[:, :], pay[:, :, key_col])
                        nc.vector.drain()
                        if high:
                            nc.vector.tensor_scalar(di[:, :], di[:, :], 8, None, ALU.logical_shift_right)
                        else:
                            nc.vector.tensor_scalar(di[:, :], di[:, :], LO - 1, None, ALU.bitwise_and)
                        nc.vector.drain()
                        nc.vector.tensor_copy(dg[:, :], di[:, :])
                        nc.vector.drain()
                        with dve.Fori(0, NB) as i:
                            for u in range(K):
                                dve.wait_ge(hist_f.sem, hist_f.at(i * K + (u + 1 - K)))
                                nc.vector.tensor_scalar(oh[:, u, :], iob[:, :], dg[:, bass.ds(i * K + u, 1)],
                                                        None, ALU.is_equal).then_inc(hist_o.sem, 1)
                        dve.wait_ge(mm_rdy.sem, mm_rdy.at(1))
                        nc.vector.tensor_copy(R0[:, :], acc[:, 0:LO]).then_inc(hist_r.sem, 1)
                        dve.wait_ge(mm_rdy.sem, mm_rdy.at(2))
                        nc.vector.tensor_copy(junk[:, 0, :], acc[:, LO:2 * LO])
                        nc.vector.drain()
                        nc.vector.tensor_tensor_scan(tt[:, :], junk[:, 0, :], junk[:, 0, :], 0.0, ALU.add, ALU.bypass)
                        nc.vector.drain()
                        nc.vector.tensor_tensor(tt[:, :], tt[:, :], junk[:, 0, :], ALU.subtract)
                        nc.vector.drain()
                        nc.vector.tensor_tensor(R0[:, :], tt[:, :], acc[:, 0:LO], ALU.add).then_inc(hist_r.sem, 1)
                        nc.vector.drain()

                        def ranks(b, h, i):
                            dve.wait_ge(act_done.sem, act_done.at(b - 1))
                            nc.vector.tensor_copy(pr[:, h, :, :], pay[:, bass.ds(b * K, K), :])
                            for u in range(K):
                                nc.vector.tensor_scalar(oh[:, u, :], iob[:, :], dg[:, bass.ds(b * K + u, 1)],
                                                        None, ALU.is_equal)
                                nc.vector.drain()
                                dve.wait_ge(mm_rdy.sem, mm_rdy.at(b * K + u + 3))
                                nc.vector.tensor_tensor_reduce(out=junk[:, u % 2, :], in0=oh[:, u, :], in1=RP[:, 0:LO],
                                                               scale=1.0, scalar=0.0, op0=ALU.mult, op1=ALU.add,
                                                               accum_out=rk[:, h, u:u + 1]).then_inc(hist_o.sem, 1)
                            nc.vector.drain()
                            nc.vector.tensor_copy(rki[:, h, :], rk[:, h, :]).then_inc(d2a.sem, 1)
                        blocks(dve, ranks)
                        dve.wait_ge(in_rdy[0].sem, in_rdy[0].at(16))
                        for u in range(1, K):
                            dve.wait_ge(in_rdy[u % 2].sem, in_rdy[u % 2].at(16 * (u // 2 + 1)))
                            nc.vector.tensor_tensor(pay[:, :, :].rearrange("p j c -> p (j c)"),
                                                    pay[:, :, :].rearrange("p j c -> p (j c)"), zz[:, :],
                                                    ALU.add).then_inc(a2d.sem, 1)
                            nc.vector.drain()

                    @block.tensor
                    def _(pe):
                        nc.tensor.matmul(acc[:, 0:LO], identb[:, :], zb[:, :], start=True, stop=False)
                        with pe.Fori(0, NB) as i:
                            for u in range(K):
                                pe.wait_ge(hist_o.sem, hist_o.at(i * K + u + 1))
                                nc.tensor.matmul(acc[:, 0:LO], identb[:, :], oh[:, u, :], start=False, stop=False)\
                                    .then_inc(hist_f.sem, 1)
                        nc.tensor.matmul(acc[:, 0:LO], identb[:, :], zb[:, :], start=False, stop=True).then_inc(mm_rdy.sem, 1)
                        pe.wait_ge(hist_r.sem, hist_r.at(1))
                        nc.tensor.matmul(acc[:, 0:LO], lower[:, :], R0[:, :], start=True, stop=True)
                        nc.tensor.matmul(acc[:, LO:2 * LO], ones[:, :], R0[:, :], start=True, stop=True).then_inc(mm_rdy.sem, 1)
                        pe.wait_ge(hist_r.sem, hist_r.at(2))
                        nc.tensor.matmul(RP[:, 0:LO], ident[:, :], R0[:, :], start=True, stop=True).then_inc(mm_rdy.sem, 1)
                        with pe.Fori(0, NB) as i:
                            for u in range(K):
                                pe.wait_ge(hist_o.sem, hist_o.at(i * K + u + 1 + EC))
                                nc.tensor.matmul(RP[:, 0:LO], identb[:, :], oh[:, u, :], start=False, stop=True,
                                                 skip_group_check=True)\
                                    .then_inc(mm_rdy.sem, 1)

                    @block.gpsimd
                    def _(pool):
                        pool.wait_ge(step.sem, step.at(1))
                        for u in range(K):
                            pool.dma_start(srt[q][u].rearrange("(p j) c -> p (j c)", p=P), zz[:, :])\
                                .then_inc(sc_done[u].sem, 16)

                        def scatter(b, h, i):
                            pool.wait_ge(d2a.sem, d2a.at(b + 1))
                            pool.nop(nofuse=True)
                            for u in range(K):
                                pool.wait_ge(sc_done[u].sem, sc_done[u].at(b * 16 + 16))
                                pool.nop(nofuse=True)
                                pool.indirect_dma_start(
                                    out=srt[q][u][:, :],
                                    out_offset=bass.IndirectOffsetOnAxis(ap=rki[:, h, u:u + 1], axis=0),
                                    in_=pr[:, h, u, :], in_offset=None).then_inc(sc_done[u].sem, 16)
                        blocks(pool, scatter)

                    @block.scalar
                    def _(act):
                        def freed(b, h, i):
                            for u in range(K):
                                act.wait_ge(sc_done[u].sem, sc_done[u].at(b * 16 + 32))
                            act.nop(nofuse=True)
                            act.sem_inc(act_done.sem, 1)
                        blocks(act, freed)
                        pf = pay[:, :, :].rearrange("p j c -> p (j c)")
                        act.dma_start(pf, srt[q][0].rearrange("(p j) c -> p (j c)", p=P)).then_inc(in_rdy[0].sem, 16)
                        for u in range(1, K):
                            if u > 1:
                                act.wait_ge(a2d.sem, a2d.at(u - 1))
                            act.dma_start(zz[:, :], srt[q][u].rearrange("(p j) c -> p (j c)", p=P))\
                                .then_inc(in_rdy[u % 2].sem, 16)
                step.base += 1
                hist_f.base += EC
                hist_o.base += 2 * EC
                hist_r.base += 2
                mm_rdy.base += 3 + EC
                act_done.base += NB
                d2a.base += NB
                a2d.base += K - 1
                in_rdy[0].base += 16 * ((K + 1) // 2)
                in_rdy[1].base += 16 * (K // 2)
                for u in range(K):
                    sc_done[u].base += 16 * (NB + 1)

        def edge_flags(name, kf):
            with ExitStack() as c:
                eq = sb(f"eq_{name}", [P, EC], fp32, c)
                rowk = sb(f"rowk_{name}", [P, P], fp32, c)
                fx = sb(f"fx_{name}", [P, 1], fp32, c)
                kb = ps(f"kb_{name}", [P, 512], fp32, c)
                with nc.Block() as block:
                    @block.vector
                    def _(dve):
                        nc.vector.memset(cont[name][:, 0:1], 0.0)
                        nc.vector.tensor_tensor(cont[name][:, 1:EC], kf[:, 1:EC], kf[:, 0:EC - 1], ALU.is_equal)
                        nc.vector.tensor_scalar(eq[:, :], kf[:, :], kf[:, 0:1], None, ALU.is_equal)
                        nc.vector.tensor_scalar(rowk[:, :], ident[:, :], kf[:, 0:1], None, ALU.mult).then_inc(step.sem, 1)
                        nc.vector.drain()
                        nc.vector.tensor_reduce(fx[:, :], eq[:, :], AX.X, ALU.add)
                        nc.vector.drain()
                        nc.vector.scalar_tensor_tensor(fix[name][:, :], fx[:, :], -1.0, pcol[:, :], ALU.add, ALU.add)
                        dve.wait_ge(mm_rdy.sem, mm_rdy.at(1))
                        nc.vector.scalar_tensor_tensor(carry[name][:, :], kb[:, 0:P], kf[:, EC - 1:EC], lower[:, :],
                                                       ALU.is_equal, ALU.mult)

                    @block.tensor
                    def _(pe):
                        pe.wait_ge(step.sem, step.at(1))
                        nc.tensor.matmul(kb[:, 0:P], ones[:, :], rowk[:, :], start=True, stop=True).then_inc(mm_rdy.sem, 1)
                step.base += 1
                mm_rdy.base += 1

        with ExitStack() as c:
            pay = sb("pay", [P, EC, 4], fp32, c)
            pi = sb("pi", [P, 2, EC], i32, c)
            pf = sb("pf", [P, EC], fp32, c)
            with nc.Block() as block:
                @block.sync
                def _(sp):
                    sp.dma_start(pi[:, 0, :], src.rearrange("(p j) -> p j", p=P)).then_inc(setup.sem, 16)
                    sp.dma_start(pi[:, 1, :], dst.rearrange("(p j) -> p j", p=P)).then_inc(setup.sem, 16)
                    sp.dma_start(pf[:, :], ew.rearrange("(p j) -> p j", p=P)).then_inc(setup.sem, 16)

                @block.vector
                def _(dve):
                    nc.vector.memset(pay[:, :, 3], 0.0)
                    dve.wait_ge(setup.sem, setup.at(48))
                    nc.vector.tensor_copy(pay[:, :, 0:2].rearrange("p j c -> p c j"), pi[:, :, :])
                    nc.vector.tensor_copy(pay[:, :, 2], pf[:, :])
            setup.base += 48
            sort_pass(0, pay, 0, False)
            sort_pass(1, pay, 0, True)
            with nc.Block() as block:
                @block.vector
                def _(dve):
                    nc.vector.tensor_copy(pf[:, :], pay[:, :, 0])
                    nc.vector.tensor_copy(ew_s[:, :], pay[:, :, 2])
                    nc.vector.tensor_copy(pi[:, :, :], pay[:, :, 0:2].rearrange("p j c -> p c j")).then_inc(step.sem, 1)

                @block.sync
                def _(sp):
                    sp.wait_ge(step.sem, step.at(1))
                    sp.dma_start(src_s.rearrange("(p j) -> p j", p=P), pi[:, 0, :]).then_inc(setup.sem, 16)
                    sp.dma_start(dst_s.rearrange("(p j) -> p j", p=P), pi[:, 1, :]).then_inc(setup.sem, 16)
                    sp.wait_ge(setup.sem, setup.at(32))
            step.base += 1
            setup.base += 32
            edge_flags("src", pf)
        with ExitStack() as c:
            di = sb("di", [P, EC], i32, c)
            df = sb("df", [P, EC], fp32, c)
            with nc.Block() as block:
                @block.sync
                def _(sp):
                    sp.dma_start(di[:, :], dst.rearrange("(p j) -> p j", p=P)).then_inc(setup.sem, 16)

                @block.vector
                def _(dve):
                    dve.wait_ge(setup.sem, setup.at(16))
                    nc.vector.tensor_copy(df[:, :], di[:, :])
            setup.base += 16
            edge_flags("dst", df)


        wcat = sb("wcat", [P, 2 * D + 2 * H])
        wuv = sb("wuv", [P, 2 * D])
        wl = sb("wl", [P, D])
        wlp = sb("wlp", [P, D])
        wb = sb("wb", [P, B, D])
        wf = sb("wf", [P, 4, D])
        gb = sb("gb", [P, 2, D])
        w2b = sb("w2b", [P, D])
        bcol = sb("bcol", [P, 4])
        b2b = sb("b2b", [P, 1])
        BW = 2 * D + 2 * H
        bias3 = sb("bias3", [3, BW], bf16)
        ones3 = sb("ones3", [3, P], bf16)
        bcat = bias3[:, :]
        with ExitStack() as c:
            at = sb("at", [P, 2, D], fp32, c)
            pt = sb("pt", [P, 2, D], fp32, c)
            br = sb("br", [1, 2, D], fp32, c)
            rest = sb("rest", [1, BW], fp32, c)
            back = sb("back", [1, BW], fp32, c)
            part = sb("part", [1, 3, BW], bf16, c)

            def row(v):
                return v.rearrange("(o d) -> o d", o=1)
            with nc.Block() as block:
                @block.sync
                def _(sp):
                    loads = [(wcat[:, 0:D], W), (wcat[:, D + 2 * H:], skip_W),
                             (wuv[:, 0:D], W1[0:D, :]), (wuv[:, D:2 * D], W1[D:2 * D, :]), (wl[:, :], Wl),
                             (wlp[:, :], loop_W), (wb[:, :, :], wbase.rearrange("b i o -> i b o")),
                             (wf[:, :, :], lw.rearrange("k i o -> i k o")),
                             (gb[:, 0, :], row(ln_g).broadcast_to([P, D])), (gb[:, 1, :], row(ln_b).broadcast_to([P, D])),
                             (w2b[:, :], W2.rearrange("d o -> o d").broadcast_to([P, D])),
                             (b2b[:, :], row(b2).broadcast_to([P, 1])),
                             (at[:, 0, :], att_s.rearrange("(o h) c -> o (h c)", o=1).broadcast_to([P, D])),
                             (at[:, 1, :], att_d.rearrange("(o h) c -> o (h c)", o=1).broadcast_to([P, D])),
                             (br[0:1, 0, :], row(gat_b)), (br[0:1, 1, :], row(skip_b)),
                             (bcol[:, 0:1], b1.rearrange("(d o) -> d o", o=1)),
                             (bcol[:, 1:2], bl.rearrange("(d o) -> d o", o=1)),
                             (bcol[:, 2:3], h_bias.rearrange("(d o) -> d o", o=1))]
                    for o, i in loads:
                        sp.dma_start(o, i).then_inc(setup.sem, 16)
                    assert len(loads) == 19
                    sp.wait_ge(step.sem, step.at(1))
                    for n in range(3):
                        sp.dma_start(bias3[n:n + 1, :], part[0:1, n, :]).then_inc(setup.sem, 16)
                    sp.wait_ge(setup.sem, setup.at(16 * 22))

                @block.vector
                def _(dve):
                    nc.vector.memset(rest[0:1, :], 0.0)
                    nc.vector.memset(bcol[:, 3:4], 0.0)
                    nc.vector.memset(ones3[:, :], 1.0)
                    dve.wait_ge(setup.sem, setup.at(16 * 19))
                    for m in range(2):
                        nc.vector.tensor_tensor(pt[:, m, :], wcat[:, 0:D], at[:, m, :], ALU.mult)
                    nc.vector.drain()
                    nc.vector.tensor_reduce(wcat[:, D:D + 2 * H], pt[:, :, :].rearrange("p m (h c) -> p (m h) c", c=C),
                                            AX.X, ALU.add)
                    nc.vector.tensor_tensor(rest[0:1, D + 2 * H:BW], br[0:1, 0, :], br[0:1, 1, :], ALU.add)
                    nc.vector.drain()
                    for n in range(3):
                        q = nc.vector.tensor_copy(part[0:1, n, :], rest[0:1, :])
                        if n < 2:
                            nc.vector.drain()
                            nc.vector.tensor_copy(back[0:1, :], part[0:1, n, :])
                            nc.vector.drain()
                            nc.vector.tensor_tensor(rest[0:1, :], rest[0:1, :], back[0:1, :], ALU.subtract)
                            nc.vector.drain()
                    q.then_inc(step.sem, 1)
        setup.base += 16 * 22
        step.base += 1

        def sp_stream(sp, load, store, lead=2):
            for b in range(lead):
                load(b, b % 2, b // 2)
            first = 2 * lead - 2
            for b in range(lead, first):
                load(b, b % 2, b // 2)
                store(b - lead, (b - lead) % 2, (b - lead) // 2)
            with sp.Fori(first // 2, NB // 2 - 1) as i:
                for h in range(2):
                    load(2 * i + h, h, i)
                    t = (h - lead) % 2
                    store(2 * i + (h - lead), t, i + (h - lead - t) // 2)
            for b in range(NB - 2, NB + lead):
                if b < NB:
                    load(b, b % 2, b // 2)
                store(b - lead, (b - lead) % 2, (b - lead) // 2)

        def stored(eng, n):
            for h in range(2):
                eng.wait_ge(st_done[h].sem, st_done[h].at(16 * n * NB // 2))

        def stats(xt, st, mv):
            for g in range(K):
                nc.vector.bn_stats(st[:, g, :], xt[:, g, :])
            nc.vector.drain()
            for g in range(K):
                q = nc.vector.bn_aggr(mv[:, g, :], st[:, g, :])
            return q

        def scale_shift(mv, sd, rs, nm):
            nc.vector.reciprocal(rs, sd)
            nc.vector.drain()
            return nc.vector.scalar_tensor_tensor(nm, mv, -1.0, rs, ALU.mult, ALU.mult)

        def inv_dev(pool, asked, n, mv, rs, answered):
            pool.wait_ge(asked.sem, asked.at(n))
            pool.nop(nofuse=True)
            nc.gpsimd.tensor_scalar(rs, mv[:, :, 1], 1e-5, None, ALU.add)
            nc.gpsimd.drain()
            nc.gpsimd.tensor_tensor(rs, rs, half[:, :], ALU.pow).then_inc(answered.sem, 1)

        def shift(mv, rs, nm):
            return nc.vector.scalar_tensor_tensor(nm, mv[:, :, 0], -1.0, rs, ALU.mult, ALU.mult)

        class Product:

            def __init__(self, c, name, mm):
                self.tp = ps(f"tp_{name}", [P, 2, 512], fp32, c)
                self.mm = mm
                self.hT = sb(f"hT_{name}", [P, K * D], fp32, c)
                self.tp_rdy, self.hT_rdy = tp_rdy, hT_rdy

            def transpose(self, pe, b, rows, rdy):
                pe.wait_ge(rdy.sem, rdy.at(b + 1))
                for g in range(K):
                    q = nc.tensor.transpose(self.tp[:, g // 4, (g % 4) * D:(g % 4 + 1) * D], rows[:, g, :], ident[:, :])
                    if g == 3 or g == K - 1:
                        q.then_inc(self.tp_rdy.sem, 1)

            def multiply(self, pe, b, w, bias, at=None):
                width = w.shape[-1]
                at = b if at is None else at
                for g in range(K):
                    if g == 0 or g == 4:
                        pe.wait_ge(self.hT_rdy.sem, self.hT_rdy.at(b * 2 + (1 if g == 0 else 2)))
                    pe.wait_ge(mm_free.sem, mm_free.at(at * K + (g - 2 if g < 3 else g - 3)))
                    o = self.mm[:, g % 4, 0:width]
                    nc.tensor.matmul(o, ones3[:, :], bias, start=True, stop=False)
                    nc.tensor.matmul(o, self.hT[:, g * D:(g + 1) * D], w, start=False, stop=True)\
                        .then_inc(mm_rdy.sem, 1)

            def copy(self, eng, b, by_dve=False):
                for m, (lo, hi) in enumerate(((0, 512), (512, K * D))):
                    eng.wait_ge(self.tp_rdy.sem, self.tp_rdy.at(b * 2 + m + 1))
                    o, t = self.hT[:, lo:hi], self.tp[:, m, 0:hi - lo]
                    q = nc.vector.tensor_copy(o, t) if by_dve else nc.scalar.activation(o, t, ACT.Copy)
                    q.then_inc(self.hT_rdy.sem, 1)

            def take(self, act, b, o, func=ACT.Copy, at=None):
                at = b if at is None else at
                for g in range(K):
                    act.wait_ge(mm_rdy.sem, mm_rdy.at(at * K + g + 1))
                    nc.scalar.activation(o[:, g, :], self.mm[:, g % 4, 0:o.shape[-1]], func).then_inc(mm_free.sem, 1)

            def end(self):
                self.tp_rdy.base += 2 * NB
                self.hT_rdy.base += 2 * NB
                mm_rdy.base += K * NB
                mm_free.base += K * NB

        class Dense:

            def __init__(self, c, name, n, shared=None):
                self.t = ps(f"dt_{name}", [P, 2, 512], fp32, c)
                self.m = ps(f"dm_{name}", [P, 2, 512], fp32, c)
                self.hT = shared.hT if shared else sb(f"dh_{name}", [P, K * D], fp32, c)
                self.oT = sb(f"do_{name}", [P, K * D], fp32, c)
                self.shared = shared
                self.there, self.copied, self.product, self.biased, self.back, self.used = dense_c[n]

            CHUNKS = ((0, 4), (4, K))

            def transpose(self, pe, b, rows, rdy):
                pe.wait_ge(rdy.sem, rdy.at(b + 1))
                pe.wait_ge(self.used.sem, self.used.at(b))
                for m, (lo, hi) in enumerate(self.CHUNKS):
                    for g in range(lo, hi):
                        q = nc.tensor.transpose(self.t[:, m, (g - lo) * D:(g - lo + 1) * D], rows[:, g, :], ident[:, :])
                    q.then_inc(self.there.sem, 1)

            def copy(self, act, b):
                for m, (lo, hi) in enumerate(self.CHUNKS):
                    act.wait_ge(self.there.sem, self.there.at(2 * b + m + 1))
                    nc.scalar.activation(self.hT[:, lo * D:hi * D], self.t[:, m, 0:(hi - lo) * D], ACT.Copy)\
                        .then_inc(self.copied.sem, 1)

            def multiply(self, pe, b, w):
                src_c = (self.shared or self).copied
                for m, (lo, hi) in enumerate(self.CHUNKS):
                    pe.wait_ge(src_c.sem, src_c.at(2 * b + m + 1))
                    nc.tensor.matmul(self.m[:, m, 0:(hi - lo) * D], w, self.hT[:, lo * D:hi * D], start=True, stop=True)\
                        .then_inc(self.product.sem, 1)

            def bias(self, act, b, col, func=ACT.Identity):
                for m, (lo, hi) in enumerate(self.CHUNKS):
                    act.wait_ge(self.product.sem, self.product.at(2 * b + m + 1))
                    nc.scalar.activation(self.oT[:, lo * D:hi * D], self.m[:, m, 0:(hi - lo) * D], func, bias=col)\
                        .then_inc(self.biased.sem, 1)

            def turn_back(self, pe, b):
                if self.shared:
                    pe.wait_ge(self.used.sem, self.used.at(b))
                for m, (lo, hi) in enumerate(self.CHUNKS):
                    pe.wait_ge(self.biased.sem, self.biased.at(2 * b + m + 1))
                    for g in range(lo, hi):
                        q = nc.tensor.transpose(self.t[:, m, (g - lo) * D:(g - lo + 1) * D], self.oT[:, g * D:(g + 1) * D],
                                                ident[:, :])
                    q.then_inc(self.back.sem, 1)

            def result(self, eng, b, m):
                lo, hi = self.CHUNKS[m]
                eng.wait_ge(self.back.sem, self.back.at(2 * b + m + 1))
                return lo, hi, self.t[:, m, 0:(hi - lo) * D]

            def end(self):
                if not self.shared:
                    self.there.base += 2 * NB
                    self.copied.base += 2 * NB
                for q in (self.product, self.biased, self.back):
                    q.base += 2 * NB
                self.used.base += NB

        def skewed(eng, body, lag=1):
            lead = lag + lag % 2
            for b in range(lead):
                body(b, b % 2, b // 2)
            with eng.Fori(lead // 2, NB // 2 - 1) as i:
                for h in range(2):
                    body(2 * i + h, h, i)
            for b in range(NB - 2, NB + lag):
                body(b, b % 2, b // 2)

        def before(h, i):
            return 1 - h, i - (1 - h)

        def flat(t):
            return t.rearrange("p g d -> p (g d)")

        def stage_base(nd=0, na=0, loads=0, stores=0, gathers=None, idx=0):
            d2a.base += nd * NB
            a2d.base += na * NB
            for h in range(2):
                in_rdy[h].base += 16 * loads * NB // 2
                st_done[h].base += 16 * stores * NB // 2
                idx_rdy[h].base += 16 * idx * NB // 2
                for t in gathers or ():
                    t[h].base += 16 * K * NB // 2

        xn = nrows(x)
        with ExitStack() as c:
            xin = sb("xin", [P, 2, K, D], fp32, c)
            st = sb("st", [P, 2, K, 6], fp32, c)
            mv = sb("mv", [P, 2, K, 2], fp32, c)
            sd = sb("sd", [P, 2, K], fp32, c)
            rs = sb("rs", [P, 2, K], fp32, c)
            nm = sb("nm", [P, 2, K], fp32, c)
            hh = sb("hh", [P, 2, K, D], fp32, c)
            o0 = sb("o0", [P, 2, K, 2 * D + 2 * H], fp32, c)
            mm = ps("n0_mm", [P, 4, 512], fp32, c)
            pr = Product(c, "n0", mm)
            with nc.Block() as block:
                @block.sync
                def _(sp):
                    def load(b, h, i):
                        sp.wait_ge(act_done.sem, act_done.at(b - 1))
                        sp.nop(nofuse=True)
                        sp.dma_start(xin[:, h, :, :].rearrange("p g d -> p (g d)"), pick(xn, b)).then_inc(in_rdy[h].sem, 16)

                    def store(b, h, i):
                        sp.wait_ge(taken.sem, taken.at(b + 1))
                        sp.nop(nofuse=True)
                        sp.dma_start(pick(nparts(G0, 0, D + H), b), o0[:, h, :, 0:D + H]).then_inc(st_done[h].sem, 16)
                        sp.dma_start(pick(nparts(AD, 0, H), b), o0[:, h, :, D + H:D + 2 * H]).then_inc(st_done[h].sem, 16)
                        sp.dma_start(pick(nparts(SK, 0, D), b), o0[:, h, :, D + 2 * H:]).then_inc(st_done[h].sem, 16)
                    sp_stream(sp, load, store)
                    stored(sp, 3)

                @block.vector
                def _(dve):
                    def body(b, h, i):
                        hp, ip = before(h, i)
                        first, last = isinstance(b, int) and b == 0, isinstance(b, int) and b == NB
                        if not last:
                            dve.wait_ge(in_rdy[h].sem, in_rdy[h].at(16 * i + 16))
                            stats(xin[:, h], st[:, h], mv[:, h]).then_inc(d2a.sem, 1)
                        if not first:
                            pr.copy(dve, b - 1, True)
                        if not last:
                            dve.wait_ge(a2d.sem, a2d.at(b + 1))
                            scale_shift(mv[:, h, :, 0], sd[:, h, :], rs[:, h, :], nm[:, h, :]).then_inc(dve_done.sem, 1)
                    skewed(dve, body)

                @block.scalar
                def _(act):
                    def body(b, h, i):
                        hp, ip = before(h, i)
                        first, last = isinstance(b, int) and b == 0, isinstance(b, int) and b == NB
                        if not last:
                            act.wait_ge(d2a.sem, d2a.at(b + 1))
                            nc.scalar.activation(sd[:, h, :], mv[:, h, :, 1], ACT.Sqrt, bias=eps5[:, :]).then_inc(a2d.sem, 1)
                            act.wait_ge(dve_done.sem, dve_done.at(b + 1))
                            for g in range(K):
                                q = nc.scalar.activation(hh[:, h, g, :], xin[:, h, g, :], ACT.Relu,
                                                         bias=nm[:, h, g:g + 1], scale=rs[:, h, g:g + 1])
                            q.then_inc(for_pe.sem, 1)
                            act.drain()
                            act.sem_inc(act_done.sem, 1)
                        if not first:
                            act.wait_ge(st_done[hp].sem, st_done[hp].at(48 * ip))
                            pr.take(act, b - 1, o0[:, hp])
                            act.drain()
                            act.sem_inc(taken.sem, 1)
                    skewed(act, body)

                @block.tensor
                def _(pe):
                    def body(b, h, i):
                        first, last = isinstance(b, int) and b == 0, isinstance(b, int) and b == NB
                        if not first:
                            pr.multiply(pe, b - 1, wcat[:, :], bcat)
                        if not last:
                            pr.transpose(pe, b, hh[:, h], for_pe)
                    skewed(pe, body)
            pr.end()
            for_pe.base += NB
            dve_done.base += NB
            act_done.base += NB
            taken.base += NB
            stage_base(nd=1, na=1, loads=1, stores=3)

        def gather_rows(pool, slot, slot_rdy, table, rows, rdy, *free):
            def body(b, h, i):
                pool.wait_ge(slot_rdy[h].sem, slot_rdy[h].at(16 * i + 16))
                pool.nop(nofuse=True)
                for c in free:
                    pool.wait_ge(c.sem, c.at(b - 1))
                    pool.nop(nofuse=True)
                for g in range(K):
                    gather(pool, rows[:, h, g, :], table, slot[:, h, g:g + 1]).then_inc(rdy[h].sem, 16)
            return body

        def gathered(sp, rdy, h, i):
            if not (isinstance(i, int) and i == 0):
                sp.wait_ge(rdy[h].sem, rdy[h].at(16 * K * i))
                sp.nop(nofuse=True)

        def add_carry(name, table, tail, width):
            with ExitStack() as c:
                fr = sb(f"fr_{table.name}", [P, table.shape[1]], fp32, c)
                cp = ps(f"cp_{table.name}", [P, 512], fp32, c)
                with nc.Block() as block:
                    @block.gpsimd
                    def _(pool):
                        gather(pool, fr[:, :], table, fix[name][:, :]).then_inc(pdma.sem, 16)
                        pool.wait_ge(step.sem, step.at(1))
                        pool.indirect_dma_start(out=table[:, :], in_=fr[:, :], in_offset=None,
                                                out_offset=bass.IndirectOffsetOnAxis(ap=fix[name][:, :], axis=0))\
                            .then_inc(pdma.sem, 16)
                        pool.wait_ge(pdma.sem, pdma.at(32))

                    @block.tensor
                    def _(pe):
                        nc.tensor.matmul(cp[:, 0:width], carry[name][:, :], tail[:, 0:width], start=True, stop=True)\
                            .then_inc(mm_rdy.sem, 1)

                    @block.vector
                    def _(dve):
                        dve.wait_ge(pdma.sem, pdma.at(16))
                        dve.wait_ge(mm_rdy.sem, mm_rdy.at(1))
                        nc.vector.tensor_tensor(fr[:, 0:width], fr[:, 0:width], cp[:, 0:width], ALU.add)\
                            .then_inc(step.sem, 1)
                pdma.base += 32
                step.base += 1
                mm_rdy.base += 1

        WT = D + 2 * H
        with ExitStack() as c:
            ib = sb("e0_ib", [P, 2, K], i32, c)
            jb = sb("e0_jb", [P, 2, K], i32, c)
            rst = sb("e0_rst", [P, EC], fp32, c)
            xr = sb("e0_xr", [P, 2, K, D + H], fp32, c)
            ar = sb("e0_ar", [P, 2, K, H], fp32, c)
            eb = sb("e0_eb", [P, K, H], fp32, c)
            mb = sb("e0_mb", [P, 2, H, K + 1], fp32, c)
            zr = sb("e0_zr", [P, 2, H, K + 1], fp32, c)
            fg = sb("e0_fg", [P, 2, 2, H, K], fp32, c)
            S = sb("e0_S", [P, 2, K, WT], fp32, c)
            src_e, dst_e, t0e = ecol(src), ecol(dst), erows(T0)
            ti = sb("e0_ti", [P, EC], i32, c)
            tf = sb("e0_tf", [P, EC], fp32, c)
            tm = sb("e0_tm", [P, EC], fp32, c)
            wcb = sb("e0_wcb", [P, NB * B], fp32, c)
            with nc.Block() as block:
                @block.sync
                def _(sp):
                    def load(b, h, i):
                        gathered(sp, row_rdy, h, i)
                        sp.dma_start(ib[:, h, :], pick(src_e, b)).then_inc(idx_rdy[h].sem, 16)
                        gathered(sp, roy_rdy, h, i)
                        sp.dma_start(jb[:, h, :], pick(dst_e, b)).then_inc(idy_rdy[h].sem, 16)

                    def store(b, h, i):
                        sp.wait_ge(dve_done.sem, dve_done.at(b + 1))
                        sp.nop(nofuse=True)
                        sp.dma_start(pick(t0e, b), S[:, h, :, :].rearrange("p g d -> p (g d)")).then_inc(st_done[h].sem, 16)
                    sp.dma_start(ti[:, :], etype.rearrange("(p j) -> p j", p=P)).then_inc(setup.sem, 16)
                    sp.dma_start(wcb[:, 0:R * B], wcomp.rearrange("(o r) b -> o (r b)", o=1).broadcast_to([P, R * B]))\
                        .then_inc(setup.sem, 16)
                    sp_stream(sp, load, store)
                    stored(sp, 1)

                @block.gpsimd
                def _(pool):
                    rows = gather_rows(pool, ib, idx_rdy, G0, xr, row_rdy)
                    scores = gather_rows(pool, jb, idy_rdy, AD, ar, roy_rdy, dve_done)

                    def body(b, h, i):
                        scores(b, h, i)
                        rows(b, h, i)
                    blocks(pool, body)

                @block.vector
                def _(dve):
                    nc.vector.tensor_scalar(rst[:, :], cont["dst"][:, :], -1.0, NEG, ALU.add, ALU.mult)
                    nc.vector.memset(mb[:, :, :, :], -NEG)
                    nc.vector.memset(wcb[:, R * B:NB * B], 0.0)
                    nc.vector.memset(wc_e[:, :, :], 0.0)
                    dve.wait_ge(setup.sem, setup.at(32))
                    nc.vector.tensor_copy(tf[:, :], ti[:, :])
                    nc.vector.memset(zr[:, :, :, :], 0.0)
                    nc.vector.memset(S[:, :, :, :], 0.0)
                    nc.vector.drain()

                    def body(b, h, i):
                        dve.wait_ge(row_rdy[h].sem, row_rdy[h].at(16 * K * i + 16 * K))
                        dve.wait_ge(roy_rdy[h].sem, roy_rdy[h].at(16 * K * i + 16 * K))
                        nc.vector.tensor_tensor(eb[:, :, :], xr[:, h, :, D:D + H], ar[:, h, :, :], ALU.add)
                        nc.vector.tensor_copy(mb[:, h, :, 0], mb[:, 1 - h, :, K])
                        nc.vector.tensor_copy(zr[:, h, :, 0], zr[:, 1 - h, :, K])
                        nc.vector.drain()
                        nc.vector.scalar_tensor_tensor(eb[:, :, :], eb[:, :, :], 0.2, eb[:, :, :], ALU.mult, ALU.max)
                        nc.vector.drain()
                        for a in range(H):
                            nc.vector.tensor_tensor_scan(mb[:, h, a, 1:K + 1], rst[:, bass.ds(b * K, K)], eb[:, :, a],
                                                         mb[:, h, a, 0:1], ALU.add, ALU.max)
                        nc.vector.drain()
                        nc.vector.tensor_tensor(fg[:, h, 1], eb[:, :, :].rearrange("p g a -> p a g"),
                                                mb[:, h, :, 1:K + 1], ALU.subtract)
                        nc.vector.tensor_tensor(fg[:, h, 0], mb[:, h, :, 0:K], mb[:, h, :, 1:K + 1], ALU.subtract)
                        nc.vector.drain()
                        nc.vector.tensor_tensor(fg[:, h, 0], fg[:, h, 0],
                                                rst[:, bass.ds(b * K, K)].rearrange("p (o g) -> p o g", o=1)
                                                .broadcast_to([P, H, K]), ALU.add).then_inc(d2a.sem, 1)
                        dve.wait_ge(a2d.sem, a2d.at(b + 1))
                        for a in range(H):
                            nc.vector.tensor_tensor_scan(zr[:, h, a, 1:K + 1], fg[:, h, 0, a, :], fg[:, h, 1, a, :],
                                                         zr[:, h, a, 0:1], ALU.mult, ALU.add)
                        xv = xr[:, h, :, 0:D].rearrange("p g (a c) -> p g a c", a=H)
                        nc.vector.tensor_tensor(xv, xv, fg[:, h, 1].rearrange("p a g -> p g a").unsqueeze(3)
                                                .broadcast_to([P, K, H, C]), ALU.mult)
                        dve.wait_ge(st_done[h].sem, st_done[h].at(16 * i))
                        for g in range(K):
                            pv = S[:, h, g - 1, 0:D] if g else S[:, 1 - h, K - 1, 0:D]
                            nc.vector.tensor_tensor(S[:, h, g, 0:D].rearrange("p (a c) -> p a c", a=H),
                                                    pv.rearrange("p (a c) -> p a c", a=H),
                                                    fg[:, h, 0, :, g].unsqueeze(2).broadcast_to([P, H, C]), ALU.mult)
                            nc.vector.drain()
                            nc.vector.tensor_tensor(S[:, h, g, 0:D], S[:, h, g, 0:D], xr[:, h, g, 0:D], ALU.add)
                            nc.vector.drain()
                        nc.vector.tensor_scalar(tm[:, :], tf[:, :], iof[:, bass.ds(b, 1)], None, ALU.is_equal)
                        nc.vector.drain()
                        for n in range(B):
                            nc.vector.scalar_tensor_tensor(wc_e[:, :, n], tm[:, :], wcb[:, bass.ds(b * B + n, 1)],
                                                           wc_e[:, :, n], ALU.mult, ALU.add)
                        nc.vector.tensor_copy(S[:, h, :, D:D + H], zr[:, h, :, 1:K + 1].rearrange("p a g -> p g a"))
                        nc.vector.tensor_copy(S[:, h, :, D + H:WT], mb[:, h, :, 1:K + 1].rearrange("p a g -> p g a"))\
                            .then_inc(dve_done.sem, 1)
                    blocks(dve, body)

                @block.scalar
                def _(act):
                    def body(b, h, i):
                        act.wait_ge(d2a.sem, d2a.at(b + 1))
                        v = fg[:, h].rearrange("p m a g -> p (m a g)")
                        nc.scalar.activation(v, v, ACT.Exp).then_inc(a2d.sem, 1)
                    blocks(act, body)
            dve_done.base += NB
            setup.base += 32
            stage_base(nd=1, na=1, stores=1, gathers=(row_rdy, roy_rdy), idx=1)
            for h in range(2):
                idy_rdy[h].base += 16 * NB // 2

            tail = S[:, 1, K - 1, :]
            with ExitStack() as c2:
                fr = sb("f0_fr", [P, WT], fp32, c2)
                cT = sb("f0_cT", [P, P], fp32, c2)
                pen = sb("f0_pen", [P, P], fp32, c2)
                dg = sb("f0_dg", [P, H, P], fp32, c2)
                vl = sb("f0_vl", [P, H, P], fp32, c2)
                vT = sb("f0_vT", [P, H, P], fp32, c2)
                top = sb("f0_top", [P, H], fp32, c2)
                ab = sb("f0_ab", [P, 2, H], fp32, c2)
                mx = sb("f0_mx", [P, H], fp32, c2)
                cs = sb("f0_cs", [P, D + H], fp32, c2)
                pc = ps("f0_pc", [P, 512], fp32, c2)
                pm = ps("f0_pm", [P, H * P], fp32, c2)
                pv = ps("f0_pv", [P, H * P], fp32, c2)
                po = ps("f0_po", [P, 512], fp32, c2)
                with nc.Block() as block:
                    @block.gpsimd
                    def _(pool):
                        gather(pool, fr[:, :], T0, fix["dst"][:, :]).then_inc(pdma.sem, 16)
                        pool.wait_ge(step.sem, step.at(3))
                        pool.indirect_dma_start(out=T0[:, :], in_=fr[:, :], in_offset=None,
                                                out_offset=bass.IndirectOffsetOnAxis(ap=fix["dst"][:, :], axis=0))\
                            .then_inc(pdma.sem, 16)
                        pool.wait_ge(pdma.sem, pdma.at(32))

                    @block.tensor
                    def _(pe):
                        nc.tensor.transpose(pc[:, 0:P], carry["dst"][:, :], ident[:, :]).then_inc(mm_rdy.sem, 1)
                        pe.wait_ge(step.sem, step.at(1))
                        nc.tensor.matmul(pm[:, :], ones[:, :], dg[:, :, :].rearrange("p a q -> p (a q)"),
                                         start=True, stop=True).then_inc(mm_rdy.sem, 1)
                        pe.wait_ge(step.sem, step.at(2))
                        for a in range(H):
                            q = nc.tensor.transpose(pv[:, a * P:(a + 1) * P], vl[:, a, :], ident[:, :])
                        q.then_inc(mm_rdy.sem, 1)
                        pe.wait_ge(for_pe.sem, for_pe.at(1))
                        for a in range(H):
                            nc.tensor.matmul(po[:, a * C:(a + 1) * C], vT[:, a, :], tail[:, a * C:(a + 1) * C],
                                             start=True, stop=True)
                            q = nc.tensor.matmul(po[:, D + a:D + a + 1], vT[:, a, :], tail[:, D + a:D + a + 1],
                                                 start=True, stop=True)
                        q.then_inc(mm_rdy.sem, 1)

                    @block.vector
                    def _(dve):
                        for a in range(H):
                            q = nc.vector.tensor_scalar(dg[:, a, :], ident[:, :], tail[:, D + H + a:D + H + a + 1],
                                                        None, ALU.mult)
                        q.then_inc(step.sem, 1)
                        dve.wait_ge(mm_rdy.sem, mm_rdy.at(1))
                        nc.vector.tensor_copy(cT[:, :], pc[:, 0:P])
                        nc.vector.drain()
                        nc.vector.tensor_scalar(pen[:, :], cT[:, :], -1.0, NEG, ALU.add, ALU.mult)
                        nc.vector.drain()
                        dve.wait_ge(mm_rdy.sem, mm_rdy.at(2))
                        for a in range(H):
                            nc.vector.tensor_tensor(vl[:, a, :], pm[:, a * P:(a + 1) * P], pen[:, :], ALU.add)
                        nc.vector.drain()
                        nc.vector.tensor_reduce(top[:, :], vl[:, :, :], AX.X, ALU.max)
                        nc.vector.drain()
                        nc.vector.tensor_tensor(vl[:, :, :], vl[:, :, :], top[:, :].unsqueeze(2).broadcast_to([P, H, P]),
                                                ALU.subtract).then_inc(d2a.sem, 1)
                        dve.wait_ge(a2d.sem, a2d.at(1))
                        for a in range(H):
                            q = nc.vector.tensor_tensor(vl[:, a, :], vl[:, a, :], cT[:, :], ALU.mult)
                        q.then_inc(step.sem, 1)
                        dve.wait_ge(pdma.sem, pdma.at(16))
                        nc.vector.tensor_tensor(mx[:, :], fr[:, D + H:WT], top[:, :], ALU.max)
                        nc.vector.drain()
                        nc.vector.tensor_tensor(ab[:, 0, :], fr[:, D + H:WT], mx[:, :], ALU.subtract)
                        nc.vector.tensor_tensor(ab[:, 1, :], top[:, :], mx[:, :], ALU.subtract).then_inc(d2a.sem, 1)
                        dve.wait_ge(mm_rdy.sem, mm_rdy.at(3))
                        nc.vector.tensor_copy(vT[:, :, :].rearrange("p a q -> p (a q)"), pv[:, :]).then_inc(for_pe.sem, 1)
                        dve.wait_ge(a2d.sem, a2d.at(2))
                        dve.wait_ge(mm_rdy.sem, mm_rdy.at(4))
                        for o, w in ((0, C), (D, 1)):
                            f = fr[:, o:o + H * w].rearrange("p (a c) -> p a c", a=H)
                            nc.vector.tensor_tensor(f, f, ab[:, 0, :].unsqueeze(2).broadcast_to([P, H, w]), ALU.mult)
                            nc.vector.tensor_tensor(cs[:, o:o + H * w].rearrange("p (a c) -> p a c", a=H),
                                                    po[:, o:o + H * w].rearrange("p (a c) -> p a c", a=H),
                                                    ab[:, 1, :].unsqueeze(2).broadcast_to([P, H, w]), ALU.mult)
                        nc.vector.drain()
                        nc.vector.tensor_copy(fr[:, D + H:WT], mx[:, :])
                        nc.vector.tensor_tensor(fr[:, 0:D + H], fr[:, 0:D + H], cs[:, :], ALU.add).then_inc(step.sem, 1)

                    @block.scalar
                    def _(act):
                        act.wait_ge(d2a.sem, d2a.at(1))
                        nc.scalar.activation(vl[:, :, :], vl[:, :, :], ACT.Exp).then_inc(a2d.sem, 1)
                        act.wait_ge(d2a.sem, d2a.at(2))
                        nc.scalar.activation(ab[:, :, :], ab[:, :, :], ACT.Exp).then_inc(a2d.sem, 1)
                pdma.base += 32
                step.base += 3
                mm_rdy.base += 4
                for_pe.base += 1
                d2a.base += 2
                a2d.base += 2

        with ExitStack() as c:
            ib = sb("n1_ib", [P, 2, K], i32, c)
            tr = sb("n1_tr", [P, 2, K, WT], fp32, c)
            g0 = sb("n1_g0", [P, 2, K, D + H], fp32, c)
            ad = sb("n1_ad", [P, 2, K, H], fp32, c)
            sk = sb("n1_sk", [P, 2, K, D], fp32, c)
            xin = sb("n1_xin", [P, 2, K, D], fp32, c)
            eb = sb("n1_eb", [P, 2, K, H], fp32, c)
            mx = sb("n1_mx", [P, K, H], fp32, c)
            fg = sb("n1_fg", [P, 2, 2, K, H], fp32, c)
            st = sb("n1_st", [P, K, 6], fp32, c)
            mv = sb("n1_mv", [P, 2, K, 2], fp32, c)
            rs = sb("n1_rs", [P, 3, K], fp32, c)
            nm = sb("n1_nm", [P, 3, K], fp32, c)
            x1 = sb("n1_x1", [P, 2, K, D], fp32, c)
            hh = sb("n1_hh", [P, 2, K, D], fp32, c)
            uv = sb("n1_uv", [P, 2, 2, K, D], fp32, c)
            pu = Dense(c, "n1u", 0)
            pv = Dense(c, "n1v", 1, shared=pu)
            lst, x1n = ncol(last_dst), nrows(X1)
            with nc.Block() as block:
                @block.sync
                def _(sp):
                    def index(b, h, i):
                        gathered(sp, nrow_rdy, h, i)
                        sp.dma_start(ib[:, h, :], pick(lst, b)).then_inc(idx_rdy[h].sem, 16)

                    def load(b, h, i):
                        if not (isinstance(b, int) and b == NB - 1):
                            index(b + 1, 1 - h, i + h)
                        if not (isinstance(b, int) and b < 2):
                            sp.wait_ge(d2v.sem, d2v.at(2 * b - 3))
                            sp.nop(nofuse=True)
                        sp.dma_start(g0[:, h, :, :].rearrange("p g d -> p (g d)"), pick(nrows(G0), b)).then_inc(in_rdy[h].sem, 16)
                        sp.dma_start(ad[:, h, :, :].rearrange("p g d -> p (g d)"), pick(nrows(AD), b)).then_inc(in_rdy[h].sem, 16)
                        sp.dma_start(sk[:, h, :, :].rearrange("p g d -> p (g d)"), pick(nrows(SK), b)).then_inc(in_rdy[h].sem, 16)
                        sp.wait_ge(rows_free.sem, rows_free.at(b - 1))
                        sp.nop(nofuse=True)
                        sp.dma_start(xin[:, h, :, :].rearrange("p g d -> p (g d)"), pick(xn, b)).then_inc(in_rdy[h].sem, 16)

                    def store(b, h, i):
                        sp.wait_ge(taken.sem, taken.at(b + 1))
                        sp.nop(nofuse=True)
                        sp.dma_start(pick(x1n, b), x1[:, h, :, :].rearrange("p g d -> p (g d)")).then_inc(st_done[h].sem, 16)
                        sp.dma_start(pick(nparts(P1, 0, D), b), hh[:, h]).then_inc(st_done[h].sem, 16)
                        sp.dma_start(pick(nparts(P1, D, 2 * D), b), uv[:, h, 1]).then_inc(st_done[h].sem, 16)
                        sp.dma_start(pick(nparts(U1, 0, D), b), uv[:, h, 0]).then_inc(st_done[h].sem, 16)
                    index(0, 0, 0)
                    sp_stream(sp, load, store, lead=3)
                    stored(sp, 4)

                @block.gpsimd
                def _(pool):
                    rows = gather_rows(pool, ib, idx_rdy, T0, tr, nrow_rdy, rows_free)
                    def body(b, h, i):
                        if not (isinstance(b, int) and b == NB - 1):
                            rows(b + 1, 1 - h, i + h)
                        inv_dev(pool, d2v, 2 * b + 1, mv[:, 0], rs[:, 0, :], v2d)
                        inv_dev(pool, d2v, 2 * b + 2, mv[:, 1], rs[:, 1 + h, :], v2d)
                    rows(0, 0, 0)
                    blocks(pool, body, hi=NB // 2 - 1)
                    for h in range(2):
                        body(NB - 2 + h, h, NB // 2 - 1)

                @block.vector
                def _(dve):
                    def own_edge(b, h, i):
                        dve.wait_ge(in_rdy[h].sem, in_rdy[h].at(64 * i + 64))
                        dve.wait_ge(nrow_rdy[h].sem, nrow_rdy[h].at(16 * K * i + 16 * K))
                        T, G, e = tr[:, h], g0[:, h], eb[:, h]
                        nc.vector.tensor_tensor(e, G[:, :, D:D + H], ad[:, h], ALU.add)
                        nc.vector.drain()
                        nc.vector.scalar_tensor_tensor(e, e, 0.2, e, ALU.mult, ALU.max)
                        nc.vector.drain()
                        nc.vector.tensor_tensor(mx[:, :, :], e, T[:, :, D + H:WT], ALU.max)
                        nc.vector.drain()
                        nc.vector.tensor_tensor(fg[:, h, 0], T[:, :, D + H:WT], mx[:, :, :], ALU.subtract)
                        nc.vector.tensor_tensor(fg[:, h, 1], e, mx[:, :, :], ALU.subtract).then_inc(d2a.sem, 1)

                    def shares(b, h):
                        T = tr[:, h]
                        dve.wait_ge(a2d.sem, a2d.at(b + 1))
                        nc.vector.tensor_tensor(T[:, :, D:D + H], T[:, :, D:D + H], fg[:, h, 0], ALU.mult)
                        nc.vector.drain()
                        nc.vector.scalar_tensor_tensor(T[:, :, D:D + H], fg[:, h, 1], 1e-16, T[:, :, D:D + H], ALU.add, ALU.add)
                        nc.vector.drain()
                        nc.vector.reciprocal(T[:, :, D:D + H], T[:, :, D:D + H])
                        nc.vector.drain()
                        nc.vector.tensor_tensor(fg[:, h], fg[:, h], T[:, :, D:D + H].unsqueeze(1).broadcast_to([P, 2, K, H]), ALU.mult)
                        nc.vector.drain()

                    def body(b, h, i):
                        more = not (isinstance(b, int) and b == NB - 1)
                        T, G = tr[:, h], g0[:, h]
                        Tv = T[:, :, 0:D].rearrange("p g (a c) -> p g a c", a=H)
                        Gv = G[:, :, 0:D].rearrange("p g (a c) -> p g a c", a=H)
                        nc.vector.tensor_tensor(Tv, Tv, fg[:, h, 0].unsqueeze(3).broadcast_to([P, K, H, C]), ALU.mult)
                        nc.vector.tensor_tensor(Gv, Gv, fg[:, h, 1].unsqueeze(3).broadcast_to([P, K, H, C]), ALU.mult)
                        nc.vector.drain()
                        nc.vector.tensor_tensor(T[:, :, 0:D], T[:, :, 0:D], G[:, :, 0:D], ALU.add)
                        nc.vector.drain()
                        nc.vector.tensor_tensor(T[:, :, 0:D], T[:, :, 0:D], sk[:, h], ALU.add)
                        nc.vector.drain()
                        stats(T[:, :, 0:D], st, mv[:, 0]).then_inc(d2v.sem, 1)
                        if more:
                            own_edge(b + 1, 1 - h, i + h)
                        dve.wait_ge(v2d.sem, v2d.at(2 * b + 1))
                        shift(mv[:, 0], rs[:, 0, :], nm[:, 0, :])
                        nc.vector.drain()
                        for g in range(K):
                            nc.vector.tensor_scalar(T[:, g, 0:D], T[:, g, 0:D], rs[:, 0, g:g + 1], nm[:, 0, g:g + 1],
                                                    ALU.mult, ALU.add)
                        nc.vector.drain()
                        for m, op in ((0, ALU.mult), (1, ALU.add)):
                            nc.vector.tensor_tensor(T[:, :, 0:D], T[:, :, 0:D],
                                                    gb[:, m:m + 1, :].broadcast_to([P, K, D]), op)
                            nc.vector.drain()
                        dve.wait_ge(st_done[h].sem, st_done[h].at(64 * i))
                        nc.vector.tensor_tensor(x1[:, h], T[:, :, 0:D], xin[:, h], ALU.add)
                        nc.vector.drain().then_inc(rows_free.sem, 1)
                        stats(x1[:, h], st, mv[:, 1]).then_inc(d2v.sem, 1)
                        if more:
                            shares(b + 1, 1 - h)
                        dve.wait_ge(v2d.sem, v2d.at(2 * b + 2))
                        shift(mv[:, 1], rs[:, 1 + h, :], nm[:, 1 + h, :]).then_inc(dve_done.sem, 1)
                    own_edge(0, 0, 0)
                    shares(0, 0)
                    blocks(dve, body, hi=NB // 2 - 1)
                    for h in range(2):
                        body(NB - 2 + h, h, NB // 2 - 1)

                @block.scalar
                def _(act):
                    def weights(b, h, i):
                        act.wait_ge(d2a.sem, d2a.at(b + 1))
                        nc.scalar.activation(fg[:, h], fg[:, h], ACT.Exp).then_inc(a2d.sem, 1)

                    def body(b, h, i):
                        hp, ip = before(h, i)
                        first, last = isinstance(b, int) and b == 0, isinstance(b, int) and b == NB
                        if first:
                            weights(b, h, i)
                        if not first:
                            pu.copy(act, b - 1)
                            pu.bias(act, b - 1, bcol[:, 0:1])
                            pv.bias(act, b - 1, bcol[:, 3:4])
                        if not first:
                            act.wait_ge(st_done[hp].sem, st_done[hp].at(64 * ip))
                            for w, p in enumerate((pu, pv)):
                                for m in range(2):
                                    lo, hi, r = p.result(act, b - 1, m)
                                    q = nc.scalar.activation(flat(uv[:, hp, w, lo:hi, :]), r, ACT.Copy)
                                q.then_inc(p.used.sem, 1)
                            act.drain()
                            act.sem_inc(taken.sem, 1)
                        if not last:
                            if not (isinstance(b, int) and b == NB - 1):
                                weights(b + 1, 1 - h, i + h)
                            act.wait_ge(dve_done.sem, dve_done.at(b + 1))
                            act.wait_ge(st_done[h].sem, st_done[h].at(64 * i))
                            for g in range(K):
                                q = nc.scalar.activation(hh[:, h, g, :], x1[:, h, g, :], ACT.Relu,
                                                         bias=nm[:, 1 + h, g:g + 1], scale=rs[:, 1 + h, g:g + 1])
                            q.then_inc(for_pe.sem, 1)
                    skewed(act, body)

                @block.tensor
                def _(pe):
                    def body(b, h, i):
                        first, last = isinstance(b, int) and b == 0, isinstance(b, int) and b == NB
                        if not first:
                            pu.multiply(pe, b - 1, wuv[:, 0:D])
                            pv.multiply(pe, b - 1, wuv[:, D:2 * D])
                            pu.turn_back(pe, b - 1)
                            pv.turn_back(pe, b - 1)
                        if not last:
                            pu.transpose(pe, b, hh[:, h], for_pe)
                    skewed(pe, body)
            pu.end()
            pv.end()
            rows_free.base += NB
            d2v.base += 2 * NB
            v2d.base += 2 * NB
            for_pe.base += NB
            dve_done.base += NB
            taken.base += NB
            stage_base(nd=1, na=1, loads=4, stores=4, gathers=(nrow_rdy,), idx=1)

        with ExitStack() as c:
            ib = sb("e1_ib", [P, 2, K], i32, c)
            jb = sb("e1_jb", [P, 2, K], i32, c)
            xr = sb("e1_xr", [P, 2, K, 2 * D], fp32, c)
            ur = sb("e1_ur", [P, 2, K, D], fp32, c)
            lg = sb("e1_lg", [P, 2, K], fp32, c)
            mk = sb("e1_mk", [P, 2, K], fp32, c)
            zr = sb("e1_zr", [P, 2, K], fp32, c)
            S = sb("e1_S", [P, 2, K, D + 2], fp32, c)
            with nc.Block() as block:
                @block.sync
                def _(sp):
                    def load(b, h, i):
                        gathered(sp, row_rdy, h, i)
                        sp.dma_start(ib[:, h, :], pick(ecol(dst_s), b)).then_inc(idx_rdy[h].sem, 16)
                        gathered(sp, roy_rdy, h, i)
                        sp.dma_start(jb[:, h, :], pick(ecol(src_s), b)).then_inc(idy_rdy[h].sem, 16)

                    def store(b, h, i):
                        sp.wait_ge(dve_done.sem, dve_done.at(b + 1))
                        sp.nop(nofuse=True)
                        sp.dma_start(pick(erows(T1), b), S[:, h, :, :].rearrange("p g d -> p (g d)")).then_inc(st_done[h].sem, 16)
                    sp_stream(sp, load, store)
                    stored(sp, 1)

                @block.gpsimd
                def _(pool):
                    rows = gather_rows(pool, ib, idx_rdy, P1, xr, row_rdy, dve_done)
                    centres = gather_rows(pool, jb, idy_rdy, U1, ur, roy_rdy)

                    def body(b, h, i):
                        rows(b, h, i)
                        centres(b, h, i)
                    blocks(pool, body)

                @block.vector
                def _(dve):
                    nc.vector.memset(S[:, :, :, :], 0.0)
                    nc.vector.memset(zr[:, :, :], 0.0)
                    nc.vector.drain()
                    nc.vector.memset(S[:, :, :, D + 1:D + 2], 1.0)
                    nc.vector.drain()

                    def body(b, h, i):
                        dve.wait_ge(row_rdy[h].sem, row_rdy[h].at(16 * K * i + 16 * K))
                        dve.wait_ge(roy_rdy[h].sem, roy_rdy[h].at(16 * K * i + 16 * K))
                        u = ur[:, h]
                        nc.vector.tensor_tensor(u, u, xr[:, h, :, D:2 * D], ALU.add)
                        nc.vector.drain()
                        nc.vector.tensor_scalar(u, u, 0.0, None, ALU.max)
                        nc.vector.drain()
                        nc.vector.tensor_tensor(u, u, w2b[:, :].unsqueeze(1).broadcast_to([P, K, D]), ALU.mult)
                        nc.vector.drain()
                        nc.vector.tensor_reduce(lg[:, h, :], u, AX.X, ALU.add).then_inc(d2a.sem, 1)
                        dve.wait_ge(a2d.sem, a2d.at(2 * b + 1))
                        nc.vector.tensor_tensor_scan(zr[:, h, :], cont["src"][:, bass.ds(b * K, K)], mk[:, h, :],
                                                     zr[:, 1 - h, K - 1:K], ALU.mult, ALU.add)
                        nc.vector.drain()
                        dve.wait_ge(st_done[h].sem, st_done[h].at(16 * i))
                        nc.vector.tensor_copy(S[:, h, :, D], zr[:, h, :])
                        dve.wait_ge(a2d.sem, a2d.at(2 * b + 2))
                        for g in range(K):
                            pv = S[:, h, g - 1, 0:D] if g else S[:, 1 - h, K - 1, 0:D]
                            q = nc.vector.scalar_tensor_tensor(S[:, h, g, 0:D], pv, cont["src"][:, bass.ds(b * K + g, 1)],
                                                               xr[:, h, g, 0:D], ALU.mult, ALU.add)
                            if g < K - 1:
                                nc.vector.drain()
                        q.then_inc(dve_done.sem, 1)
                        nc.vector.drain()
                    blocks(dve, body)

                @block.scalar
                def _(act):
                    def body(b, h, i):
                        act.wait_ge(d2a.sem, d2a.at(b + 1))
                        nc.scalar.activation(mk[:, h, :], lg[:, h, :], ACT.Sigmoid, bias=b2b[:, :]).then_inc(a2d.sem, 1)
                        act.drain()
                        for g in range(K):
                            q = nc.scalar.activation(xr[:, h, g, 0:D], xr[:, h, g, 0:D], ACT.Copy, scale=mk[:, h, g:g + 1])
                        q.then_inc(a2d.sem, 1)
                    blocks(act, body)
            dve_done.base += NB
            stage_base(nd=1, na=2, stores=1, gathers=(row_rdy, roy_rdy), idx=1)
            for h in range(2):
                idy_rdy[h].base += 16 * NB // 2
            add_carry("src", T1, S[:, 1, K - 1, :], D + 1)

        with ExitStack() as c:
            ib = sb("n2_ib", [P, 2, K], i32, c)
            tr = sb("n2_tr", [P, 2, K, D + 2], fp32, c)
            h1 = sb("n2_h1", [P, 2, K, D], fp32, c)
            x1 = sb("n2_x1", [P, 2, K, D], fp32, c)
            zi = sb("n2_zi", [P, 2, K], fp32, c)
            em = sb("n2_em", [P, 2, K, D], fp32, c)
            x2 = sb("n2_x2", [P, 2, K, D], fp32, c)
            st = sb("n2_st", [P, K, 6], fp32, c)
            mv = sb("n2_mv", [P, 2, K, 2], fp32, c)
            rs = sb("n2_rs", [P, 2, K], fp32, c)
            nm = sb("n2_nm", [P, 2, K], fp32, c)
            h2 = sb("n2_h2", [P, 2, K, D], fp32, c)
            lo = sb("n2_lo", [P, 2, K, D], fp32, c)
            pa = Dense(c, "n2a", 0)
            pb = Dense(c, "n2b", 1)
            with nc.Block() as block:
                @block.sync
                def _(sp):
                    def load(b, h, i):
                        gathered(sp, nrow_rdy, h, i)
                        sp.dma_start(ib[:, h, :], pick(ncol(last_src), b)).then_inc(idx_rdy[h].sem, 16)
                        sp.wait_ge(rows_free.sem, rows_free.at(b - 1))
                        sp.nop(nofuse=True)
                        sp.dma_start(h1[:, h], pick(nparts(P1, 0, D), b)).then_inc(in_rdy[h].sem, 16)

                    blocks(sp, load)
                    for h in range(2):
                        sp.wait_ge(st_done[h].sem, st_done[h].at(16 * NB // 2))
                        sp.wait_ge(st2_done[h].sem, st2_done[h].at(32 * NB // 2))

                @block.gpsimd
                def _(pool):
                    rows = gather_rows(pool, ib, idx_rdy, T1, tr, nrow_rdy, rows_free)

                    def body(b, h, i):
                        if not (isinstance(b, int) and b >= NB - 1):
                            rows(b + 1, 1 - h, i + h)
                        if not (isinstance(b, int) and b == 0):
                            inv_dev(pool, d2v, b, mv[:, 1 - h], rs[:, 1 - h, :], v2d)
                    rows(0, 0, 0)
                    skewed(pool, body)

                @block.vector
                def _(dve):
                    def body(b, h, i):
                        hp, ip = before(h, i)
                        """Block b's mix, block b - 2's shift, block b - 1's residual."""
                        has = lambda lag: not isinstance(b, int) or 0 <= b - lag < NB
                        if has(0):
                            dve.wait_ge(in_rdy[h].sem, in_rdy[h].at(16 * i + 16))
                            dve.wait_ge(nrow_rdy[h].sem, nrow_rdy[h].at(16 * K * i + 16 * K))
                            T = tr[:, h]
                            nc.vector.tensor_scalar(zi[:, 0, :], T[:, :, D], 1e-9, None, ALU.add)
                            nc.vector.tensor_scalar(zi[:, 1, :], T[:, :, D + 1], -0.5, 1.0, ALU.mult, ALU.add)
                            nc.vector.drain()
                            nc.vector.reciprocal(zi[:, 0, :], zi[:, 0, :])
                            nc.vector.drain()
                            nc.vector.tensor_scalar(zi[:, 0, :], zi[:, 0, :], 0.5, None, ALU.mult)
                            nc.vector.tensor_tensor(h1[:, h], h1[:, h], zi[:, 1, :].unsqueeze(2).broadcast_to([P, K, D]), ALU.mult)
                            nc.vector.drain()
                            nc.vector.tensor_tensor(T[:, :, 0:D], T[:, :, 0:D], zi[:, 0, :].unsqueeze(2).broadcast_to([P, K, D]), ALU.mult)
                            nc.vector.drain()
                            nc.vector.tensor_tensor(em[:, h], T[:, :, 0:D], h1[:, h], ALU.add).then_inc(for_pe.sem, 1)
                            nc.vector.drain().then_inc(rows_free.sem, 1)
                        if has(2):
                            dve.wait_ge(v2d.sem, v2d.at(b - 1))
                            shift(mv[:, h], rs[:, h, :], nm[:, h, :]).then_inc(dve_done.sem, 1)
                        if has(1):
                            dve.wait_ge(in2_rdy[hp].sem, in2_rdy[hp].at(16 * ip + 16))
                            dve.wait_ge(st2_done[hp].sem, st2_done[hp].at(32 * ip))
                            for m in range(2):
                                g0_, g1_, r = pa.result(dve, b - 1, m)
                                q = nc.vector.tensor_tensor(flat(x2[:, hp, g0_:g1_, :]), r, flat(x1[:, hp, g0_:g1_, :]), ALU.add)
                            q.then_inc(pa.used.sem, 1)
                            nc.vector.drain()
                            stats(x2[:, hp], st, mv[:, hp]).then_inc(d2v.sem, 1)
                    skewed(dve, body, lag=2)

                @block.scalar
                def _(act):
                    def load(b, h):
                        act.dma_start(flat(x1[:, h]), pick(nrows(X1), b)).then_inc(in2_rdy[h].sem, 16)

                    def body(b, h, i):
                        has = lambda lag: not isinstance(b, int) or 0 <= b - lag < NB
                        hp, ip = before(h, i)
                        if has(1):
                            pa.copy(act, b - 1)
                        if has(3):
                            pb.copy(act, b - 3)
                        if has(1):
                            pa.bias(act, b - 1, bcol[:, 1:2], ACT.Relu)
                        if has(2):
                            act.wait_ge(dve_done.sem, dve_done.at(b - 1))
                            act.nop(nofuse=True)
                            if has(0):
                                load(b, h)
                            act.wait_ge(st2_done[h].sem, st2_done[h].at(32 * (i - 1)))
                            for g in range(K):
                                q = nc.scalar.activation(h2[:, h, g, :], x2[:, h, g, :], ACT.Relu,
                                                         bias=nm[:, h, g:g + 1], scale=rs[:, h, g:g + 1])
                            q.then_inc(for_pe2.sem, 1)
                            act.wait_ge(for_pe2.sem, for_pe2.at(b - 1))
                            act.nop(nofuse=True)
                            act.dma_start(pick(nrows(X2), b - 2), flat(x2[:, h])).then_inc(st2_done[h].sem, 16)
                            act.dma_start(pick(nrows(H2), b - 2), flat(h2[:, h])).then_inc(st2_done[h].sem, 16)
                        elif has(0):
                            load(b, h)
                        if has(3):
                            pb.bias(act, b - 3, bcol[:, 2:3])
                            act.wait_ge(st_done[hp].sem, st_done[hp].at(16 * (ip - 1)))
                            for m in range(2):
                                g0_, g1_, r = pb.result(act, b - 3, m)
                                q = nc.scalar.activation(flat(lo[:, hp, g0_:g1_, :]), r, ACT.Copy)
                            q.then_inc(pb.used.sem, 1)
                            act.drain().then_inc(taken2.sem, 1)
                            act.wait_ge(taken2.sem, taken2.at(b - 2))
                            act.nop(nofuse=True)
                            act.dma_start(pick(nrows(LW), b - 3), flat(lo[:, hp])).then_inc(st_done[hp].sem, 16)
                    skewed(act, body, lag=3)

                @block.tensor
                def _(pe):
                    def body(b, h, i):
                        has = lambda lag: not isinstance(b, int) or 0 <= b - lag < NB
                        if has(1):
                            pa.multiply(pe, b - 1, wl[:, :])
                        if has(3):
                            pb.multiply(pe, b - 3, wlp[:, :])
                        if has(1):
                            pa.turn_back(pe, b - 1)
                        if has(3):
                            pb.turn_back(pe, b - 3)
                        if has(0):
                            pa.transpose(pe, b, em[:, h], for_pe)
                        if has(2):
                            pb.transpose(pe, b - 2, h2[:, h], for_pe2)
                    skewed(pe, body, lag=3)
            pa.end()
            pb.end()
            for q in (for_pe, for_pe2, dve_done, rows_free, taken2, d2v, v2d):
                q.base += NB
            for h in range(2):
                in2_rdy[h].base += 16 * NB // 2
                st2_done[h].base += 32 * NB // 2
            stage_base(loads=1, stores=1, gathers=(nrow_rdy,), idx=1)

        with ExitStack() as c:
            ib = sb("e2_ib", [P, 2, K], i32, c)
            xr = sb("e2_xr", [P, 2, K, D], fp32, c)
            ws = sb("e2_ws", [P, 2, B, D], fp32, c)
            xT = sb("e2_xT", [P, 2, B * D], fp32, c)
            S = sb("e2_S", [P, 2, K, D], fp32, c)
            tp = ps("e2_tp", [P, 2, B * D], fp32, c)
            mm = ps("e2_mm", [P, 2, 512], fp32, c)
            with nc.Block() as block:
                @block.sync
                def _(sp):
                    def load(b, h, i):
                        gathered(sp, row_rdy, h, i)
                        sp.dma_start(ib[:, h, :], pick(ecol(src), b)).then_inc(idx_rdy[h].sem, 16)

                    def store(b, h, i):
                        sp.wait_ge(dve_done.sem, dve_done.at(b + 1))
                        sp.nop(nofuse=True)
                        sp.dma_start(pick(erows(T2), b), S[:, h, :, :].rearrange("p g d -> p (g d)")).then_inc(st_done[h].sem, 16)
                    sp_stream(sp, load, store)
                    stored(sp, 1)

                @block.gpsimd
                def _(pool):
                    blocks(pool, gather_rows(pool, ib, idx_rdy, H2, xr, row_rdy, rows_free))

                @block.tensor
                def _(pe):
                    def turn(n, s):
                        pe.wait_ge(for_pe.sem, for_pe.at(n + 1))
                        pe.wait_ge(hT_rdy.sem, hT_rdy.at(2 * n - 2))
                        for k in range(B):
                            q = nc.tensor.transpose(tp[:, s, k * D:(k + 1) * D], ws[:, s, k, :], ident[:, :])
                            if k % 4 == 3:
                                q.then_inc(tp_rdy.sem, 1)

                    def multiply(n, s):
                        pe.wait_ge(mm_free.sem, mm_free.at(n - 1))
                        for k in range(B):
                            if k % 4 == 0:
                                pe.wait_ge(hT_rdy.sem, hT_rdy.at(2 * n + k // 4 + 1))
                            q = nc.tensor.matmul(mm[:, s, 0:D], xT[:, s, k * D:(k + 1) * D], wb[:, k, :],
                                                 start=(k == 0), stop=(k == B - 1))
                        q.then_inc(mm_rdy.sem, 1)

                    def body(b, h, i):
                        for g in range(K):
                            if not (isinstance(b, int) and b == NB - 1 and g == K - 1):
                                turn(b * K + g + 1, (h + g + 1) % 2)
                            multiply(b * K + g, (h + g) % 2)
                    turn(0, 0)
                    with pe.Fori(0, NB // 2 - 1) as i:
                        for h in range(2):
                            body(2 * i + h, h, i)
                    for h in range(2):
                        body(NB - 2 + h, h, NB // 2 - 1)

                @block.scalar
                def _(act):
                    def body(b, h, i):
                        for g in range(K):
                            s, n = (h + g) % 2, b * K + g
                            act.wait_ge(mm_rdy.sem, mm_rdy.at(n - 1))
                            for m in range(2):
                                act.wait_ge(tp_rdy.sem, tp_rdy.at(2 * n + m + 1))
                                nc.scalar.activation(xT[:, s, m * 512:(m + 1) * 512], tp[:, s, m * 512:(m + 1) * 512],
                                                     ACT.Copy).then_inc(hT_rdy.sem, 1)
                    blocks(act, body)

                @block.vector
                def _(dve):
                    nc.vector.memset(S[:, :, :, :], 0.0)
                    nc.vector.drain()

                    def weigh(b, h, i, g):
                        n, s = b * K + g, (h + g) % 2
                        if g == 0:
                            dve.wait_ge(row_rdy[h].sem, row_rdy[h].at(16 * K * i + 16 * K))
                        dve.wait_ge(tp_rdy.sem, tp_rdy.at(2 * n - 2))
                        q = nc.vector.tensor_tensor(ws[:, s], xr[:, h, g:g + 1, :].broadcast_to([P, B, D]),
                                                    wc_e[:, bass.ds(n, 1), :].rearrange("p o b -> p (o b)")
                                                    .unsqueeze(2).broadcast_to([P, B, D]), ALU.mult)
                        q.then_inc(for_pe.sem, 1)

                    def body(b, h, i):
                        end = isinstance(b, int) and b == NB - 1
                        dve.wait_ge(st_done[h].sem, st_done[h].at(16 * i))
                        for g in range(K):
                            if g < K - 2:
                                weigh(b, h, i, g + 2)
                            elif not end:
                                weigh(b + 1, 1 - h, i + h, g + 2 - K)
                            if g == K - 3:
                                nc.vector.drain().then_inc(rows_free.sem, 1)
                            pv = S[:, h, g - 1, :] if g else S[:, 1 - h, K - 1, :]
                            dve.wait_ge(mm_rdy.sem, mm_rdy.at(b * K + g + 1))
                            nc.vector.scalar_tensor_tensor(S[:, h, g, :], pv, cont["dst"][:, bass.ds(b * K + g, 1)],
                                                           mm[:, (h + g) % 2, 0:D], ALU.mult, ALU.add)\
                                .then_inc(mm_free.sem, 1)
                            q = nc.vector.drain()
                        q.then_inc(dve_done.sem, 1)
                    weigh(0, 0, 0, 0)
                    weigh(0, 0, 0, 1)
                    with dve.Fori(0, NB // 2 - 1) as i:
                        for h in range(2):
                            body(2 * i + h, h, i)
                    for h in range(2):
                        body(NB - 2 + h, h, NB // 2 - 1)
            dve_done.base += NB
            rows_free.base += NB
            for q in (for_pe, mm_rdy, mm_free):
                q.base += EC
            for q in (tp_rdy, hT_rdy):
                q.base += 2 * EC
            stage_base(stores=1, gathers=(row_rdy,), idx=1)
            add_carry("dst", T2, S[:, 1, K - 1, :], D)

        own = sb("own", [P, K])
        sumq = sb("sumq", [P, 4, D])
        with ExitStack() as c:
            ib = sb("n3_ib", [P, 2, K], i32, c)
            tr = sb("n3_tr", [P, 2, K, D], fp32, c)
            lo = sb("n3_lo", [P, 2, K, D], fp32, c)
            x2 = sb("n3_x2", [P, 2, K, D], fp32, c)
            x3 = sb("n3_x3", [P, 2, K, D], fp32, c)
            st = sb("n3_st", [P, K, 6], fp32, c)
            mv = sb("n3_mv", [P, 2, K, 2], fp32, c)
            sd = sb("n3_sd", [P, 2, K], fp32, c)
            rs = sb("n3_rs", [P, 2, K], fp32, c)
            nm = sb("n3_nm", [P, 2, K], fp32, c)
            h3 = sb("n3_h3", [P, 2, K, D], fp32, c)
            sq = sb("n3_sq", [P, 2, K, D], fp32, c)
            acc = ps("n3_acc", [P, 512], fp32, c)
            with nc.Block() as block:
                @block.sync
                def _(sp):
                    def load(b, h, i):
                        gathered(sp, nrow_rdy, h, i)
                        sp.dma_start(ib[:, h, :], pick(ncol(last_dst), b)).then_inc(idx_rdy[h].sem, 16)
                        sp.wait_ge(dve_done.sem, dve_done.at(b - 1))
                        sp.nop(nofuse=True)
                        for t, o in ((LW, lo), (X2, x2)):
                            sp.dma_start(o[:, h, :, :].rearrange("p g d -> p (g d)"), pick(nrows(t), b)).then_inc(in_rdy[h].sem, 16)

                    def store(b, h, i):
                        sp.wait_ge(act_done.sem, act_done.at(b + 1))
                        sp.nop(nofuse=True)
                        for t, o in ((X3, x3), (Q[0], h3)):
                            sp.dma_start(pick(nrows(t), b), o[:, h, :, :].rearrange("p g d -> p (g d)")).then_inc(st_done[h].sem, 16)
                    sp_stream(sp, load, store)
                    stored(sp, 2)

                @block.gpsimd
                def _(pool):
                    nc.gpsimd.memset(own[:, :], 1.0).then_inc(step.sem, 1)
                    pool.wait_ge(step.sem, step.at(1))
                    nc.gpsimd.affine_select(out=own[:, :], in_=own[:, :], compare_op=ALU.is_ge, fill=0.0,
                                            base=N - 1 - (NB - 1) * K * P, pattern=[[-1, K]], channel_multiplier=-K)\
                        .then_inc(step.sem, 1)
                    blocks(pool, gather_rows(pool, ib, idx_rdy, T2, tr, nrow_rdy, dve_done))

                @block.vector
                def _(dve):
                    dve.wait_ge(step.sem, step.at(2))

                    def body(b, h, i):
                        dve.wait_ge(in_rdy[h].sem, in_rdy[h].at(32 * i + 32))
                        dve.wait_ge(nrow_rdy[h].sem, nrow_rdy[h].at(16 * K * i + 16 * K))
                        nc.vector.tensor_tensor(lo[:, h], lo[:, h], tr[:, h], ALU.add)
                        nc.vector.drain()
                        dve.wait_ge(st_done[h].sem, st_done[h].at(32 * i))
                        nc.vector.tensor_scalar(lo[:, h], lo[:, h], 0.0, None, ALU.max)
                        nc.vector.drain()
                        nc.vector.tensor_tensor(x3[:, h], lo[:, h], x2[:, h], ALU.add)
                        nc.vector.drain()
                        stats(x3[:, h], st, mv[:, h]).then_inc(d2a.sem, 1)
                        dve.wait_ge(a2d.sem, a2d.at(b + 1))
                        q = scale_shift(mv[:, h, :, 0], sd[:, h, :], rs[:, h, :], nm[:, h, :])
                        if isinstance(b, int) and b == NB - 1:
                            nc.vector.drain()
                            nc.vector.tensor_tensor(rs[:, h, :], rs[:, h, :], own[:, :], ALU.mult)
                            q = nc.vector.tensor_tensor(nm[:, h, :], nm[:, h, :], own[:, :], ALU.mult)
                        q.then_inc(dve_done.sem, 1)
                    with dve.Fori(0, NB // 2 - 1) as i:
                        for h in range(2):
                            body(2 * i + h, h, i)
                    for h in range(2):
                        body(NB - 2 + h, h, NB // 2 - 1)
                    dve.wait_ge(mm_rdy.sem, mm_rdy.at(2))
                    nc.vector.tensor_copy(sumq[:, 0, :], acc[:, 0:D])

                @block.scalar
                def _(act):
                    def body(b, h, i):
                        act.wait_ge(d2a.sem, d2a.at(b + 1))
                        nc.scalar.activation(sd[:, h, :], mv[:, h, :, 1], ACT.Sqrt, bias=eps5[:, :]).then_inc(a2d.sem, 1)
                        act.wait_ge(dve_done.sem, dve_done.at(b + 1))
                        act.wait_ge(st_done[h].sem, st_done[h].at(32 * i))
                        for g in range(K):
                            nc.scalar.activation(h3[:, h, g, :], x3[:, h, g, :], ACT.Relu,
                                                 bias=nm[:, h, g:g + 1], scale=rs[:, h, g:g + 1])
                        act.drain()
                        act.sem_inc(act_done.sem, 1)
                        act.wait_ge(mm_free.sem, mm_free.at(b - 1))
                        nc.scalar.activation(sq[:, h], h3[:, h], ACT.Square).then_inc(for_pe.sem, 1)
                    blocks(act, body)

                @block.tensor
                def _(pe):
                    nc.tensor.matmul(acc[:, 0:D], ones[:, :], zero[:, 0:D], start=True, stop=False).then_inc(mm_rdy.sem, 1)

                    def body(b, h, i):
                        pe.wait_ge(for_pe.sem, for_pe.at(b + 1))
                        for g in range(K):
                            q = nc.tensor.matmul(acc[:, 0:D], ones[:, :], sq[:, h, g, :], start=False, stop=False)
                        q.then_inc(mm_free.sem, 1)
                    blocks(pe, body)
                    nc.tensor.matmul(acc[:, 0:D], ones[:, :], zero[:, 0:D], start=False, stop=True).then_inc(mm_rdy.sem, 1)
            step.base += 2
            mm_rdy.base += 2
            mm_free.base += NB
            for_pe.base += NB
            dve_done.base += NB
            act_done.base += NB
            stage_base(nd=1, na=1, loads=2, stores=2, gathers=(nrow_rdy,), idx=1)

        scale = sb("scale", [P, 4, D])
        beta = sb("beta", [P, 4, D])
        coef = sb("coef", [P, 3, D])

        def scale_of(k):
            with nc.Block() as block:
                @block.vector
                def _(dve):
                    if k == 0:
                        nc.vector.tensor_scalar(sumq[:, 0, :], sumq[:, 0, :], 1e-12, None, ALU.max)
                        nc.vector.drain()
                    nc.vector.memset(mid[:, :], 0.0).then_inc(d2a.sem, 1)
                    dve.wait_ge(a2d.sem, a2d.at(1))
                    nc.vector.reciprocal(scale[:, k, :], beta[:, k, :])

                @block.scalar
                def _(act):
                    act.wait_ge(d2a.sem, d2a.at(1))
                    nc.scalar.activation(beta[:, k, :], sumq[:, k, :], ACT.Sqrt).then_inc(a2d.sem, 1)
            d2a.base += 1
            a2d.base += 1
        mid = sb("mid", [P, D])
        scale_of(0)

        def sum_rows(pe, acc, rows):
            nc.tensor.matmul(acc[:, 0:D], ones[:, :], zero[:, 0:D], start=True, stop=False)

            def body(b, h, i):
                pe.wait_ge(for_pe.sem, for_pe.at(b + 1))
                for g in range(K):
                    q = nc.tensor.matmul(acc[:, 0:D], ones[:, :], rows[:, h, g, :], start=False, stop=False)
                q.then_inc(mm_free.sem, 1)
            blocks(pe, body)
            nc.tensor.matmul(acc[:, 0:D], ones[:, :], zero[:, 0:D], start=False, stop=True).then_inc(mm_rdy.sem, 1)

        for k in range(1, 4):
            T = T3[k - 1]
            with ExitStack() as c:
                ib = sb(f"l{k}_ib", [P, 2, K], i32, c)
                xr = sb(f"l{k}_xr", [P, 2, K, D], fp32, c)
                S = sb(f"l{k}_S", [P, 2, K, D], fp32, c)
                with nc.Block() as block:
                    @block.sync
                    def _(sp):
                        def load(b, h, i):
                            gathered(sp, row_rdy, h, i)
                            sp.dma_start(ib[:, h, :], pick(ecol(dst_s), b)).then_inc(idx_rdy[h].sem, 16)

                        def store(b, h, i):
                            sp.wait_ge(dve_done.sem, dve_done.at(b + 1))
                            sp.nop(nofuse=True)
                            sp.dma_start(pick(erows(T), b), flat(S[:, h])).then_inc(st_done[h].sem, 16)
                        sp_stream(sp, load, store)
                        stored(sp, 1)

                    @block.gpsimd
                    def _(pool):
                        blocks(pool, gather_rows(pool, ib, idx_rdy, Q[k - 1], xr, row_rdy, dve_done))

                    @block.scalar
                    def _(act):
                        def body(b, h, i):
                            act.wait_ge(row_rdy[h].sem, row_rdy[h].at(16 * K * i + 16 * K))
                            for g in range(K):
                                q = nc.scalar.activation(xr[:, h, g, :], xr[:, h, g, :], ACT.Copy,
                                                         scale=ew_s[:, bass.ds(b * K + g, 1)])
                            q.then_inc(a2d.sem, 1)
                        blocks(act, body)

                    @block.vector
                    def _(dve):
                        nc.vector.memset(S[:, :, :, :], 0.0)
                        nc.vector.drain()

                        def body(b, h, i):
                            dve.wait_ge(st_done[h].sem, st_done[h].at(16 * i))
                            dve.wait_ge(a2d.sem, a2d.at(b + 1))
                            for g in range(K):
                                pv = S[:, h, g - 1, :] if g else S[:, 1 - h, K - 1, :]
                                q = nc.vector.scalar_tensor_tensor(S[:, h, g, :], pv, cont["src"][:, bass.ds(b * K + g, 1)],
                                                                   xr[:, h, g, :], ALU.mult, ALU.add)
                                if g == K - 1:
                                    q.then_inc(dve_done.sem, 1)
                                nc.vector.drain()
                        blocks(dve, body)
                dve_done.base += NB
                stage_base(na=1, stores=1, gathers=(row_rdy,), idx=1)
                add_carry("src", T, S[:, 1, K - 1, :], D)

            with ExitStack() as c:
                ib = sb(f"a{k}_ib", [P, 2, K], i32, c)
                tr = sb(f"a{k}_tr", [P, 2, K, D], fp32, c)
                uo = sb(f"a{k}_uo", [P, 2, K, D], fp32, c)
                q1 = sb(f"a{k}_q1", [P, 2, K, D], fp32, c)
                pq = sb(f"a{k}_pq", [P, 2, K, D], fp32, c)
                acc = ps(f"a{k}_acc", [P, 512], fp32, c)
                with nc.Block() as block:
                    @block.sync
                    def _(sp):
                        def load(b, h, i):
                            gathered(sp, nrow_rdy, h, i)
                            sp.dma_start(ib[:, h, :], pick(ncol(last_src), b)).then_inc(idx_rdy[h].sem, 16)
                            sp.wait_ge(dve_done.sem, dve_done.at(b - 1))
                            sp.nop(nofuse=True)
                            sp.dma_start(flat(q1[:, h]), pick(nrows(Q[k - 1]), b)).then_inc(in_rdy[h].sem, 16)

                        def store(b, h, i):
                            sp.wait_ge(act_done.sem, act_done.at(b + 1))
                            sp.nop(nofuse=True)
                            sp.dma_start(pick(nrows(UU[k - 1]), b), flat(uo[:, h])).then_inc(st_done[h].sem, 16)
                        sp_stream(sp, load, store)
                        stored(sp, 1)

                    @block.gpsimd
                    def _(pool):
                        blocks(pool, gather_rows(pool, ib, idx_rdy, T, tr, nrow_rdy, dve_done, act_done))

                    @block.scalar
                    def _(act):
                        def body(b, h, i):
                            act.wait_ge(nrow_rdy[h].sem, nrow_rdy[h].at(16 * K * i + 16 * K))
                            act.wait_ge(st_done[h].sem, st_done[h].at(16 * i))
                            nc.scalar.activation(flat(uo[:, h]), flat(tr[:, h]), ACT.Copy).then_inc(act_done.sem, 1)
                        blocks(act, body)

                    @block.vector
                    def _(dve):
                        def body(b, h, i):
                            dve.wait_ge(nrow_rdy[h].sem, nrow_rdy[h].at(16 * K * i + 16 * K))
                            dve.wait_ge(in_rdy[h].sem, in_rdy[h].at(16 * i + 16))
                            dve.wait_ge(mm_free.sem, mm_free.at(b - 1))
                            nc.vector.tensor_tensor(pq[:, h], tr[:, h], q1[:, h], ALU.mult).then_inc(for_pe.sem, 1)
                            nc.vector.drain().then_inc(dve_done.sem, 1)
                        blocks(dve, body)
                        dve.wait_ge(mm_rdy.sem, mm_rdy.at(1))
                        nc.vector.tensor_tensor(mid[:, :], acc[:, 0:D], scale[:, k - 1, :], ALU.mult)
                        nc.vector.drain()
                        nc.vector.tensor_tensor(mid[:, :], mid[:, :], scale[:, k - 1, :], ALU.mult)
                        nc.vector.drain()
                        nc.vector.tensor_tensor(coef[:, 1, :], mid[:, :], scale[:, k - 1, :], ALU.mult)
                        nc.vector.tensor_copy(coef[:, 0, :], scale[:, k - 1, :])
                        if k > 1:
                            nc.vector.tensor_tensor(coef[:, 2, :], beta[:, k - 1, :], scale[:, k - 2, :], ALU.mult)

                    @block.tensor
                    def _(pe):
                        sum_rows(pe, acc, pq)
                dve_done.base += NB
                act_done.base += NB
                for_pe.base += NB
                mm_free.base += NB
                mm_rdy.base += 1
                stage_base(loads=1, stores=1, gathers=(nrow_rdy,), idx=1)

            with ExitStack() as c:
                u = sb(f"b{k}_u", [P, 2, K, D], fp32, c)
                q1 = sb(f"b{k}_q1", [P, 2, K, D], fp32, c)
                q2 = sb(f"b{k}_q2", [P, 2, K, D], fp32, c)
                qo = sb(f"b{k}_qo", [P, 2, K, D], fp32, c)
                sq = sb(f"b{k}_sq", [P, 2, K, D], fp32, c)
                acc = ps(f"b{k}_acc", [P, 512], fp32, c)
                ins = [(u, UU[k - 1]), (q1, Q[k - 1])] + ([(q2, Q[k - 2])] if k > 1 else [])
                with nc.Block() as block:
                    @block.sync
                    def _(sp):
                        def load(b, h, i):
                            sp.wait_ge(dve_done.sem, dve_done.at(b - 1))
                            sp.nop(nofuse=True)
                            for o, t in ins:
                                sp.dma_start(flat(o[:, h]), pick(nrows(t), b)).then_inc(in_rdy[h].sem, 16)

                        def store(b, h, i):
                            sp.wait_ge(dve_done.sem, dve_done.at(b + 1))
                            sp.nop(nofuse=True)
                            sp.dma_start(pick(nrows(Q[k]), b), flat(qo[:, h])).then_inc(st_done[h].sem, 16)
                        sp_stream(sp, load, store)
                        stored(sp, 1)

                    @block.vector
                    def _(dve):
                        def body(b, h, i):
                            dve.wait_ge(in_rdy[h].sem, in_rdy[h].at(16 * len(ins) * (i + 1)))
                            for m, (o, _t) in enumerate(ins):
                                nc.vector.tensor_tensor(o[:, h], o[:, h], coef[:, m:m + 1, :].broadcast_to([P, K, D]), ALU.mult)
                            nc.vector.drain()
                            dve.wait_ge(st_done[h].sem, st_done[h].at(16 * i))
                            dve.wait_ge(act_done.sem, act_done.at(b - 1))
                            q = nc.vector.tensor_tensor(qo[:, h], u[:, h], q1[:, h], ALU.subtract)
                            if k > 1:
                                nc.vector.drain()
                                q = nc.vector.tensor_tensor(qo[:, h], qo[:, h], q2[:, h], ALU.subtract)
                            q.then_inc(dve_done.sem, 1)
                        blocks(dve, body)
                        dve.wait_ge(mm_rdy.sem, mm_rdy.at(1))
                        nc.vector.tensor_copy(sumq[:, k, :], acc[:, 0:D])

                    @block.scalar
                    def _(act):
                        def body(b, h, i):
                            act.wait_ge(dve_done.sem, dve_done.at(b + 1))
                            act.wait_ge(mm_free.sem, mm_free.at(b - 1))
                            nc.scalar.activation(flat(sq[:, h]), flat(qo[:, h]), ACT.Square).then_inc(for_pe.sem, 1)
                            act.drain()
                            act.sem_inc(act_done.sem, 1)
                        blocks(act, body)

                    @block.tensor
                    def _(pe):
                        sum_rows(pe, acc, sq)
                dve_done.base += NB
                act_done.base += NB
                for_pe.base += NB
                mm_free.base += NB
                mm_rdy.base += 1
                stage_base(loads=len(ins), stores=1)
            scale_of(k)

        with ExitStack() as c:
            dg = sb("o_dg", [P, 4, D], fp32, c)
            sc = sb("o_sc", [P, 4], fp32, c)
            qi = sb("o_qi", [P, 2, 4, K, D], fp32, c)
            x3 = sb("o_x3", [P, 2, K, D], fp32, c)
            hT = sb("o_hT", [P, 4, K * D], fp32, c)
            y = sb("o_y", [P, 2, K, D], fp32, c)
            tp = ps("o_tp", [P, 2, 2, 512], fp32, c)
            mm = ps("o_mm", [P, 4, 512], fp32, c)
            on = nrows(out)
            with nc.Block() as block:
                @block.sync
                def _(sp):
                    def load(b, h, i):
                        sp.wait_ge(dve_done.sem, dve_done.at(b - 1))
                        sp.nop(nofuse=True)
                        for k in range(4):
                            sp.dma_start(flat(qi[:, h, k]), pick(nrows(Q[k]), b)).then_inc(in_rdy[h].sem, 16)
                        sp.dma_start(flat(x3[:, h]), pick(nrows(X3), b)).then_inc(in_rdy[h].sem, 16)

                    def store(b, h, i):
                        sp.wait_ge(dve_done.sem, dve_done.at(b + 1))
                        sp.nop(nofuse=True)
                        sp.dma_start(pick(on, b), flat(y[:, h])).then_inc(st_done[h].sem, 16)
                    sp_stream(sp, load, store)
                    stored(sp, 1)

                @block.vector
                def _(dve):
                    nc.vector.tensor_tensor(dg[:, :, :], scale[:, :, :], ident[:, :].unsqueeze(1).broadcast_to([P, 4, D]), ALU.mult)
                    nc.vector.drain()
                    nc.vector.tensor_reduce(sc[:, :], dg[:, :, :], AX.X, ALU.add)
                    nc.vector.drain()
                    for k in range(4):
                        q = nc.vector.tensor_scalar(wf[:, k, :], wf[:, k, :], sc[:, k:k + 1], None, ALU.mult)
                    q.then_inc(step.sem, 1)

                    def body(b, h, i):
                        for n, k in enumerate((1, 3)):
                            dve.wait_ge(tp_rdy.sem, tp_rdy.at(4 * b + k + 1))
                            nc.vector.tensor_copy(hT[:, k, 0:512], tp[:, 1, 0, :])
                            nc.vector.tensor_copy(hT[:, k, 512:K * D], tp[:, 1, 1, 0:K * D - 512]).then_inc(hT2_rdy.sem, 1)
                        dve.wait_ge(a2d.sem, a2d.at(b + 1))
                        dve.wait_ge(in_rdy[h].sem, in_rdy[h].at(80 * i + 80))
                        nc.vector.tensor_tensor(y[:, h], y[:, h], x3[:, h], ALU.add).then_inc(dve_done.sem, 1)
                    blocks(dve, body)

                @block.scalar
                def _(act):
                    def body(b, h, i):
                        for n, k in enumerate((0, 2)):
                            act.wait_ge(tp_rdy.sem, tp_rdy.at(4 * b + k + 1))
                            nc.scalar.activation(hT[:, k, 0:512], tp[:, 0, 0, :], ACT.Copy)
                            nc.scalar.activation(hT[:, k, 512:K * D], tp[:, 0, 1, 0:K * D - 512], ACT.Copy).then_inc(hT_rdy.sem, 1)
                        act.wait_ge(st_done[h].sem, st_done[h].at(16 * i))
                        for g in range(K):
                            act.wait_ge(mm_rdy.sem, mm_rdy.at(b * K + g + 1))
                            nc.scalar.activation(y[:, h, g, :], mm[:, g % 4, 0:D], ACT.Relu).then_inc(mm_free.sem, 1)
                        act.drain()
                        act.sem_inc(a2d.sem, 1)
                    blocks(act, body)

                @block.tensor
                def _(pe):
                    pe.wait_ge(step.sem, step.at(1))

                    def body(b, h, i):
                        pe.wait_ge(in_rdy[h].sem, in_rdy[h].at(80 * i + 80))
                        for k in range(4):
                            cr = hT2_rdy if k % 2 else hT_rdy
                            pe.wait_ge(cr.sem, cr.at(2 * b + k // 2))
                            for g in range(K):
                                q = nc.tensor.transpose(tp[:, k % 2, g // 4, (g % 4) * D:(g % 4 + 1) * D], qi[:, h, k, g, :],
                                                        ident[:, :])
                            q.then_inc(tp_rdy.sem, 1)
                        pe.wait_ge(hT_rdy.sem, hT_rdy.at(2 * b + 2))
                        pe.wait_ge(hT2_rdy.sem, hT2_rdy.at(2 * b + 2))
                        for g in range(K):
                            pe.wait_ge(mm_free.sem, mm_free.at(b * K + g - 3))
                            for k in range(4):
                                q = nc.tensor.matmul(mm[:, g % 4, 0:D], hT[:, k, g * D:(g + 1) * D], wf[:, k, :],
                                                     start=(k == 0), stop=(k == 3))
                            q.then_inc(mm_rdy.sem, 1)
                    blocks(pe, body)


_INS = ["x", "src", "dst", "edge_type_32", "edge_weight", "L0_gnn_W", "L0_gnn_att_src", "L0_gnn_att_dst",
        "L0_gnn_gat_bias", "L0_gnn_skip_W", "L0_gnn_skip_b", "L0_gnn_ln_g", "L0_gnn_ln_b", "L1_gnn_W1", "L1_gnn_b1",
        "L1_gnn_W2", "L1_gnn_b2", "L1_gnn_Wl", "L1_gnn_bl", "L2_gnn_weight", "L2_gnn_w_comp", "L2_gnn_h_bias",
        "L2_gnn_loop_weight", "L3_gnn_weights"]
_FILL = {"x": 0, "src": N, "dst": N, "edge_type_32": 0, "edge_weight": 0}


def kernel(**inputs):
    import numpy as _np
    import concourse.bacc as _bacc
    from concourse import mybir as _mybir
    from concourse.bass_utils import run_bass_kernel_spmd as _run

    nc = _bacc.Bacc("TRN2", target_bir_lowering=False, num_devices=1)
    arrays, args = {}, []
    for name in _INS:
        a = _np.ascontiguousarray(inputs[name])
        if name in _FILL:
            a = _np.concatenate([a, _np.full((NP - N,) + a.shape[1:], _FILL[name], a.dtype)])
        arrays[f"in_{name}_dram"] = a
        args.append(nc.dram_tensor(f"in_{name}_dram", a.shape, _mybir.dt.from_np(a.dtype), kind="ExternalInput").ap())
    args.append(nc.dram_tensor("out_0_dram", (NP, D), _mybir.dt.float32, kind="ExternalOutput").ap())
    gnn(nc, *args)
    r = _run(nc, [arrays], core_ids=[0])
    return r.results[0]["out_0_dram"][0:N]
```
